# Optimizing a Trainium2 kernel written in Bass

```python
import numpy as np
import jax
import jax.numpy as jnp

def _softmax(x, axis=-1):
    return jax.nn.softmax(x, axis=axis)

def _gelu(x):
    return jax.nn.gelu(x, approximate=True)

def _silu(x):
    return jax.nn.silu(x)

def _sigmoid(x):
    return jax.nn.sigmoid(x)

def _layernorm(x, axis=-1, eps=1e-05):
    m = jnp.mean(x, axis=axis, keepdims=True)
    v = jnp.var(x, axis=axis, keepdims=True)
    return (x - m) / jnp.sqrt(v + eps)

def _scatter_add(tgt, idx, src, axis=0):
    return tgt.at[idx].add(src)

def _segment_sum(src, seg, n):
    return jax.ops.segment_sum(src, seg, n)
kernel_name = 'mk_flamingo_gated_d2_seqx_r8_9cf661'

def setup_inputs(seed: int=0):
    np.random.seed(seed)
    _w = jnp.asarray

    def _rec_inputs():
        import jax
        import jax.numpy as jnp
        _rk = jax.random.key(seed)
        x = 7.22e-05 + 1 * jax.random.normal(jax.random.fold_in(_rk, 1), (16, 64, 128), jnp.float32)
        _lenS = 64 - jax.random.randint(jax.random.fold_in(_rk, 7), (16,), 0, max(1, 64 // 4) + 1, jnp.int32)
        _lenS2 = 64 - jax.random.randint(jax.random.fold_in(_rk, 8), (16,), 0, max(1, 64 // 4) + 1, jnp.int32)
        _ctx_1024P = jax.random.normal(jax.random.fold_in(_rk, 11), (16, 16, 128), jnp.float32)
        _ctx_1024c = jax.random.dirichlet(jax.random.fold_in(_rk, 511), 0.3 * jnp.ones((16,), jnp.float32), (16, 64))
        _ctx_1024t = jnp.einsum('bsk,bkd->bsd', _ctx_1024c, _ctx_1024P)
        _ctx_1024t = _ctx_1024t * jax.lax.rsqrt(jnp.mean(jnp.square(_ctx_1024t)) + 1e-12) * 0.953939
        ctx_1024 = -0.000514642 + 1.00011 * (_ctx_1024t + 0.3 * jax.random.normal(jax.random.fold_in(_rk, 611), (16, 64, 128), jnp.float32))
        itok_BxS_8_8191 = jax.random.randint(jax.random.fold_in(_rk, 12), (16, 64), 8, 1024, jnp.int32)
        itok_BxS2_1_8191 = jax.random.randint(jax.random.fold_in(_rk, 13), (16, 64), 1, 1024, jnp.int32)
        _validS = jnp.arange(64)[None, :] < _lenS[:, None]
        _validS2 = jnp.arange(64)[None, :] < _lenS2[:, None]
        _causal = jnp.tril(jnp.ones((64, 64), dtype=bool))
        mask_BxSxS2_if1 = jnp.where(jnp.ones((16, 64, 64), dtype=bool), 1, 0).astype(jnp.int32)
        _g = jax.random.normal(jax.random.fold_in(_rk, 9001), (2, 2), jnp.float32)
        _g = jnp.sign(_g) * jnp.maximum(jnp.abs(_g), 1.0) + (_g == 0) * 1.0
        g_xattn = _g[0]
        g_ffn = _g[1]
        return (x, ctx_1024, itok_BxS_8_8191, itok_BxS2_1_8191, mask_BxSxS2_if1, g_xattn, g_ffn)
    x, ctx_1024, itok_BxS_8_8191, itok_BxS2_1_8191, mask_BxSxS2_if1, g_xattn, g_ffn = _rec_inputs()

    def _L0_xattn_setup():
        import jax, jax.numpy as jnp
        import numpy as np
        B, L_ENC, L_DEC, D = (16, 64, 128, 128)
        key = jax.random.key(seed)
        k1, k2, k3, k4, k5, k6 = jax.random.split(key, 6)
        encoder_hc = jax.random.normal(k1, (B, L_ENC, D), dtype=jnp.float32)
        decoder_hq = jax.random.normal(k2, (B, L_DEC, D), dtype=jnp.float32)
        w_sim = jax.random.normal(k3, (3 * D,), dtype=jnp.float32) * 0.02
        b_sim = jax.random.normal(k4, (1,), dtype=jnp.float32) * 0.02
        W_qv = jax.random.normal(k5, (4 * D, D), dtype=jnp.float32) * 0.02
        b_qv = jax.random.normal(k6, (D,), dtype=jnp.float32) * 0.02
        return {'encoder_hc': encoder_hc, 'decoder_hq': decoder_hq, 'w_sim': w_sim, 'b_sim': b_sim, 'W_qv': W_qv, 'b_qv': b_qv}
    _L0_xattn_all = _L0_xattn_setup()
    _L0_xattn_in = {k: v for k, v in _L0_xattn_all.items() if k in ('w_sim', 'b_sim', 'W_qv', 'b_qv')}
    del _L0_xattn_all

    def _L0_ffn_setup():
        import jax, jax.numpy as jnp
        import numpy as np
        DIM = 128
        HIDDEN = 384
        SCALE = 1.0 / 127.0

        def _dequant(w_int, dtype):
            return w_int.astype(dtype) * jnp.asarray(SCALE, dtype)
        key = jax.random.key(seed)
        k_x, k_g, k_u, k_d = jax.random.split(key, 4)
        x = jax.random.normal(k_x, (4, 256, DIM), dtype=jnp.float32)
        w_gate = jax.random.randint(k_g, (HIDDEN, DIM), -127, 128, dtype=jnp.int32)
        w_up = jax.random.randint(k_u, (HIDDEN, DIM), -127, 128, dtype=jnp.int32)
        w_down = jax.random.randint(k_d, (DIM, HIDDEN), -127, 128, dtype=jnp.int32)
        return {'x': x, 'w_gate': w_gate, 'w_up': w_up, 'w_down': w_down}
    _L0_ffn_all = _L0_ffn_setup()
    _L0_ffn_in = {k: v for k, v in _L0_ffn_all.items() if k in ('w_gate', 'w_up', 'w_down')}
    del _L0_ffn_all

    def _L1_xattn_setup():
        import jax, jax.numpy as jnp
        import numpy as np
        DIM = 128
        NUM_HEADS = 16
        HEAD_DIM = DIM // NUM_HEADS

        def _slopes(num_heads):
            ratio = 2.0 ** (-8.0 / num_heads)
            return jnp.asarray([ratio ** i for i in range(1, num_heads + 1)], dtype=jnp.float32)
        key = jax.random.key(seed)
        ks = jax.random.split(key, 10)
        b, q_len, k_len = (2, 256, 512)
        query = jax.random.normal(ks[0], (b, q_len, DIM), dtype=jnp.float32)
        keys = jax.random.normal(ks[1], (b, k_len, DIM), dtype=jnp.float32)
        values = jax.random.normal(ks[2], (b, k_len, DIM), dtype=jnp.float32)
        query_pos = jnp.sort(jax.random.randint(ks[3], (b, q_len), 0, 1024), axis=-1)
        key_pos = jnp.sort(jax.random.randint(ks[4], (b, k_len), 0, 1024), axis=-1)
        mask = jnp.ones((b, q_len, k_len), dtype=jnp.int32)
        lim = float(np.sqrt(6.0 / (DIM + DIM)))
        W_q = jax.random.uniform(ks[5], (DIM, DIM), minval=-lim, maxval=lim, dtype=jnp.float32)
        W_k = jax.random.uniform(ks[6], (DIM, DIM), minval=-lim, maxval=lim, dtype=jnp.float32)
        W_v = jax.random.uniform(ks[7], (DIM, DIM), minval=-lim, maxval=lim, dtype=jnp.float32)
        W_o = jax.random.uniform(ks[8], (DIM, DIM), minval=-lim, maxval=lim, dtype=jnp.float32)
        return {'query': query, 'keys': keys, 'values': values, 'W_q': W_q, 'W_k': W_k, 'W_v': W_v, 'W_o': W_o, 'query_pos': query_pos, 'key_pos': key_pos, 'mask': mask}
    _L1_xattn_all = _L1_xattn_setup()
    _L1_xattn_in = {k: v for k, v in _L1_xattn_all.items() if k in ('W_q', 'W_k', 'W_v', 'W_o')}
    del _L1_xattn_all

    def _L1_ffn_setup():
        import jax, jax.numpy as jnp
        import numpy as np
        DIM, HEADS, FFN, E = (128, 16, 512, 8)
        B, S = (2, 128)
        EPS = 1e-05

        def _ln(x, g, b):
            mu = jnp.mean(x, axis=-1, keepdims=True)
            var = jnp.mean((x - mu) ** 2, axis=-1, keepdims=True)
            return (x - mu) * jax.lax.rsqrt(var + EPS) * g + b
        key = jax.random.key(seed)
        ks = jax.random.split(key, 20)
        sd = 0.02
        d, f = (DIM, FFN)
        return {'x': jax.random.normal(ks[0], (B, S, d), jnp.float32), 'ln1_g': jnp.ones((d,), jnp.float32), 'ln1_b': jnp.zeros((d,), jnp.float32), 'Wqkv': jax.random.normal(ks[1], (d, 3 * d), jnp.float32) * sd, 'bqkv': jnp.zeros((3 * d,), jnp.float32), 'Wo': jax.random.normal(ks[2], (d, d), jnp.float32) * sd, 'bo': jnp.zeros((d,), jnp.float32), 'ln2_g': jnp.ones((d,), jnp.float32), 'ln2_b': jnp.zeros((d,), jnp.float32), 'gate_w': jax.random.normal(ks[3], (d, E), jnp.float32) * sd, 'W1': jax.random.normal(ks[4], (E, d, f), jnp.float32) * sd, 'b1': jnp.zeros((E, f), jnp.float32), 'W2': jax.random.normal(ks[5], (E, f, d), jnp.float32) * sd, 'b2': jnp.zeros((E, d), jnp.float32), 'rW1': jax.random.normal(ks[6], (d, f), jnp.float32) * sd, 'rb1': jnp.zeros((f,), jnp.float32), 'rW2': jax.random.normal(ks[7], (f, d), jnp.float32) * sd, 'rb2': jnp.zeros((d,), jnp.float32), 'coef_w': jax.random.normal(ks[8], (d, 2), jnp.float32) * sd, 'coef_b': jnp.zeros((2,), jnp.float32)}
    _L1_ffn_all = _L1_ffn_setup()
    _L1_ffn_in = {k: v for k, v in _L1_ffn_all.items() if k in ('ln1_g', 'ln1_b', 'Wqkv', 'bqkv', 'Wo', 'bo', 'ln2_g', 'ln2_b', 'gate_w', 'W1', 'b1', 'W2', 'b2', 'rW1', 'rb1', 'rW2', 'rb2', 'coef_w', 'coef_b')}
    del _L1_ffn_all
    return {'x': x, 'ctx_1024': ctx_1024, 'itok_BxS_8_8191': itok_BxS_8_8191, 'itok_BxS2_1_8191': itok_BxS2_1_8191, 'mask_BxSxS2_if1': mask_BxSxS2_if1, 'g_xattn': g_xattn, 'g_ffn': g_ffn, 'L0_xattn_w_sim': _L0_xattn_in['w_sim'], 'L0_xattn_b_sim': _L0_xattn_in['b_sim'], 'L0_xattn_W_qv': _L0_xattn_in['W_qv'], 'L0_xattn_b_qv': _L0_xattn_in['b_qv'], 'L0_ffn_w_gate': _L0_ffn_in['w_gate'], 'L0_ffn_w_up': _L0_ffn_in['w_up'], 'L0_ffn_w_down': _L0_ffn_in['w_down'], 'L1_xattn_W_q': _L1_xattn_in['W_q'], 'L1_xattn_W_k': _L1_xattn_in['W_k'], 'L1_xattn_W_v': _L1_xattn_in['W_v'], 'L1_xattn_W_o': _L1_xattn_in['W_o'], 'L1_ffn_ln1_g': _L1_ffn_in['ln1_g'], 'L1_ffn_ln1_b': _L1_ffn_in['ln1_b'], 'L1_ffn_Wqkv': _L1_ffn_in['Wqkv'], 'L1_ffn_bqkv': _L1_ffn_in['bqkv'], 'L1_ffn_Wo': _L1_ffn_in['Wo'], 'L1_ffn_bo': _L1_ffn_in['bo'], 'L1_ffn_ln2_g': _L1_ffn_in['ln2_g'], 'L1_ffn_ln2_b': _L1_ffn_in['ln2_b'], 'L1_ffn_gate_w': _L1_ffn_in['gate_w'], 'L1_ffn_W1': _L1_ffn_in['W1'], 'L1_ffn_b1': _L1_ffn_in['b1'], 'L1_ffn_W2': _L1_ffn_in['W2'], 'L1_ffn_b2': _L1_ffn_in['b2'], 'L1_ffn_rW1': _L1_ffn_in['rW1'], 'L1_ffn_rb1': _L1_ffn_in['rb1'], 'L1_ffn_rW2': _L1_ffn_in['rW2'], 'L1_ffn_rb2': _L1_ffn_in['rb2'], 'L1_ffn_coef_w': _L1_ffn_in['coef_w'], 'L1_ffn_coef_b': _L1_ffn_in['coef_b']}

def reference(x, ctx_1024, itok_BxS_8_8191, itok_BxS2_1_8191, mask_BxSxS2_if1, g_xattn, g_ffn, L0_xattn_w_sim, L0_xattn_b_sim, L0_xattn_W_qv, L0_xattn_b_qv, L0_ffn_w_gate, L0_ffn_w_up, L0_ffn_w_down, L1_xattn_W_q, L1_xattn_W_k, L1_xattn_W_v, L1_xattn_W_o, L1_ffn_ln1_g, L1_ffn_ln1_b, L1_ffn_Wqkv, L1_ffn_bqkv, L1_ffn_Wo, L1_ffn_bo, L1_ffn_ln2_g, L1_ffn_ln2_b, L1_ffn_gate_w, L1_ffn_W1, L1_ffn_b1, L1_ffn_W2, L1_ffn_b2, L1_ffn_rW1, L1_ffn_rb1, L1_ffn_rW2, L1_ffn_rb2, L1_ffn_coef_w, L1_ffn_coef_b):
    import jax
    import jax.numpy as jnp

    def _L0_xattn_ref(encoder_hc, decoder_hq, w_sim, b_sim, W_qv, b_qv):
        import jax, jax.numpy as jnp
        import numpy as np
        B, L_ENC, L_DEC, D = (16, 64, 128, 128)
        d = encoder_hc.shape[-1]
        w1, w2, w3 = (w_sim[:d], w_sim[d:2 * d], w_sim[2 * d:])
        Sim = (encoder_hc @ w1)[:, :, None] + (decoder_hq @ w2)[:, None, :] + jnp.einsum('bid,bjd->bij', encoder_hc * w3, decoder_hq) + b_sim[0]
        A = jax.nn.softmax(Sim, axis=2)
        hq_hat = jnp.einsum('bij,bjd->bid', A, decoder_hq)
        Batt = jax.nn.softmax(jnp.max(Sim, axis=2), axis=1)
        hc_bar = jnp.einsum('bi,bid->bd', Batt, encoder_hc)[:, None, :]
        hc_hat = jnp.broadcast_to(hc_bar, encoder_hc.shape)
        feats = jnp.concatenate([encoder_hc, hq_hat, encoder_hc * hq_hat, encoder_hc * hc_hat], axis=-1)
        hcq = feats @ W_qv + b_qv
        return hcq

    def _L0_ffn_ref(x, w_gate, w_up, w_down):
        import jax, jax.numpy as jnp
        import numpy as np
        DIM = 128
        HIDDEN = 384
        SCALE = 1.0 / 127.0

        def _dequant(w_int, dtype):
            return w_int.astype(dtype) * jnp.asarray(SCALE, dtype)
        wg = _dequant(w_gate, x.dtype)
        wu = _dequant(w_up, x.dtype)
        wd = _dequant(w_down, x.dtype)
        gate = jnp.einsum('bsd,hd->bsh', x, wg)
        up = jnp.einsum('bsd,hd->bsh', x, wu)
        h = jax.nn.silu(gate) * up
        return jnp.einsum('bsh,dh->bsd', h, wd)

    def _L1_xattn_ref(query, keys, values, W_q, W_k, W_v, W_o, query_pos, key_pos, mask):
        import jax, jax.numpy as jnp
        import numpy as np
        DIM = 128
        NUM_HEADS = 16
        HEAD_DIM = DIM // NUM_HEADS

        def _slopes(num_heads):
            ratio = 2.0 ** (-8.0 / num_heads)
            return jnp.asarray([ratio ** i for i in range(1, num_heads + 1)], dtype=jnp.float32)
        b, q_len, _ = query.shape
        k_len = keys.shape[1]
        scale = 1.0 / np.sqrt(HEAD_DIM)
        Q = (query @ W_q.T).reshape(b, q_len, NUM_HEADS, HEAD_DIM).transpose(0, 2, 1, 3)
        K = (keys @ W_k.T).reshape(b, k_len, NUM_HEADS, HEAD_DIM).transpose(0, 2, 1, 3)
        V = (values @ W_v.T).reshape(b, k_len, NUM_HEADS, HEAD_DIM).transpose(0, 2, 1, 3)
        scores = jnp.einsum('bhqd,bhkd->bhqk', Q, K) * scale
        dist = (query_pos[:, :, None] - key_pos[:, None, :]).astype(scores.dtype)
        bias = -_slopes(NUM_HEADS)[None, :, None, None] * dist[:, None, :, :]
        scores = scores + bias
        scores = jnp.where(mask[:, None, :, :] == 0, -jnp.inf, scores)
        m = jnp.max(scores, axis=-1, keepdims=True)
        e = jnp.exp(scores - m)
        attn = e / (1.0 + jnp.sum(e, axis=-1, keepdims=True))
        out = jnp.einsum('bhqk,bhkd->bhqd', attn, V)
        out = out.transpose(0, 2, 1, 3).reshape(b, q_len, DIM)
        return out @ W_o.T

    def _L1_ffn_ref(x, ln1_g, ln1_b, Wqkv, bqkv, Wo, bo, ln2_g, ln2_b, gate_w, W1, b1, W2, b2, rW1, rb1, rW2, rb2, coef_w, coef_b):
        import jax, jax.numpy as jnp
        import numpy as np
        DIM, HEADS, FFN, E = (128, 16, 512, 8)
        B, S = (2, 128)
        EPS = 1e-05

        def _ln(x, g, b):
            mu = jnp.mean(x, axis=-1, keepdims=True)
            var = jnp.mean((x - mu) ** 2, axis=-1, keepdims=True)
            return (x - mu) * jax.lax.rsqrt(var + EPS) * g + b
        b, s, d = x.shape
        h, dh = (HEADS, d // HEADS)
        xn = _ln(x, ln1_g, ln1_b)
        qkv = xn @ Wqkv + bqkv
        q, k, v = jnp.split(qkv, 3, axis=-1)
        q = q.reshape(b, s, h, dh)
        k = k.reshape(b, s, h, dh)
        v = v.reshape(b, s, h, dh)
        scores = jnp.einsum('bqhd,bkhd->bhqk', q, k) / jnp.sqrt(jnp.float32(dh))
        attn = jax.nn.softmax(scores, axis=-1)
        ctx = jnp.einsum('bhqk,bkhd->bqhd', attn, v).reshape(b, s, d)
        x = x + ctx @ Wo + bo
        xn2 = _ln(x, ln2_g, ln2_b)
        xt = xn2.reshape(b * s, d)
        probs = jax.nn.softmax(xt @ gate_w, axis=-1)
        gate_val = jnp.max(probs, axis=-1, keepdims=True)
        expert_idx = jnp.argmax(probs, axis=-1)
        oh = jax.nn.one_hot(expert_idx, E, dtype=xt.dtype)
        xe = jnp.einsum('te,td->etd', oh, xt)
        he = jax.nn.gelu(jnp.einsum('etd,edf->etf', xe, W1) + b1[:, None, :], approximate=False)
        ye = jnp.einsum('etf,efd->etd', he, W2) + b2[:, None, :]
        moe_out = jnp.einsum('te,etd->td', oh, ye) * gate_val
        rm = jax.nn.gelu(xt @ rW1 + rb1, approximate=False) @ rW2 + rb2
        coef = jax.nn.softmax(xt @ coef_w + coef_b, axis=-1)
        ff = moe_out * coef[:, 0:1] + rm * coef[:, 1:2]
        return x + ff.reshape(b, s, d)
    x = x + jnp.tanh(g_xattn[0]) * _L0_xattn_ref(_layernorm(x, axis=-1), ctx_1024, L0_xattn_w_sim, L0_xattn_b_sim, L0_xattn_W_qv, L0_xattn_b_qv)
    x = x + jnp.tanh(g_ffn[0]) * _L0_ffn_ref(_layernorm(x, axis=-1), L0_ffn_w_gate, L0_ffn_w_up, L0_ffn_w_down)
    x = x + jnp.tanh(g_xattn[1]) * _L1_xattn_ref(_layernorm(x, axis=-1), ctx_1024, ctx_1024, L1_xattn_W_q, L1_xattn_W_k, L1_xattn_W_v, L1_xattn_W_o, itok_BxS_8_8191, itok_BxS2_1_8191, mask_BxSxS2_if1)
    x = x + jnp.tanh(g_ffn[1]) * _L1_ffn_ref(_layernorm(x, axis=-1), L1_ffn_ln1_g, L1_ffn_ln1_b, L1_ffn_Wqkv, L1_ffn_bqkv, L1_ffn_Wo, L1_ffn_bo, L1_ffn_ln2_g, L1_ffn_ln2_b, L1_ffn_gate_w, L1_ffn_W1, L1_ffn_b1, L1_ffn_W2, L1_ffn_b2, L1_ffn_rW1, L1_ffn_rb1, L1_ffn_rW2, L1_ffn_rb2, L1_ffn_coef_w, L1_ffn_coef_b)
    return x

_drawn_inputs = setup_inputs


def setup_inputs(seed=0):
    import zlib

    import numpy as np

    out = dict(_drawn_inputs(seed))
    spreads = {'g_ffn': (-1.0, 0.6),
     'L1_ffn_ln1_g': (1.0, 0.6),
     'L1_ffn_ln1_b': (0.0, 2.0),
     'L1_ffn_bqkv': (0.0, 2.0),
     'L1_ffn_bo': (0.0, 2.0),
     'L1_ffn_ln2_g': (1.0, 0.6),
     'L1_ffn_ln2_b': (0.0, 2.0),
     'L1_ffn_b1': (0.0, 2.0),
     'L1_ffn_b2': (0.0, 2.0),
     'L1_ffn_rb1': (0.0, 2.0),
     'L1_ffn_rb2': (0.0, 2.0),
     'L1_ffn_coef_b': (0.0, 2.0)}
    factors = {'L1_xattn_W_q': 8.0,
     'L1_xattn_W_k': 8.0,
     'L1_xattn_W_v': 8.0,
     'L1_xattn_W_o': 8.0,
     'L1_ffn_Wqkv': 8.0,
     'L1_ffn_Wo': 8.0,
     'L1_ffn_gate_w': 51.07,
     'L1_ffn_W1': 61.751,
     'L1_ffn_W2': 50.009,
     'L1_ffn_rW1': 28.389,
     'L1_ffn_rW2': 24.209,
     'L1_ffn_coef_w': 33.519}
    for name, (base, spread) in spreads.items():
        noise = np.random.default_rng([zlib.crc32(name.encode()), seed]).standard_normal(out[name].shape)
        drawn = base * np.exp(spread * noise) if base else spread * noise
        out[name] = jnp.asarray(drawn.astype(out[name].dtype))
    for name, factor in factors.items():
        out[name] = (out[name] * factor).astype(out[name].dtype)
    return out
```

```python
from contextlib import ExitStack

import numpy as np
import concourse.bass as bass
from concourse import mybir

F32 = mybir.dt.float32
I32 = mybir.dt.int32
ALU = mybir.AluOpType
ACT = mybir.ActivationFunctionType
AX_X = mybir.AxisListType.X

P = 128
BANK = 512
EPS = 1e-5


def flamingo_layers(nc: bass.Bass, a, out: bass.AP):
    B, SEQ, D = a["x"].shape
    T = B * SEQ // P
    N = B * SEQ
    HALF = T // 2
    H = 16
    DH = D // H
    R = 2
    HG = H // R
    CH = T * R
    HID = a["L0_ffn_w_gate"].shape[0]
    HC = HID // P
    E, _, F = a["L1_ffn_W1"].shape
    FC = F // P
    SCALE = 1.0 / float(np.sqrt(DH))
    slopes = [(2.0 ** (-8.0 / H)) ** i for i in range(1, H + 1)]

    ctx = ExitStack()
    with ctx:
        def sb(name, shape, dt=F32):
            return ctx.enter_context(nc.sbuf_tensor(name, shape, dt))

        def sem(name):
            return ctx.enter_context(nc.semaphore(name))

        X0 = sb("x_in", [P, T, D])
        X1 = sb("x_after_l0_xattn", [P, T, D])
        X2 = sb("x_after_l0_ffn", [P, T, D])
        X3 = sb("x_after_l1_xattn", [P, T, D])
        XN = sb("xn", [P, T, D])
        XB = sb("x_plus_bias", [P, T, D])
        XT = sb("xT", [P, N])
        C = sb("ctx_tokens", [P, T, D])
        CJ = sb("ctx_by_tile_parity", [P, T // 2, 2, D])
        U = C
        X4 = CJ[:, :, :, :].rearrange("p k q d -> p (k q) d")
        CT = sb("ctxT", [P, N])
        C3T = sb("ctxT_w3_w1", [P, N])
        FEATS = sb("features_then_hidden", [P, 3, N])
        HT, EHT, EHC, HB = FEATS[:, 0, :], FEATS[:, 1, :], FEATS[:, 2, :], FEATS
        KT = sb("kT", [P, N])
        QT = sb("qT", [P, N])
        KBD = sb("k_block_diagonal", [P, B, HG, SEQ])
        BIAS = sb("position_bias", [P, T, H, SEQ])
        VBD = sb("v_block_diagonal", [P, B, HG, 2, DH + 1])
        SSB = sb("scores_sb", [P, 2, HG, SEQ])
        SM = sb("scores_less_max", [P, 2, HG, SEQ])
        PT = sb("probsT", [P, 2, HG // 2, P])
        ON = sb("attention_out", [P, T, D])
        ident = sb("ident", [P, P])
        mask8 = sb("head_mask", [P, HG])
        slope = sb("slope", [P, H])
        bmask = sb("batch_row_mask", [P, 2])
        neg_half = sb("neg_half", [P, T])
        w2b = sb("w2_over_rows", [P, SEQ])
        bsim = sb("b_sim", [P, 1])
        gates = sb("gates", [P, 4])
        tg = sb("tanh_gates", [P, 4])
        bqv = sb("b_qv_rows", [P, D])
        bqvg = sb("b_qv_gated", [P, D])
        wqv = sb("w_qv", [P, 4, D])
        wfi = sb("ffn_w_int", [P, 3 * HC, D], I32)
        wff = sb("ffn_w", [P, 3 * HC, D])
        wfT = sb("ffn_wT", [P, 3 * HC, P])
        SG = sb("silu_gate", [P, 2, BANK])
        xw = sb("xattn_w", [P, 4, D])
        xwT = sb("xattn_wT", [P, 4, P])
        kpos = sb("key_pos_rows", [P, T, SEQ], I32)
        msk = sb("mask", [P, T, SEQ], I32)
        mneg = sb("mask_neg_inf", [P, T, SEQ])
        ndist = sb("minus_dist", [P, T, SEQ])
        sim = sb("sim_less_max", [P, T, SEQ])
        AT = sb("attnT", [P, T // 2, P])
        stats = sb("bn_stats", [P, T, 6])
        mv = sb("mean_var", [P, T, 2])
        rstd = sb("rstd", [P, T])
        m8 = sb("row_max", [P, T])
        mf8 = sb("row_max_sim", [P, T])
        s8 = sb("row_sum", [P, T])
        r8 = sb("row_recip", [P, T])
        bt = sb("batt_rows", [T, 2, SEQ])
        bts = sb("batt_stats", [T, 3, 2])
        battm = sb("batt_masked", [P, T, 2])
        hc = sb("hc_barT", [P, B])
        mx = sb("head_max", [P, 2, HG])
        den = sb("head_den", [P, T, H])
        rec = sb("head_recip", [P, T, H])
        wqkv = sb("w_qkv", [P, 3 * D])
        bv = sb("b_v_rows", [P, D])
        wo = sb("w_o", [P, D])
        bo = sb("b_o_rows", [P, D])
        wgc = sb("gate_and_coef_w", [P, E + 2])
        coefb = sb("coef_b_rows", [P, 2])
        lg = sb("logits", [P, T, E + 2])
        gm = sb("gate_small", [P, T, 8])
        ge = sb("gate_exp", [P, T, E])
        oh = sb("one_hot", [P, T, E])
        rev = sb("expert_rank", [P, E])
        ohT = sb("scaled_one_hotT", [E, N])
        rw1 = sb("rW1", [P, F])
        rw2 = sb("rW2", [P, FC, D])
        b2 = sb("b2_rows", [E, D])
        VEC = (("L0_xattn_w_sim", 3), ("L1_ffn_bqkv", 3), ("L1_ffn_ln1_g", 1), ("L1_ffn_ln1_b", 1),
               ("L1_ffn_ln2_g", 1), ("L1_ffn_ln2_b", 1), ("L1_ffn_b1", E * FC), ("L1_ffn_rb1", FC))
        NVEC = sum(n for _, n in VEC)
        vrows = sb("vector_rows", [NVEC, P])
        vec = sb("vector_cols", [P, NVEC])
        wsim, bqk, ln1, ln2 = vec[:, 0:3], vec[:, 3:5], vec[:, 6:8], vec[:, 8:10]
        b1 = vec[:, 10:10 + (E + 1) * FC].rearrange("p (e c) -> p e c", c=FC)
        qrows = sb("query_pos_rows", [T, P], I32)
        qrowf = sb("query_pos_rows_f32", [T, P])
        qpos = sb("query_pos_cols", [P, T])
        rb2 = sb("rb2_rows", [P, D])
        late = BIAS[:, :, :, :].rearrange("p t h j -> p (t h j)")
        w1 = late[:, 0:E * F].rearrange("p (e f) -> p e f", e=E)
        w2 = late[:, E * F:2 * E * F].rearrange("p (e c d) -> p e c d", e=E, c=FC)
        G = KBD[:, :, :, :].rearrange("p b h j -> p (b h j)").rearrange("p (u c n) -> p u c n", u=2, c=FC)

        def W1(e, c):
            return (w1[:, e, :] if e < E else rw1[:, :])[:, c * P:(c + 1) * P]

        def W2(e, c):
            return w2[:, e, c, :] if e < E else rw2[:, c, :]

        PS = ctx.enter_context(nc.psum_tensor("ps", [P, 8, BANK], F32))

        ctx_in, cj_in, x_in, xw_in, fw_in, pos_in, small_in, moe_in, out_done = (
            sem(n) for n in "ctx_in cj_in x_in xw_in fw_in pos_in small_in moe_in out_done".split())
        ident_ready, mask_ready, rstd_ready, fw_ready, bqvg_ready, bias_ready, kbd_ready, vones_ready, xb_ready = (
            sem(n) for n in "ident_ready mask_ready rstd_ready fw_ready bqvg_ready bias_ready kbd_ready vones_ready xb_ready".split())
        tg_ready, ctxT_act, xT_act, xwT_ready, fwT_ready, kT_ready, a_exp, aT_ready, batt_exp, hT_ready = (
            sem(n) for n in "tg_ready ctxT_act xT_act xwT_ready fwT_ready kT_ready a_exp aT_ready batt_exp hT_ready".split())
        silu_ready, q_act, p_ready, onT_act, gelu_ready, gexp_ready, ohT_ready, gsum_ready = (
            sem(n) for n in "silu_ready q_act p_ready onT_act gelu_ready gexp_ready ohT_ready gsum_ready".split())
        var_ready, xn_ready, xT_dve, ctxT_dve, w2b_ready, mf_ready, sim_ready, a_ready, bt_ready, battm_ready, feat_ready = (
            sem(n) for n in "var_ready xn_ready xT_dve ctxT_dve w2b_ready mf_ready sim_ready a_ready bt_ready battm_ready feat_ready".split())
        x_done, h_ready, s_evac, sm_ready, on_ready, onT_dve, v_ready, q_dve, lg_ready, ohs_ready, acc_done, k_dve, btmax_ready = (
            sem(n) for n in "x_done h_ready s_evac sm_ready on_ready onT_dve v_ready q_dve lg_ready ohs_ready acc_done k_dve btmax_ready".split())
        ctxT_ps, xnT_ps, sim_ps, xwT_ps, fwT_ps, mT_ps, aT_ps, kT_ps, hq_ps, btT_ps, hc_ps, v_ps, y_ps, gu_ps = (
            sem(n) for n in "ctxT_ps xnT_ps sim_ps xwT_ps fwT_ps mT_ps aT_ps kT_ps hq_ps btT_ps hc_ps v_ps y_ps gu_ps".split())
        q_ps, s_ps, t_ps, o_ps, onT_ps, lg_ps, ohT_ps, b2_ps, h1_ps, moe_ps = (
            sem(n) for n in "q_ps s_ps t_ps o_ps onT_ps lg_ps ohT_ps b2_ps h1_ps moe_ps".split())
        vec_in, qrow_ready, vec_ps, vec_ready = sem("vec_in"), sem("qrow_ready"), sem("vec_ps"), sem("vec_ready")
        dve_step, act_step, pool_step = sem("dve_step"), sem("act_step"), sem("pool_step")
        block = ctx.enter_context(nc.Block())

        def tokens(ap):
            return ap.rearrange("(t q) s d -> (q s) t d", q=2)

        def rows(ap, n=P):
            return ap.unsqueeze(0).broadcast_to([n, ap.shape[0]])

        def over(ap, axis, shape):
            return ap.unsqueeze(axis).broadcast_to(shape)

        BANK4 = lambda t: (t // HALF, slice((t % HALF) * P, (t % HALF + 1) * P))
        OB = [2, 3, 6]

        def o_slot(t):
            return OB[t // 3], (t % 3) * H * (DH + 1)

        SB, TB = [4, 5], [0, 1]

        SMALL = 16 * 5
        MOE = 16 * (3 + 1 + E)
        POS = 16 * (4 + 1 + 1 + 2 + 1 + 4)
        VECS = 16 * (len(VEC) + 1)
        V_BANKS = [(0, 1), (6, 7)]

        @block.sync
        def _(sp):
            for h in range(2):
                sl = slice(h * HALF, (h + 1) * HALF)
                sp.dma_start(X0[:, sl, :], tokens(a["x"])[:, sl, :]).then_inc(x_in, 16)
            for q in range(2):
                for u in range(2):
                    sp.dma_start(CJ[q * SEQ:(q + 1) * SEQ, :, u, :],
                                 a["ctx_1024"].rearrange("(k q u) s d -> q u s k d", q=2, u=2)[q, u]).then_inc(cj_in, 16)
            sp.dma_start(wqv[:, :, :], a["L0_xattn_W_qv"].rearrange("(c p) d -> p c d", p=P)).then_inc(small_in, 16)
            for n, name in enumerate(("L1_xattn_W_q", "L1_xattn_W_k", "L1_xattn_W_v", "L1_xattn_W_o")):
                sp.dma_start(xw[:, n, :], a[name]).then_inc(xw_in, 16)
            sp.dma_start(wqkv[:, :], a["L1_ffn_Wqkv"]).then_inc(small_in, 16)
            sp.dma_start(wo[:, :], a["L1_ffn_Wo"]).then_inc(small_in, 16)
            sp.dma_start(wgc[:, 0:E], a["L1_ffn_gate_w"]).then_inc(small_in, 16)
            sp.dma_start(wgc[:, E:E + 2], a["L1_ffn_coef_w"]).then_inc(small_in, 16)
            sp.dma_start(rw1[:, :], a["L1_ffn_rW1"]).then_inc(moe_in, 16)
            sp.dma_start(rw2[:, :, :], a["L1_ffn_rW2"].rearrange("(c p) d -> p c d", p=P)).then_inc(moe_in, 16)
            sp.dma_start(b2[:, :], a["L1_ffn_b2"]).then_inc(moe_in, 16)
            sp.wait_ge(s_evac, CH)
            sp.dma_start(w1, a["L1_ffn_W1"].rearrange("e p f -> p e f")).then_inc(moe_in, 16)
            for e in range(E):
                sp.dma_start(w2[:, e, :, :], a["L1_ffn_W2"][e].rearrange("(c p) d -> p c d", p=P)).then_inc(moe_in, 16)
            for h in range(2):
                sl = slice(h * HALF, (h + 1) * HALF)
                sp.wait_ge(acc_done, HALF * (h + 1))
                sp.dma_start(tokens(out)[:, sl, :], X0[:, sl, :]).then_inc(out_done, 16)
            sp.wait_ge(out_done, 32)

        @block.scalar
        def _(act):
            steps = [0]

            def link(ins):
                steps[0] += 1
                ins.then_inc(act_step, 1)
                act.wait_ge(act_step, steps[0])

            def copy(dst, src):
                return nc.scalar.activation(dst, src, ACT.Copy)

            at = 0
            for name, n in VEC:
                src = a[name] if n > 1 else a[name].unsqueeze(0)
                if name == "L1_ffn_b1":
                    src = src.rearrange("e (c p) -> (e c) p", p=P)
                elif n > 1:
                    src = src.rearrange("(c p) -> c p", p=P)
                act.dma_start(vrows[at:at + n, :], src).then_inc(vec_in, 16)
                at += n
            act.dma_start(qrows[:, :], a["itok_BxS_8_8191"].rearrange("(t q) s -> t (q s)", q=2)).then_inc(vec_in, 16)
            act.dma_start(C[:, :, :], tokens(a["ctx_1024"])).then_inc(ctx_in, 16)
            for n, (name, i) in enumerate((("g_xattn", 0), ("g_ffn", 0), ("g_xattn", 1), ("g_ffn", 1))):
                act.dma_start(gates[:, n:n + 1], rows(a[name][i:i + 1])).then_inc(pos_in, 16)
            act.dma_start(bsim[:, :], rows(a["L0_xattn_b_sim"])).then_inc(pos_in, 16)
            act.dma_start(bqv[:, :], rows(a["L0_xattn_b_qv"])).then_inc(pos_in, 16)
            for n, name in enumerate(("L0_ffn_w_gate", "L0_ffn_w_up")):
                act.dma_start(wfi[:, n * HC:(n + 1) * HC, :], a[name].rearrange("(c p) d -> p c d", p=P)).then_inc(fw_in, 16)
            act.dma_start(wfi[:, 2 * HC:3 * HC, :], a["L0_ffn_w_down"].rearrange("p (c d) -> p c d", c=HC)).then_inc(fw_in, 16)
            for q in range(2):
                act.dma_start(kpos[q * SEQ:(q + 1) * SEQ, :, :],
                              over(a["itok_BxS2_1_8191"].rearrange("(t q) s -> q t s", q=2)[q], 0, [SEQ, T, SEQ])).then_inc(pos_in, 16)
            act.dma_start(msk[:, :, :], a["mask_BxSxS2_if1"].rearrange("(t q) i j -> (q i) t j", q=2)).then_inc(pos_in, 16)
            for dst, src in ((bv, a["L1_ffn_bqkv"][2 * D:3 * D]), (bo, a["L1_ffn_bo"]), (rb2, a["L1_ffn_rb2"]),
                             (coefb, a["L1_ffn_coef_b"])):
                act.dma_start(dst[:, :], rows(src)).then_inc(pos_in, 16)

            act.wait_ge(vec_in, VECS)
            copy(qrowf[:, :], qrows[:, :]).then_inc(qrow_ready, 1)
            act.wait_ge(vec_ps, 1)
            copy(vec[:, :], PS[:, 4, 0:NVEC])
            copy(qpos[:, :], PS[:, 4, NVEC:NVEC + T]).then_inc(vec_ready, 1)
            act.wait_ge(pos_in, POS)
            nc.scalar.activation(tg[:, :], gates[:, :], ACT.Tanh).then_inc(tg_ready, 1)
            for h in range(2):
                act.wait_ge(ctxT_ps, h + 1)
                copy(CT[:, h * BANK:(h + 1) * BANK], PS[:, h, :]).then_inc(ctxT_act, 1)
            act.wait_ge(xnT_ps, 1)
            copy(XT[:, 0:BANK], PS[:, 2, :]).then_inc(xT_act, 1)
            act.wait_ge(xwT_ps, 1)
            copy(xwT[:, :, :].rearrange("p c d -> p (c d)"), PS[:, 5, :]).then_inc(xwT_ready, 1)
            act.wait_ge(sim_ready, 1)
            nc.scalar.activation(sim[:, :, :], sim[:, :, :], ACT.Exp).then_inc(a_exp, 1)
            act.wait_ge(btmax_ready, 1)
            nc.scalar.activation(bt[:, :, :], bt[:, :, :], ACT.Exp).then_inc(batt_exp, 1)
            act.wait_ge(fwT_ps, 1)
            copy(wfT[:, 0:4, :].rearrange("p c d -> p (c d)"), PS[:, 6, :])
            copy(wfT[:, 4:8, :].rearrange("p c d -> p (c d)"), PS[:, 7, :])
            copy(wfT[:, 8, :], PS[:, 0, 0:P]).then_inc(fwT_ready, 1)
            act.wait_ge(aT_ps, 1)
            copy(AT[:, :, :].rearrange("p c d -> p (c d)"), PS[:, 1, :]).then_inc(aT_ready, 1)
            for h in range(2):
                act.wait_ge(kT_ps, h + 1)
                copy(KT[:, h * BANK:(h + 1) * BANK], PS[:, 6 + h, :]).then_inc(kT_ready, 1)
            act.wait_ge(hq_ps, 1)
            for par in range(2):
                copy(HT.rearrange("p (k u n) -> p u k n", u=2, n=P)[:, par], PS[:, 2 + par, :].rearrange("p (k n) -> p k n", n=P))\
                    .then_inc(hT_ready, 1)

            act.wait_ge(xnT_ps, 3)
            copy(XT[:, 0:BANK], PS[:, 2, :]).then_inc(xT_act, 1)
            for i in range(2 * HC):
                act.wait_ge(gu_ps, i + 1)
                if i >= 2:
                    act.wait_ge(h_ready, i - 1)
                nc.scalar.activation(SG[:, i % 2, :], PS[:, i % 2, :], ACT.Silu).then_inc(silu_ready, 1)

            def attention(k):
                act.wait_ge(xnT_ps, 2 * (2 + k) + 1)
                if k == 0:
                    copy(XT[:, 0:BANK], PS[:, 2, :]).then_inc(xT_act, 1)
                else:
                    nc.scalar.activation(XT[:, 0:BANK], PS[:, 2, :], ACT.Identity, bias=ln1[:, 1:2],
                                         scale=ln1[:, 0:1]).then_inc(xT_act, 1)
                if k == 0:
                    act.wait_ge(q_ps, 1)
                    nc.scalar.activation(QT[:, 0:BANK], PS[:, 0, :], ACT.Copy, scale=SCALE).then_inc(q_act, 1)
                for n in range(CH):
                    g = CH * k + n
                    act.wait_ge(t_ps, g + 1)
                    if g >= 2:
                        act.wait_ge(o_ps, g - 1)
                    nc.scalar.activation(PT[:, g % 2, :, :].rearrange("p c d -> p (c d)"), PS[:, TB[g % 2], :],
                                         ACT.Exp).then_inc(p_ready, 1)
                act.wait_ge(onT_ps, 2 * k + 1)
                copy(XT[:, 0:BANK], PS[:, 4, :]).then_inc(onT_act, 1)

            attention(0)
            attention(1)

            act.wait_ge(xnT_ps, 9)
            nc.scalar.activation(XT[:, 0:BANK], PS[:, 2, :], ACT.Identity, bias=ln2[:, 1:2],
                                 scale=ln2[:, 0:1]).then_inc(xT_act, 1)
            act.wait_ge(gsum_ready, 1)
            nc.scalar.activation(ge[:, :, :], ge[:, :, :], ACT.Exp)
            nc.scalar.activation(gm[:, :, 2:4], gm[:, :, 2:4], ACT.Exp).then_inc(gexp_ready, 1)
            act.wait_ge(ohT_ps, 1)
            for h in range(2):
                r = copy(ohT[:, h * BANK:(h + 1) * BANK], PS[0:E, 2 + h, :])
            r.then_inc(ohT_ready, 1)
            for e in range(E + 1):
                for h in range(2):
                    if e >= 2:
                        act.wait_ge(moe_ps, 2 * (e - 2) + h + 1)
                    for c in range(FC):
                        i = (2 * e + h) * FC + c
                        act.wait_ge(h1_ps, i + 1)
                        nc.scalar.activation(G[:, e % 2, c, h * BANK:(h + 1) * BANK], PS[:, (0, 1, 4, 5)[i % 4], :],
                                             ACT.Gelu, bias=b1[:, e, c:c + 1]).then_inc(gelu_ready, 1)


        @block.gpsimd
        def _(pool):
            steps = [0]

            def link(ins):
                steps[0] += 1
                ins.then_inc(pool_step, 1)
                pool.wait_ge(pool_step, steps[0])

            g = nc.gpsimd
            link(g.memset(ident[:], 0.0))
            g.affine_select(out=ident[:, :], in_=ident[:, :], compare_op=ALU.not_equal, fill=1.0, base=0,
                            pattern=[[-1, P]], channel_multiplier=1).then_inc(ident_ready, 1)
            g.memset(neg_half[:], -0.5)
            g.memset(bmask[:], 0.0)
            link(g.memset(mask8[:], 1.0))
            for r in range(R):
                v = mask8[r * SEQ:(r + 1) * SEQ, :]
                link(g.affine_select(out=v, in_=v, compare_op=ALU.is_ge, fill=0.0, base=0,
                                     pattern=[[-DH, HG]], channel_multiplier=1))
                link(g.affine_select(out=v, in_=v, compare_op=ALU.is_ge, fill=0.0, base=DH - 1,
                                     pattern=[[DH, HG]], channel_multiplier=-1))
                link(g.memset(bmask[r * SEQ:(r + 1) * SEQ, r:r + 1], 1.0))
            for h in range(H):
                g.memset(slope[:, h:h + 1], slopes[h])
            for e in range(E):
                g.memset(rev[:, e:e + 1], float(E - e))
            g.memset(VBD[:, :, :, :, :], 0.0)
            link(g.memset(mneg[:, :, :], 0.0))
            for u in range(2):
                g.memset(VBD[u * SEQ:(u + 1) * SEQ, :, :, u, DH:DH + 1], 1.0).then_inc(mask_ready, 1)
                pool.wait_ge(mask_ready, u + 1)

            def rsqrt(k):
                pool.wait_ge(var_ready, k + 1)
                g.tensor_tensor(rstd[:, :], mv[:, :, 1], neg_half[:, :], ALU.pow).then_inc(rstd_ready, 1)

            rsqrt(0)
            pool.wait_ge(fw_in, 48)
            g.tensor_scalar(wff[:, :, :], wfi[:, :, :], float(np.float32(1.0 / 127.0)), None, ALU.mult).then_inc(fw_ready, 1)
            pool.wait_ge(pos_in, POS)
            pool.wait_ge(tg_ready, 1)
            link(g.tensor_scalar(bqvg[:, :], bqv[:, :], tg[:, 0:1], None, ALU.mult))
            pool.wait_ge(x_in, 32)
            g.tensor_tensor(XB[:, :, :], X0[:, :, :], over(bqvg[:, :], 1, [P, T, D]), ALU.add).then_inc(xb_ready, 1)
            link(g.tensor_scalar(mneg[:, :, :], msk[:, :, :], 0.0, -3e38, ALU.is_equal, ALU.mult))
            link(g.tensor_scalar(mneg[:, :, :], mneg[:, :, :], 10.0, None, ALU.mult))
            pool.wait_ge(vec_ready, 1)
            link(g.tensor_copy(ndist[:, :, :], kpos[:, :, :]))
            link(g.tensor_tensor(ndist[:, :, :], ndist[:, :, :], over(qpos[:, :], 2, [P, T, SEQ]), ALU.subtract))
            link(g.tensor_tensor(ndist[:, :, :], ndist[:, :, :], mneg[:, :, :], ALU.add))
            rsqrt(1)
            for h in range(2):
                pool.wait_ge(kT_ready, h + 1)
            for h in range(HG):
                g.tensor_scalar(KBD[:, :, h, :], KT[:, :].rearrange("p (b j) -> p b j", b=B), mask8[:, h:h + 1],
                                None, ALU.mult).then_inc(kbd_ready, 1)
            for t in range(T):
                g.tensor_tensor(BIAS[:, t, :, :], over(ndist[:, t, :], 1, [P, H, SEQ]),
                                over(slope[:, :], 2, [P, H, SEQ]), ALU.mult).then_inc(bias_ready, 1)
            rsqrt(2)
            rsqrt(3)
            rsqrt(4)
            pool.wait_ge(xn_ready, 4 * T)
            g.tensor_tensor(XB[:, :, :], U[:, :, :], over(bo[:, :], 1, [P, T, D]), ALU.add).then_inc(xb_ready, 1)
            rsqrt(5)

        @block.vector
        def _(dve):
            steps = [0]
            v = nc.vector

            def link(ins):
                steps[0] += 1
                ins.then_inc(dve_step, 1)
                dve.wait_ge(dve_step, steps[0])

            def norm(k, src, dst):
                for t in range(T):
                    last = v.bn_stats(stats[:, t, :], src[:, t, :])
                link(last)
                for t in range(T):
                    last = v.bn_aggr(mv[:, t, :], stats[:, t, :])
                link(last)
                v.tensor_scalar(mv[:, :, 1], mv[:, :, 1], EPS, None, ALU.add).then_inc(var_ready, 1)
                dve.wait_ge(rstd_ready, k + 1)
                for t in range(T):
                    v.tensor_scalar(dst[:, t, :], src[:, t, :], mv[:, t, 0:1], rstd[:, t:t + 1],
                                    ALU.subtract, ALU.mult).then_inc(xn_ready, 1)

            dve.wait_ge(x_in, 32)
            norm(0, X0, XN)
            dve.wait_ge(pos_in, POS)
            dve.wait_ge(vec_ready, 1)
            v.memset(w2b[:, :], 0.0).then_inc(w2b_ready, 1)
            dve.wait_ge(w2b_ready, 1)
            v.tensor_scalar(w2b[:, :], w2b[:, :], wsim[:, 1:2], None, ALU.add).then_inc(w2b_ready, 1)
            for h in range(2):
                dve.wait_ge(ctxT_ps, h + 1)
                dve.wait_ge(ctxT_act, h + 1)
                v.tensor_scalar(C3T[:, h * BANK:(h + 1) * BANK], PS[:, h, :], wsim[:, 2:3], wsim[:, 0:1],
                                ALU.mult, ALU.add).then_inc(ctxT_dve, 1)
            dve.wait_ge(xnT_ps, 2)
            v.tensor_copy(XT[:, BANK:N], PS[:, 3, :]).then_inc(xT_dve, 1)
            dve.wait_ge(sim_ps, 1)
            S3 = PS[:, 4, :].rearrange("p (t j) -> p t j", t=T)
            link(v.tensor_reduce(m8[:, :], S3, AX_X, ALU.max))
            v.tensor_scalar(mf8[:, :], m8[:, :], bsim[:, 0:1], None, ALU.add).then_inc(mf_ready, 1)
            v.tensor_tensor(sim[:, :, :], S3, over(m8[:, :], 2, [P, T, SEQ]), ALU.subtract).then_inc(sim_ready, 1)
            dve.wait_ge(a_exp, 1)
            link(v.tensor_reduce(s8[:, :], sim[:, :, :], AX_X, ALU.add))
            link(v.reciprocal(r8[:, :], s8[:, :]))
            v.tensor_tensor(sim[:, :, :], sim[:, :, :], over(r8[:, :], 2, [P, T, SEQ]), ALU.mult).then_inc(a_ready, 1)
            dve.wait_ge(mT_ps, 1)
            M3 = PS[0:T, 5, 0:P].rearrange("p (q i) -> p q i", q=2)
            link(v.tensor_reduce(bts[:, 0, :], M3, AX_X, ALU.max))
            v.tensor_tensor(bt[:, :, :], M3, over(bts[:, 0, :], 2, [T, 2, SEQ]), ALU.subtract).then_inc(btmax_ready, 1)
            dve.wait_ge(batt_exp, 1)
            link(v.tensor_reduce(bts[:, 1, :], bt[:, :, :], AX_X, ALU.add))
            link(v.reciprocal(bts[:, 2, :], bts[:, 1, :]))
            v.tensor_tensor(bt[:, :, :], bt[:, :, :], over(bts[:, 2, :], 2, [T, 2, SEQ]), ALU.mult).then_inc(bt_ready, 1)
            dve.wait_ge(btT_ps, 1)
            dve.wait_ge(mask_ready, 2)
            for q in range(2):
                v.tensor_scalar(battm[:, :, q], PS[:, 5, P:P + T], bmask[:, q:q + 1], None,
                                ALU.mult).then_inc(battm_ready, 1)
            dve.wait_ge(hc_ps, 1)
            link(v.tensor_copy(hc[:, :], PS[:, 4, 0:B]))
            dve.wait_ge(xT_act, 1)
            v.tensor_tensor(EHC[:, :].rearrange("p (b i) -> p b i", b=B), XT[:, :].rearrange("p (b i) -> p b i", b=B),
                            over(hc[:, :], 2, [P, B, SEQ]), ALU.mult).then_inc(feat_ready, 1)
            dve.wait_ge(hT_ready, 2)
            for h in range(2):
                sl = slice(h * BANK, (h + 1) * BANK)
                v.tensor_tensor(EHT[:, sl], XT[:, sl], HT[:, sl], ALU.mult).then_inc(feat_ready, 1)

            def v_spread(k):
                dve.wait_ge(v_ps, k + 1)
                dve.wait_ge(mask_ready, 2)
                vb = V_BANKS[k]
                for u in range(2):
                    for h in range(2):
                        rs = slice(u * SEQ, (u + 1) * SEQ)
                        dst = VBD[rs, h * HG:(h + 1) * HG, :, u, 0:DH]
                        src = PS[rs, vb[h], :].rearrange("p (b m d) -> p b m d", b=HG, d=DH)
                        if k == 0:
                            v.tensor_copy(dst, src).then_inc(v_ready, 1)
                        else:
                            bias = bv[rs, :].rearrange("p (m u d) -> p m u d", u=2, d=DH)[:, :, u, :]
                            v.tensor_tensor(dst, src, over(bias, 1, [SEQ, HG, HG, DH]), ALU.add).then_inc(v_ready, 1)

            def gated(k, xin, xout, scale_by, gate):
                for h in range(2):
                    dve.wait_ge(y_ps, 2 * k + h + 1)
                    sl = slice(h * HALF, (h + 1) * HALF)
                    yp = PS[:, 6 + h, :].rearrange("p (t d) -> p t d", t=HALF)
                    if gate is None:
                        r = v.tensor_tensor(xout[:, sl, :], yp, xin[:, sl, :], ALU.add)
                    else:
                        r = v.scalar_tensor_tensor(xout[:, sl, :], yp, tg[:, gate:gate + 1], xin[:, sl, :], ALU.mult, ALU.add)
                    r.then_inc(x_done, 1)
                dve.wait_ge(x_done, 2 * k + 2)

            v_spread(0)
            dve.wait_ge(tg_ready, 1)
            dve.wait_ge(xb_ready, 1)
            gated(0, XB, X1, None, 0)

            norm(1, X1, XN)
            dve.wait_ge(xnT_ps, 4)
            v.tensor_copy(XT[:, BANK:N], PS[:, 3, :]).then_inc(xT_dve, 1)
            for i in range(2 * HC):
                h, c = divmod(i, HC)
                dve.wait_ge(gu_ps, i + 1)
                dve.wait_ge(silu_ready, i + 1)
                v.tensor_tensor(HB[:, c, h * BANK:(h + 1) * BANK], SG[:, i % 2, :], PS[:, 4 + i % 2, :],
                                ALU.mult).then_inc(h_ready, 1)
            gated(1, X1, X2, None, 1)

            def attention(k):
                dve.wait_ge(xnT_ps, 2 * (2 + k) + 2)
                if k == 0:
                    v.tensor_copy(XT[:, BANK:N], PS[:, 3, :]).then_inc(xT_dve, 1)
                    dve.wait_ge(q_ps, 2)
                    v.tensor_scalar(QT[:, BANK:N], PS[:, 1, :], SCALE, None, ALU.mult).then_inc(q_dve, 1)
                else:
                    v.tensor_scalar(XT[:, BANK:N], PS[:, 3, :], ln1[:, 0:1], ln1[:, 1:2], ALU.mult, ALU.add).then_inc(xT_dve, 1)
                    for h in range(2):
                        dve.wait_ge(q_ps, 2 + h + 1)
                        v.tensor_scalar(QT[:, h * BANK:(h + 1) * BANK], PS[:, h, :], bqk[:, 0:1], SCALE,
                                        ALU.add, ALU.mult).then_inc(q_dve, 1)
                    for h in range(2):
                        dve.wait_ge(kT_ps, 2 + h + 1)
                        v.tensor_scalar(KT[:, h * BANK:(h + 1) * BANK], PS[:, 4 + h, :], bqk[:, 1:2], None,
                                        ALU.add).then_inc(k_dve, 1)
                    dve.wait_ge(k_dve, 2)
                    for h in range(HG):
                        v.tensor_scalar(KBD[:, :, h, :], KT[:, :].rearrange("p (b j) -> p b j", b=B), mask8[:, h:h + 1],
                                        None, ALU.mult).then_inc(kbd_ready, 1)
                    v_spread(1)
                for n in range(CH):
                    g = CH * k + n
                    t, r = divmod(n, R)
                    dve.wait_ge(s_ps, g + 1)
                    sp3 = PS[:, SB[g % 2], :].rearrange("p (h j) -> p h j", h=HG)
                    if k == 0:
                        dve.wait_ge(bias_ready, t + 1)
                        v.tensor_tensor(SSB[:, g % 2, :, :], sp3, BIAS[:, t, r * HG:(r + 1) * HG, :], ALU.add).then_inc(s_evac, 1)
                        dve.wait_ge(s_evac, n + 1)
                        sp3 = SSB[:, g % 2, :, :]
                    link(v.tensor_reduce(mx[:, g % 2, :], sp3, AX_X, ALU.max))
                    if g >= 2:
                        dve.wait_ge(t_ps, g - 1)
                    v.tensor_tensor(SM[:, g % 2, :, :], sp3, over(mx[:, g % 2, :], 2, [P, HG, SEQ]),
                                    ALU.subtract).then_inc(sm_ready, 1)
                for t in range(T):
                    if t % 3 == 0:
                        dve.wait_ge(o_ps, CH * k + R * min(t + 3, T))
                    bank, at = o_slot(t)
                    o4 = PS[:, bank, at:at + H * (DH + 1)].rearrange("p (h d) -> p h d", h=H)
                    link(v.tensor_scalar(den[:, t, :], o4[:, :, DH], 1.0 - k, None, ALU.add))
                    link(v.reciprocal(rec[:, t, :], den[:, t, :]))
                    v.tensor_tensor(ON[:, t, :].rearrange("p (h d) -> p h d", h=H), o4[:, :, 0:DH],
                                    over(rec[:, t, :], 2, [P, H, DH]), ALU.mult).then_inc(on_ready, 1)
                dve.wait_ge(onT_ps, 2 * k + 2)
                v.tensor_copy(XT[:, BANK:N], PS[:, 5, :]).then_inc(onT_dve, 1)

            norm(2, X2, XN)
            attention(0)
            gated(2, X2, X3, None, 2)

            norm(3, X3, U)
            dve.wait_ge(xn_ready, 4 * T)
            norm(4, U, XN)
            attention(1)
            dve.wait_ge(xb_ready, 2)
            gated(3, XB, X4, None, None)

            norm(5, X4, XN)
            dve.wait_ge(xnT_ps, 10)
            v.tensor_scalar(XT[:, BANK:N], PS[:, 3, :], ln2[:, 0:1], ln2[:, 1:2], ALU.mult, ALU.add).then_inc(xT_dve, 1)
            dve.wait_ge(lg_ps, 1)
            L3 = PS[:, 0, 0:T * (E + 2)].rearrange("p (t e) -> p t e", t=T)
            v.tensor_tensor(lg[:, :, E:E + 2], L3[:, :, E:E + 2], over(coefb[:, :], 1, [P, T, 2]), ALU.add)
            link(v.tensor_copy(lg[:, :, 0:E], L3[:, :, 0:E]))
            v.tensor_reduce(gm[:, :, 0], lg[:, :, 0:E], AX_X, ALU.max)
            link(v.tensor_reduce(gm[:, :, 1], lg[:, :, E:E + 2], AX_X, ALU.max))
            v.tensor_tensor(ge[:, :, :], lg[:, :, 0:E], over(gm[:, :, 0], 2, [P, T, E]), ALU.subtract)
            v.tensor_tensor(gm[:, :, 2:4], lg[:, :, E:E + 2], over(gm[:, :, 1], 2, [P, T, 2]), ALU.subtract).then_inc(gsum_ready, 1)
            link(v.tensor_tensor(oh[:, :, :], lg[:, :, 0:E], over(gm[:, :, 0], 2, [P, T, E]), ALU.is_equal))
            link(v.tensor_tensor(oh[:, :, :], oh[:, :, :], over(rev[:, :], 1, [P, T, E]), ALU.mult))
            link(v.tensor_reduce(gm[:, :, 6], oh[:, :, :], AX_X, ALU.max))
            link(v.tensor_tensor(oh[:, :, :], over(rev[:, :], 1, [P, T, E]), over(gm[:, :, 6], 2, [P, T, E]), ALU.is_equal))
            dve.wait_ge(gexp_ready, 1)
            v.tensor_reduce(gm[:, :, 4], ge[:, :, :], AX_X, ALU.add)
            link(v.tensor_reduce(gm[:, :, 5], gm[:, :, 2:4], AX_X, ALU.add))
            link(v.reciprocal(gm[:, :, 4:6], gm[:, :, 4:6]))
            link(v.tensor_tensor(gm[:, :, 2:4], gm[:, :, 2:4], over(gm[:, :, 5], 2, [P, T, 2]), ALU.mult))
            link(v.tensor_tensor(gm[:, :, 7], gm[:, :, 4], gm[:, :, 2], ALU.mult))
            v.tensor_tensor(oh[:, :, :], oh[:, :, :], over(gm[:, :, 7], 2, [P, T, E]), ALU.mult).then_inc(ohs_ready, 1)
            dve.wait_ge(ohs_ready, 1)
            for t in range(T):
                last = v.scalar_tensor_tensor(U[:, t, :], rb2[:, :], gm[:, t, 3:4], X4[:, t, :], ALU.mult, ALU.add)
            link(last)
            dve.wait_ge(b2_ps, 1)
            for h in range(2):
                sl = slice(h * HALF, (h + 1) * HALF)
                last = v.tensor_tensor(U[:, sl, :], PS[:, 6 + h, :].rearrange("p (t d) -> p t d", t=HALF), U[:, sl, :], ALU.add)
            last.then_inc(x_done, 1)
            dve.wait_ge(x_done, 9)
            for e in range(E + 1):
                for t in range(T):
                    if t % HALF == 0:
                        dve.wait_ge(moe_ps, 2 * e + t // HALF + 1)
                    bank, sl = BANK4(t)
                    s = oh[:, t, e:e + 1] if e < E else gm[:, t, 3:4]
                    r = v.scalar_tensor_tensor(U[:, t, :], PS[:, (2, 6)[e % 2] + bank, sl], s, U[:, t, :], ALU.mult, ALU.add)
                    if t % HALF == HALF - 1:
                        r.then_inc(x_done, 1)
                dve.wait_ge(x_done, 9 + 2 * (e + 1))
            for t in range(T):
                v.scalar_tensor_tensor(X0[:, t, :], U[:, t, :], tg[:, 3:4], X3[:, t, :], ALU.mult, ALU.add).then_inc(acc_done, 1)


        @block.tensor
        def _(pe):
            mm, tr = nc.tensor.matmul, nc.tensor.transpose

            def norm_transpose(k):
                for t in range(T):
                    bank, sl = BANK4(t)
                    if t % HALF == 0:
                        pe.wait_ge(xn_ready, T * k + HALF * (bank + 1))
                    r = tr(PS[:, 2 + bank, sl], XN[:, t, :], ident[:, :])
                    if t % HALF == HALF - 1:
                        r.then_inc(xnT_ps, 1)

            pe.wait_ge(ident_ready, 1)
            pe.wait_ge(vec_in, VECS)
            tr(PS[:, 4, 0:NVEC], vrows[:, :], ident[0:NVEC, 0:NVEC])
            pe.wait_ge(qrow_ready, 1)
            tr(PS[:, 4, NVEC:NVEC + T], qrowf[:, :], ident[0:T, 0:T]).then_inc(vec_ps, 1)
            pe.wait_ge(ctx_in, 16)
            for t in range(T):
                bank, sl = BANK4(t)
                r = tr(PS[:, bank, sl], C[:, t, :], ident[:, :])
                if t % HALF == HALF - 1:
                    r.then_inc(ctxT_ps, 1)
            norm_transpose(0)
            pe.wait_ge(ctxT_dve, 2)
            pe.wait_ge(ctxT_act, 2)
            pe.wait_ge(w2b_ready, 2)
            pe.wait_ge(xT_act, 1)
            pe.wait_ge(xT_dve, 1)
            for b in range(B):
                t, q = divmod(b, 2)
                bs = slice(b * SEQ, (b + 1) * SEQ)
                o = PS[q * SEQ:(q + 1) * SEQ, 4, t * SEQ:(t + 1) * SEQ]
                mm(o, XT[:, bs], C3T[:, bs], start=True, stop=False)
                r = mm(o, w2b[:, :], CT[:, bs], start=False, stop=True)
            r.then_inc(sim_ps, 1)
            pe.wait_ge(xw_in, 64)
            for n in range(4):
                r = tr(PS[:, 5, n * P:(n + 1) * P], xw[:, n, :], ident[:, :])
            r.then_inc(xwT_ps, 1)
            pe.wait_ge(fw_ready, 1)
            for n in range(3 * HC):
                r = tr(PS[:, (6, 7, 0)[n // 4], (n % 4) * P:(n % 4 + 1) * P], wff[:, n, :], ident[:, :])
            r.then_inc(fwT_ps, 1)
            pe.wait_ge(mf_ready, 1)
            pe.wait_ge(xwT_ready, 1)
            tr(PS[0:T, 5, 0:P], mf8[:, :], ident[:, :]).then_inc(mT_ps, 1)
            pe.wait_ge(a_ready, 1)
            for n in range(T // 2):
                r = tr(PS[:, 1, n * P:(n + 1) * P], sim[:, 2 * n:2 * n + 2, :].rearrange("p t j -> p (t j)"), ident[:, :])
            r.then_inc(aT_ps, 1)
            pe.wait_ge(fwT_ready, 1)
            for h in range(2):
                mm(PS[:, 6 + h, :], xwT[:, 1, :], CT[:, h * BANK:(h + 1) * BANK], start=True, stop=True).then_inc(kT_ps, 1)
            pe.wait_ge(aT_ready, 1)
            pe.wait_ge(cj_in, 64)
            for t in range(T):
                k, par = divmod(t, 2)
                rs = slice(par * SEQ, (par + 1) * SEQ)
                for q in range(2):
                    at = k * P + q * SEQ
                    r = mm(PS[:, 2 + par, at:at + SEQ], CJ[rs, k, q, :], AT[rs, k, q * SEQ:(q + 1) * SEQ], start=True, stop=True)
            r.then_inc(hq_ps, 1)
            pe.wait_ge(bt_ready, 1)
            tr(PS[:, 5, P:P + T], bt[:, :, :].rearrange("p q i -> p (q i)"), ident[0:T, 0:T]).then_inc(btT_ps, 1)
            pe.wait_ge(battm_ready, 2)
            for t in range(T):
                r = mm(PS[:, 4, 2 * t:2 * t + 2], XN[:, t, :], battm[:, t, :], start=True, stop=True)
            r.then_inc(hc_ps, 1)

            def values(k, xT, w):
                for b in range(B):
                    bs = slice(b * SEQ, (b + 1) * SEQ)
                    at = (b % HG) * SEQ
                    for u in range(2):
                        r = mm(PS[u * SEQ:(u + 1) * SEQ, V_BANKS[k][b // HG], at:at + SEQ], xT[:, bs],
                               w.rearrange("p (m u d) -> p m u d", u=2, d=DH)[:, :, u, :], start=True, stop=True)
                r.then_inc(v_ps, 1)

            values(0, CT, xwT[:, 2, :])

            def project(lhs_of, ws):
                for t in range(T):
                    bank, sl = BANK4(t)
                    for c, w in enumerate(ws):
                        r = mm(PS[:, 6 + bank, sl], lhs_of(t, c), w, start=(c == 0), stop=(c == len(ws) - 1))
                    if t % HALF == HALF - 1:
                        r.then_inc(y_ps, 1)

            pe.wait_ge(small_in, SMALL)
            pe.wait_ge(feat_ready, 3)
            pe.wait_ge(kT_ready, 2)
            feats = [XT, HT, EHT, EHC]
            project(lambda t, c: feats[c][:, t * P:(t + 1) * P], [wqv[:, c, :] for c in range(4)])

            norm_transpose(1)
            pe.wait_ge(v_ready, 4)
            for i in range(2 * HC):
                h, c = divmod(i, HC)
                if c == 0:
                    pe.wait_ge(xT_dve if h else xT_act, 2)
                if i >= 2:
                    pe.wait_ge(h_ready, i - 1)
                mm(PS[:, i % 2, :], wfT[:, c, :], XT[:, h * BANK:(h + 1) * BANK], start=True, stop=True)
                mm(PS[:, 4 + i % 2, :], wfT[:, HC + c, :], XT[:, h * BANK:(h + 1) * BANK], start=True, stop=True).then_inc(gu_ps, 1)
            pe.wait_ge(h_ready, 2 * HC)
            project(lambda t, c: HB[:, c, t * P:(t + 1) * P], [wfT[:, 2 * HC + c, :] for c in range(HC)])

            def attention(k):
                pe.wait_ge(xT_act, 3 + k)
                pe.wait_ge(xT_dve, 3 + k)
                wq = xwT[:, 0, :] if k == 0 else wqkv[:, 0:D]
                for h in range(2):
                    mm(PS[:, h, :], wq, XT[:, h * BANK:(h + 1) * BANK], start=True, stop=True).then_inc(q_ps, 1)
                if k == 1:
                    for h in range(2):
                        mm(PS[:, 4 + h, :], wqkv[:, D:2 * D], XT[:, h * BANK:(h + 1) * BANK], start=True, stop=True).then_inc(kT_ps, 1)
                    values(1, XT, wqkv[:, 2 * D:3 * D])
                    pe.wait_ge(k_dve, 2)
                if k == 0:
                    pe.wait_ge(q_act, 1)
                pe.wait_ge(q_dve, (1, 3)[k])
                pe.wait_ge(kbd_ready, HG * (k + 1))
                pe.wait_ge(v_ready, 4 * (k + 1))

                def scores(n):
                    g = CH * k + n
                    t, r = divmod(n, R)
                    if n >= 2:
                        pe.wait_ge(*((s_evac, n - 1) if k == 0 else (sm_ready, g - 1)))
                    rs = slice(r * SEQ, (r + 1) * SEQ)
                    for q in range(2):
                        b = 2 * t + q
                        i = mm(PS[q * SEQ:(q + 1) * SEQ, SB[g % 2], :], QT[rs, b * SEQ:(b + 1) * SEQ],
                               KBD[rs, b, :, :].rearrange("p h j -> p (h j)"), start=True, stop=True)
                    i.then_inc(s_ps, 1)

                def turn(n):
                    g = CH * k + n
                    pe.wait_ge(sm_ready, g + 1)
                    if g >= 2:
                        pe.wait_ge(p_ready, g - 1)
                    for m in range(HG // 2):
                        i = tr(PS[:, TB[g % 2], m * P:(m + 1) * P],
                               SM[:, g % 2, 2 * m:2 * m + 2, :].rearrange("p h j -> p (h j)"), ident[:, :])
                    i.then_inc(t_ps, 1)

                def weigh(n):
                    g = CH * k + n
                    t, r = divmod(n, R)
                    pe.wait_ge(p_ready, g + 1)
                    bank, at = o_slot(t)
                    for m in range(HG // 2):
                        hp = r * (HG // 2) + m
                        for q in range(2):
                            c = at + hp * 2 * (DH + 1)
                            i = mm(PS[q * SEQ:(q + 1) * SEQ, bank, c:c + 2 * (DH + 1)], PT[:, g % 2, m, q * SEQ:(q + 1) * SEQ],
                                   VBD[:, 2 * t + q, hp, :, :].rearrange("p u d -> p (u d)"), start=True, stop=True)
                    i.then_inc(o_ps, 1)

                for n in range(CH + 2):
                    if n < CH:
                        scores(n)
                    if 1 <= n <= CH:
                        turn(n - 1)
                    if n >= 2:
                        weigh(n - 2)
                for t in range(T):
                    bank, sl = BANK4(t)
                    if t % HALF == 0:
                        pe.wait_ge(on_ready, T * k + HALF * (bank + 1))
                    r = tr(PS[:, 4 + bank, sl], ON[:, t, :], ident[:, :])
                    if t % HALF == HALF - 1:
                        r.then_inc(onT_ps, 1)
                pe.wait_ge(onT_act, k + 1)
                pe.wait_ge(onT_dve, k + 1)
                project(lambda t, c: XT[:, t * P:(t + 1) * P], [xwT[:, 3, :] if k == 0 else wo[:, :]])

            norm_transpose(2)
            attention(0)
            norm_transpose(4)
            attention(1)
            norm_transpose(5)
            pe.wait_ge(xT_act, 5)
            pe.wait_ge(xT_dve, 5)
            for t in range(T):
                r = mm(PS[:, 0, t * (E + 2):(t + 1) * (E + 2)], XT[:, t * P:(t + 1) * P], wgc[:, :], start=True, stop=True)
            r.then_inc(lg_ps, 1)
            pe.wait_ge(ohs_ready, 1)
            for t in range(T):
                bank, sl = BANK4(t)
                r = tr(PS[0:E, 2 + bank, sl], oh[:, t, :], ident[:, :])
            r.then_inc(ohT_ps, 1)
            pe.wait_ge(ohT_ready, 1)
            pe.wait_ge(moe_in, MOE)
            for t in range(T):
                bank, sl = BANK4(t)
                r = mm(PS[:, 6 + bank, sl], ohT[:, t * P:(t + 1) * P], b2[:, :], start=True, stop=True)
            r.then_inc(b2_ps, 1)

            def hidden(u):
                e, h = divmod(u, 2)
                for c in range(FC):
                    i = u * FC + c
                    if i >= 4:
                        pe.wait_ge(gelu_ready, i - 3)
                    mm(PS[:, (0, 1, 4, 5)[i % 4], :], W1(e, c), XT[:, h * BANK:(h + 1) * BANK],
                       start=True, stop=True).then_inc(h1_ps, 1)

            def down(u):
                e, h = divmod(u, 2)
                pe.wait_ge(gelu_ready, (u + 1) * FC)
                pe.wait_ge(x_done, 9 if e < 2 else 9 + 2 * (e - 2) + h + 1)
                for t in range(h * HALF, (h + 1) * HALF):
                    _, sl = BANK4(t)
                    for c in range(FC):
                        r = mm(PS[:, (2, 6)[e % 2] + h, sl], G[:, e % 2, c, t * P:(t + 1) * P], W2(e, c),
                               start=(c == 0), stop=(c == FC - 1))
                r.then_inc(moe_ps, 1)

            for u in range(2 * (E + 1) + 1):
                if u < 2 * (E + 1):
                    hidden(u)
                if u >= 1:
                    down(u - 1)


def kernel(**inputs):
    import numpy as _np
    import concourse.bacc as _bacc
    from concourse import mybir as _mybir
    from concourse.bass_utils import run_bass_kernel_spmd as _run

    nc = _bacc.Bacc("TRN2", target_bir_lowering=False, num_devices=1)
    arrays, args = {}, {}
    for name, value in inputs.items():
        v = _np.ascontiguousarray(value)
        arrays[f"in_{name}"] = v
        args[name] = nc.dram_tensor(f"in_{name}", v.shape, _mybir.dt.from_np(v.dtype), kind="ExternalInput").ap()
    out = nc.dram_tensor("out_0", inputs["x"].shape, _mybir.dt.float32, kind="ExternalOutput").ap()
    flamingo_layers(nc, args, out)
    r = _run(nc, [arrays], core_ids=[0])
    return r.results[0]["out_0"]
```

```python
from contextlib import ExitStack

import numpy as np
import concourse.bass as bass
from concourse import mybir

F32 = mybir.dt.float32
I32 = mybir.dt.int32
BF16 = mybir.dt.bfloat16
ALU = mybir.AluOpType
ACT = mybir.ActivationFunctionType
AX_X = mybir.AxisListType.X

P = 128
BANK = 512
EPS = 1e-5


def flamingo_layers(nc: bass.Bass, a, out: bass.AP):
    B, SEQ, D = a["x"].shape
    N = B * SEQ
    T = N // P
    HALF = T // 2
    BH = B // 2
    H = 16
    DH = D // H
    R = 2
    HG = H // R
    CH = T * R
    HID = a["L0_ffn_w_gate"].shape[0]
    HC = HID // P
    E, _, F = a["L1_ffn_W1"].shape
    FC = F // P
    BLOCKS = T + E - 1
    SLOTS = BLOCKS * P
    ROW = D + 4
    NOWHERE = 4 * N
    WB = 3
    SCALE = 1.0 / float(np.sqrt(DH))
    slopes = [(2.0 ** (-8.0 / H)) ** i for i in range(1, H + 1)]
    assert D == P and E == T and 2 * BANK == N

    ctx = ExitStack()
    with ctx:
        def sb(name, shape, dt=F32):
            return ctx.enter_context(nc.sbuf_tensor(name, shape, dt))

        def sem(name):
            return ctx.enter_context(nc.semaphore(name))

        X0 = sb("x_in", [P, T, D])
        X1 = sb("x_after_l0_xattn", [P, T, D])
        X2, X3 = X0, X1
        XN = sb("xn", [P, T, D])
        XB = sb("x_plus_bias", [P, T, D])
        XT = sb("xT", [P, N])
        C = sb("ctx_tokens", [P, T, D])
        U = C
        ABD = sb("attn_block_diagonal", [P, T, P])
        X4 = ABD
        CT = sb("ctxT", [P, N])
        C3T = sb("ctxT_w3_w1", [P, N])
        FEATS = sb("features_then_hidden", [P, 4, N])
        HT, EHT, EHC, HB = FEATS[:, 0, :], FEATS[:, 1, :], FEATS[:, 2, :], FEATS
        HR = FEATS
        KT = sb("kT", [P, N])
        QT = sb("qT", [P, N])
        KBD = sb("k_block_diagonal", [P, B, HG, SEQ])
        EW = 2 * F + FC + D
        LATE = sb("position_bias_then_experts", [P, max(T * H * SEQ, E * EW)])
        BIAS = LATE[:, 0:T * H * SEQ].rearrange("p (t h j) -> p t h j", t=T, h=H)
        VBD = sb("v_block_diagonal", [P, B, HG, 2, DH + 1])
        SSB = sb("scores_sb", [P, 2, HG, SEQ])
        SM = sb("scores_less_max", [P, 2, HG, SEQ])
        PT = sb("probsT", [P, 2, HG // 2, P])
        ON = sb("attention_out", [P, T, D])
        ident = sb("ident", [P, P])
        warm = sb("warm", [P, BANK], BF16)
        mask8 = sb("head_mask", [P, HG])
        slope = sb("slope", [P, H])
        bmask = sb("batch_row_mask", [P, 2])
        neg_half = sb("neg_half", [P, T])
        w2b = sb("w2_over_rows", [P, SEQ])
        bsim = sb("b_sim", [P, 1])
        gates = sb("gates", [P, 4])
        tg = sb("tanh_gates", [P, 4])
        TG_A, TG_C, TG_B, TG_D = (tg[:, i:i + 1] for i in range(4))
        bqv = sb("b_qv_rows", [P, D])
        bqvg = sb("b_qv_gated", [P, D])
        wqv = sb("w_qv", [P, 4, D])
        wfi = sb("ffn_w_int", [P, 3 * HC, D], I32)
        wff = wfi[:, :, :].bitcast(F32)
        wfT = sb("ffn_wT", [P, 3 * HC, P])
        SG = sb("silu_gate", [P, 2, BANK])
        xw = sb("xattn_w", [P, 4, D])
        xwT = sb("xattn_wT", [P, 4, P])
        kpos = sb("key_pos_rows", [P, T, SEQ], I32)
        msk = sb("mask", [P, T, SEQ], I32)
        mneg = msk[:, :, :].bitcast(F32)
        ndist = sb("minus_dist", [P, T, SEQ])
        sim = sb("sim_less_max", [P, T, SEQ])
        BASE = sb("attnT_then_base_rows", [P, T, ROW])
        AT = BASE[:, :, 0:P]
        stats = sb("bn_stats", [P, T, 6])
        mv = sb("mean_var", [P, T, 2])
        ve = sb("var_plus_eps", [P, T])
        ve2 = sb("var_plus_eps_inner", [P, T])
        rstd = sb("rstd", [P, T])
        rstd1 = sb("rstd_outer", [P, T])
        m8 = sb("row_max", [P, T])
        mf8 = sb("row_max_sim", [P, T])
        s8 = sb("row_sum", [P, T])
        r8 = sb("row_recip", [P, T])
        bt = sb("batt_rows", [HALF, 2, 2, SEQ])
        bts = sb("batt_stats", [HALF, 2, 3, 2])
        battm = sb("batt_masked", [P, T, 2])
        hc = sb("hc_barT", [P, B])
        mx = sb("head_max", [P, 2, HG])
        den = sb("head_den", [P, T, H])
        rec = sb("head_recip", [P, T, H])
        wqkv = sb("w_qkv", [P, 3 * D])
        bqs = sb("b_q_scaled", [P, 1])
        bv = sb("b_v_rows", [P, D])
        wo = sb("w_o", [P, D])
        bo = sb("b_o_rows", [P, D])
        wgc = sb("gate_and_coef_w", [P, E + 2])
        coefb = sb("coef_b_rows", [P, 2])
        lg = sb("logits", [P, T, E + 2])
        gm = sb("gate_small", [P, T, 8])
        ge = sb("gate_exp", [P, T, E])
        oh = sb("one_hot", [P, T, E])
        rev = sb("expert_rank", [P, E])
        tri = sb("before", [P, P])
        ones = sb("ones", [P, P])
        ranks = sb("ranks", [P, 5, T * E])
        seg = sb("scan_restarts", [P, E, T])
        nth = sb("multiples", [P, E, T])
        blk = sb("block_numbers", [1, BLOCKS, E])
        cnt = sb("block_counts", [P, 4, E])
        own = sb("block_of_expert", [1, BLOCKS, E])
        bexp = sb("block_expert", [1, BLOCKS])
        bexpi = sb("block_expert_int", [1, BLOCKS], I32)
        slot = sb("slot", [P, T], I32)
        fill = sb("empty_row", [P, ROW])
        HB2 = SSB[:, :, :, :].rearrange("p u h j -> p (u h j)").rearrange("p (u c n) -> p u c n", u=2, c=FC)
        sm_flat = SM[:, :, :, :].rearrange("p u h j -> p (u h j)").rearrange("p (u d) -> p u d", d=D)
        XST, YB, OUTB = sm_flat[:, 0:2, :], sm_flat[:, 2:4, :], sm_flat[:, 4:8, :]
        rw1 = sb("rW1", [P, F])
        rw2 = sb("rW2", [P, FC, D])
        rb2 = sb("rb2_rows", [P, D])
        VEC = (("L1_ffn_bqkv", 3), ("L1_ffn_ln1_g", 1), ("L1_ffn_ln1_b", 1),
               ("L1_ffn_ln2_g", 1), ("L1_ffn_ln2_b", 1), ("L1_ffn_b1", E * FC), ("L1_ffn_rb1", FC))
        NVEC = sum(n for _, n in VEC)
        srows = sb("w_sim_rows", [3, P])
        wsim = sb("w_sim_cols", [P, 3])
        vrows = sb("vector_rows", [NVEC, P])
        vec = sb("vector_cols", [P, NVEC])
        bqk, ln1, ln2 = vec[:, 0:2], vec[:, 3:5], vec[:, 5:7]
        b1 = vec[:, 7:7 + (E + 1) * FC].rearrange("p (e c) -> p e c", c=FC)
        qrows = sb("query_pos_rows", [T, P], I32)
        qrowf = sb("query_pos_rows_f32", [T, P])
        qpos = sb("query_pos_cols", [P, T])
        experts = LATE[:, 0:E * EW].rearrange("p (e w) -> p e w", e=E)
        w1_all = experts[:, :, 0:F]
        w2_all = experts[:, :, F:2 * F].rearrange("p e (c d) -> p e c d", c=FC)
        b1_all = experts[:, :, 2 * F:2 * F + FC]
        b2_all = experts[:, :, 2 * F + FC:EW]
        spare = KBD[:, :, :, :].rearrange("p b h j -> p (b h j)")
        WBUF = spare[:, 0:WB * EW].rearrange("p (k w) -> p k w", k=WB)
        XS = spare[:, WB * EW:WB * EW + SLOTS].rearrange("p (k d) -> p k d", k=BLOCKS)
        BS = spare[:, WB * EW + SLOTS:WB * EW + SLOTS + BLOCKS * ROW].rearrange("p (k r) -> p k r", k=BLOCKS)
        assert WB * EW + SLOTS + BLOCKS * ROW <= B * HG * SEQ

        xs_dram = nc.dram_tensor("xs_by_slot", (SLOTS, D), F32).ap()
        bs_dram = nc.dram_tensor("base_by_slot", (SLOTS, ROW), F32).ap()
        PS = ctx.enter_context(nc.psum_tensor("ps", [P, 8, BANK], F32))

        USES = [("early", 0, 5), ("ctxT", 0, 6), ("ctxT", 1, 7), ("xnT_A", 0, 2), ("xnT_A", 1, 3), ("sim", 0, 4),
                ("sim", 1, 5), ("xwT", 0, 0), ("fwT", 0, 1), ("fwT", 1, 6), ("fwT", 2, 7), ("mT", 0, 2), ("mT", 1, 3),
                ("k_C", 0, 0), ("aT", 0, 4), ("k_C", 1, 1), ("aT", 1, 5), ("btT", 0, 2), ("hq", 0, 6), ("hc", 0, 3),
                ("btT", 1, 2), ("hq", 1, 7), ("hc", 1, 3), ("v_C", 0, 0), ("v_C", 1, 1), ("y_A", 0, 4), ("vecT", 0, 6),
                ("y_A", 1, 5), ("xnT_B", 0, 6)]
        USES += [u for i in range(HC) for u in (("gate", i, i % 2), ("up", i, 2 + i % 2))] + [("xnT_B", 1, 7), ("y_B", 0, 4)]
        USES += [u for i in range(HC, 2 * HC) for u in (("gate", i, i % 2), ("up", i, 2 + i % 2))] + [("y_B", 1, 5)]
        USES += [("xnT_C", 0, 6), ("q_C", 0, 6), ("xnT_C", 1, 7), ("q_C", 1, 7)]
        for k, kind in enumerate("CD"):
            for n in range(CH + 2):
                if n < CH:
                    USES.append((f"s_{kind}", n, 4 + n % 2))
                if 1 <= n <= CH:
                    USES.append((f"t_{kind}", n - 1, (n - 1) % 2))
                if n >= 2 and n % R == 0:
                    USES.append((f"o_{kind}", (n - 2) // R, 2 + (n - 2) // R % 2))
                USES += {("C", 11): [("onT_C", 0, 6)], ("C", 12): [("y_C", 0, 7)], ("C", 15): [("xnT_D", 0, 6)],
                         ("C", 17): [("q_D", 0, 7), ("k_D", 0, 6), ("v_D", 0, 7)],
                         ("D", 1): [("onT_C", 1, 6)], ("D", 2): [("y_C", 1, 7)], ("D", 5): [("xnT_D", 1, 6)],
                         ("D", 6): [("q_D", 1, 7), ("k_D", 1, 6), ("v_D", 1, 7)],
                         ("D", 11): [("onT_D", 0, 6)], ("D", 12): [("y_D", 0, 7)], ("D", 15): [("xnT_E", 0, 6)],
                         ("D", 16): [("lg", 0, 7)]}.get((kind, n), [])
        HBANKS = (0, 1, 4, 5)
        DENSE = [("dense", i, HBANKS[i % 4]) for i in range(2 * FC)]
        USES += [("onT_D", 1, 6), DENSE[0], ("y_D", 1, 7)] + DENSE[1:FC] + [("xnT_E", 1, 6), ("lg", 1, 7)]
        USES += DENSE[FC:FC + 2] + [("rank", 0, 6)] + DENSE[FC + 2:] + [("ry", 0, 2), ("ry", 1, 3), ("xsT", 0, 6)]
        for k in range(BLOCKS + 1):
            if k + 1 < BLOCKS:
                USES.append(("xsT", k + 1, 6 + (k + 1) % 2))
            if k < BLOCKS:
                USES.append(("eh", k, k % 2))
            if k >= 1:
                USES.append(("ey", k - 1, 4 + (k - 1) % 2))
        use = {}
        for name, i, b in USES:
            use[name, i] = (b, sum(1 for x, _ in use.values() if x == b))

        bank_full = [sem(f"bank{b}_full") for b in range(8)]
        bank_taken = [sem(f"bank{b}_taken") for b in range(8)]

        def bank(name, i=0):
            return use[name, i][0]

        def filled(name, i=0):
            b, n = use[name, i]
            return bank_full[b], n + 1

        def taken(name, i=0):
            b, n = use[name, i]
            return bank_taken[b], n + 1

        def empty(pe, name, i=0):
            b, n = use[name, i]
            if n:
                pe.wait_ge(bank_taken[b], n)
            return b

        (ctx_in, wsim_in, qrow_in, bsim_in, xw_in, fw_in, pos_in, gate_in, rows_in, wqv_in, w_in, vec_in, moe_in, rmlp_in,
         prefilled, x_scattered, base_scattered, bs_in) = (
            sem(n) for n in ("ctx_in wsim_in qrow_in bsim_in xw_in fw_in pos_in gate_in rows_in wqv_in w_in vec_in moe_in rmlp_in "
                             "prefilled x_scattered base_scattered bs_in").split())
        x_in = [sem("x0_in"), sem("x1_in")]
        xs_in = [sem(f"xs_in{n}") for n in range(3)]
        out_done = [sem(f"out_done{n}") for n in range(4)]
        ident_ready, mask_ready, rstd_ready, rstd1_ready, xb_ready, bias_ready, fill_ready, sub_ready, warm_ready, pv_first = (
            sem(n) for n in "ident_ready mask_ready rstd_ready rstd1_ready xb_ready bias_ready fill_ready sub_ready warm_ready pv_first".split())
        tg_ready, qrow_ready, fw_ready, a_exp, batt_exp, silu_ready, p_ready, kbd_act, gexp_ready = (
            sem(n) for n in "tg_ready qrow_ready fw_ready a_exp batt_exp silu_ready p_ready kbd_act gexp_ready".split())
        (var_ready, var1_ready, xn_ready, w2b_ready, c3_ready, mf_ready, sim_ready, a_ready, btmax_ready, bt_ready, battm_ready,
         feat_ready, h_ready, mx_ready, sm_ready, on_ready, kbd_dve, k_ready, gsum_ready, oh_ready, slot_ready, base_ready,
         x3_ready, w_copied, xsT_ready, ey_ready, bqs_ready) = (
            sem(n) for n in ("var_ready var1_ready xn_ready w2b_ready c3_ready mf_ready sim_ready a_ready btmax_ready bt_ready "
                             "battm_ready feat_ready h_ready mx_ready sm_ready on_ready kbd_dve k_ready gsum_ready oh_ready "
                             "slot_ready base_ready x3_ready w_copied xsT_ready ey_ready bqs_ready").split())
        dve_step, act_step, pool_step = sem("dve_step"), sem("act_step"), sem("pool_step")
        block = ctx.enter_context(nc.Block())

        def tokens(ap):
            return ap.rearrange("(t q) s d -> (q s) t d", q=2)

        def rows(ap, n=P):
            return ap.unsqueeze(0).broadcast_to([n, ap.shape[0]])

        def over(ap, axis, shape):
            return ap.unsqueeze(axis).broadcast_to(shape)

        def tiles(h):
            return slice(h * HALF, (h + 1) * HALF)

        def half(h):
            return slice(h * BANK, (h + 1) * BANK)

        def tile_cols(t):
            return slice((t % HALF) * P, (t % HALF + 1) * P)

        def by_tile(b):
            return PS[:, b, :].rearrange("p (t d) -> p t d", t=HALF)

        VECS = 16 * len(VEC)
        POS = 16 * 3
        ROWS = 16 * 4
        WEIGHTS = 16 * 4
        MOE = 16 * (1 + E + 1)
        XS_PARTS = ((0, 2), (2, 7), (7, BLOCKS))
        KD = 5
        STAGES = "ABCDE"

        @block.sync
        def _(sp):
            for h in range(2):
                sp.dma_start(X0[:, tiles(h), :], tokens(a["x"])[:, tiles(h), :]).then_inc(x_in[h], 16)
            sp.dma_start(qrows[:, :], a["itok_BxS_8_8191"].rearrange("(t q) s -> t (q s)", q=2)).then_inc(qrow_in, 16)
            for q in range(2):
                sp.dma_start(kpos[q * SEQ:(q + 1) * SEQ, :, :],
                             over(a["itok_BxS2_1_8191"].rearrange("(t q) s -> q t s", q=2)[q], 0, [SEQ, T, SEQ])).then_inc(pos_in, 16)
            sp.dma_start(msk[:, :, :], a["mask_BxSxS2_if1"].rearrange("(t q) i j -> (q i) t j", q=2)).then_inc(pos_in, 16)
            for n, name in enumerate(("L1_xattn_W_q", "L1_xattn_W_k", "L1_xattn_W_v", "L1_xattn_W_o")):
                sp.dma_start(xw[:, n, :], a[name]).then_inc(xw_in, 16)
            sp.dma_start(wqv[:, :, :], a["L0_xattn_W_qv"].rearrange("(c p) d -> p c d", p=P)).then_inc(wqv_in, 16)
            at = 0
            for name, n in VEC:
                src = a[name] if n > 1 else a[name].unsqueeze(0)
                if name == "L1_ffn_b1":
                    src = src.rearrange("e (c p) -> (e c) p", p=P)
                elif n > 1:
                    src = src.rearrange("(c p) -> c p", p=P)
                sp.dma_start(vrows[at:at + n, :], src).then_inc(vec_in, 16)
                at += n
            sp.dma_start(wqkv[:, :], a["L1_ffn_Wqkv"]).then_inc(w_in, 16)
            sp.dma_start(wo[:, :], a["L1_ffn_Wo"]).then_inc(w_in, 16)
            sp.dma_start(wgc[:, 0:E], a["L1_ffn_gate_w"]).then_inc(w_in, 16)
            sp.dma_start(wgc[:, E:E + 2], a["L1_ffn_coef_w"]).then_inc(w_in, 16)
            for dst, src in ((bv, a["L1_ffn_bqkv"][2 * D:3 * D]), (bo, a["L1_ffn_bo"]), (rb2, a["L1_ffn_rb2"]),
                             (coefb, a["L1_ffn_coef_b"])):
                sp.dma_start(dst[:, :], rows(src)).then_inc(rows_in, 16)
            sp.dma_start(rw1[:, :], a["L1_ffn_rW1"]).then_inc(rmlp_in, 16)
            sp.dma_start(rw2[:, :, :], a["L1_ffn_rW2"].rearrange("(c p) d -> p c d", p=P)).then_inc(rmlp_in, 16)
            sp.wait_ge(fill_ready, 1)
            sp.dma_start(xs_dram.rearrange("(k p) d -> p k d", p=P), over(fill[:, 0:D], 1, [P, BLOCKS, D])).then_inc(prefilled, 16)
            sp.dma_start(bs_dram.rearrange("(k p) r -> p k r", p=P), over(fill[:, :], 1, [P, BLOCKS, ROW])).then_inc(prefilled, 16)
            sp.wait_ge(*taken("s_C", CH - 2))
            sp.wait_ge(*taken("s_C", CH - 1))
            sp.dma_start(w1_all, a["L1_ffn_W1"].rearrange("e p f -> p e f")).then_inc(moe_in, 16)
            for e in range(E):
                sp.dma_start(w2_all[:, e, :, :], a["L1_ffn_W2"][e].rearrange("(c p) d -> p c d", p=P)).then_inc(moe_in, 16)
            sp.dma_start(b2_all, over(a["L1_ffn_b2"], 0, [P, E, D])).then_inc(moe_in, 16)
            sp.wait_ge(x_scattered, 16 * T)
            for n, (k0, k1) in enumerate(XS_PARTS):
                sp.dma_start(XS[:, k0:k1, :], xs_dram.rearrange("(k p) d -> p k d", p=P)[:, k0:k1, :]).then_inc(xs_in[n], 16)
            sp.wait_ge(base_scattered, 16 * T)
            sp.dma_start(BS, bs_dram.rearrange("(k p) r -> p k r", p=P)).then_inc(bs_in, 16)

        @block.scalar
        def _(act):
            def copy(dst, src, scale=None):
                if scale is None:
                    return nc.scalar.activation(dst, src, ACT.Copy)
                return nc.scalar.activation(dst, src, ACT.Copy, scale=scale)

            act.dma_start(srows[:, :], a["L0_xattn_w_sim"].rearrange("(c p) -> c p", p=P)).then_inc(wsim_in, 16)
            act.dma_start(C[:, :, :], tokens(a["ctx_1024"])).then_inc(ctx_in, 16)
            act.dma_start(gates[:, 0:2], rows(a["g_xattn"])).then_inc(gate_in, 16)
            act.dma_start(gates[:, 2:4], rows(a["g_ffn"])).then_inc(gate_in, 16)
            act.dma_start(bsim[:, :], rows(a["L0_xattn_b_sim"])).then_inc(bsim_in, 16)
            act.dma_start(bqv[:, :], rows(a["L0_xattn_b_qv"])).then_inc(bsim_in, 16)
            for n, name in enumerate(("L0_ffn_w_gate", "L0_ffn_w_up")):
                act.dma_start(wfi[:, n * HC:(n + 1) * HC, :], a[name].rearrange("(c p) d -> p c d", p=P)).then_inc(fw_in, 16)
            act.dma_start(wfi[:, 2 * HC:3 * HC, :], a["L0_ffn_w_down"].rearrange("p (c d) -> p c d", c=HC)).then_inc(fw_in, 16)

            act.wait_ge(qrow_in, 16)
            copy(qrowf[:, :], qrows[:, :]).then_inc(qrow_ready, 1)
            for h in range(2):
                act.wait_ge(*filled("ctxT", h))
                copy(CT[:, half(h)], PS[:, bank("ctxT", h), :]).then_inc(taken("ctxT", h)[0], 1)
            act.wait_ge(*filled("early"))
            copy(wsim[:, :], PS[:, bank("early"), 0:3])
            copy(qpos[:, :], PS[:, bank("early"), 3:3 + T]).then_inc(taken("early")[0], 1)
            act.wait_ge(gate_in, 32)
            nc.scalar.activation(tg[:, :], gates[:, :], ACT.Tanh).then_inc(tg_ready, 1)
            for h in range(2):
                act.wait_ge(*filled("xnT_A", h))
                copy(XT[:, half(h)], PS[:, bank("xnT_A", h), :]).then_inc(taken("xnT_A", h)[0], 1)
            act.wait_ge(fw_in, 48)
            copy(wff, wfi[:, :, :], float(np.float32(1.0 / 127.0))).then_inc(fw_ready, 1)
            act.wait_ge(*filled("xwT"))
            copy(xwT[:, :, :].rearrange("p c d -> p (c d)"), PS[:, bank("xwT"), :]).then_inc(taken("xwT")[0], 1)
            for h in range(2):
                act.wait_ge(sim_ready, h + 1)
                nc.scalar.activation(sim[:, tiles(h), :], sim[:, tiles(h), :], ACT.Exp).then_inc(a_exp, 1)
                act.wait_ge(btmax_ready, h + 1)
                nc.scalar.activation(bt[:, h, :, :], bt[:, h, :, :], ACT.Exp).then_inc(batt_exp, 1)
            for n in range(3):
                act.wait_ge(*filled("fwT", n))
                k = min(4, 3 * HC - 4 * n)
                copy(wfT[:, 4 * n:4 * n + k, :].rearrange("p c d -> p (c d)"), PS[:, bank("fwT", n), 0:k * P]).then_inc(taken("fwT", n)[0], 1)
            for h in range(2):
                act.wait_ge(*filled("k_C", h))
                copy(KT[:, half(h)], PS[:, bank("k_C", h), :]).then_inc(taken("k_C", h)[0], 1)
                act.wait_ge(*filled("aT", h))
                copy(AT[:, tiles(h), :], by_tile(bank("aT", h))).then_inc(taken("aT", h)[0], 1)
            for h in range(2):
                act.wait_ge(*filled("hq", h))
                copy(HT[:, half(h)], PS[:, bank("hq", h), :]).then_inc(taken("hq", h)[0], 1)
            act.wait_ge(mask_ready, 2)
            for h in range(2):
                act.wait_ge(*filled("v_C", h))
                for u in range(2):
                    rs = slice(u * SEQ, (u + 1) * SEQ)
                    r = copy(VBD[rs, h * BH:(h + 1) * BH, :, u, 0:DH],
                             PS[rs, bank("v_C", h), :].rearrange("p (b m d) -> p b m d", b=BH, d=DH))
                r.then_inc(taken("v_C", h)[0], 1)
            act.wait_ge(*filled("vecT"))
            copy(vec[:, :], PS[:, bank("vecT"), 0:NVEC]).then_inc(taken("vecT")[0], 1)
            act.wait_ge(*taken("k_C", 1))

            def keys(h, heads):
                for m in heads:
                    nc.scalar.activation(KBD[:, h * BH:(h + 1) * BH, m, :], KT[:, half(h)].rearrange("p (b j) -> p b j", b=BH),
                                         ACT.Copy, scale=mask8[:, m:m + 1]).then_inc(kbd_act, 1)

            for h in range(2):
                act.wait_ge(*filled("xnT_B", h))
                copy(XT[:, half(h)], PS[:, bank("xnT_B", h), :]).then_inc(taken("xnT_B", h)[0], 1)
                for i in range(h * HC, (h + 1) * HC):
                    act.wait_ge(*filled("gate", i))
                    if i >= 2:
                        act.wait_ge(h_ready, i - 1)
                    nc.scalar.activation(SG[:, i % 2, :], PS[:, bank("gate", i), :], ACT.Silu).then_inc(taken("gate", i)[0], 1)
                    if h == 0 or i == 2 * HC - 1:
                        keys(1, range(2 * (i % HC), 2 * (i % HC) + 2) if h == 0 else range(2 * HC, HG))

            def queries(kind, h):
                act.wait_ge(*filled(f"q_{kind}", h))
                o, i = QT[:, half(h)], PS[:, bank(f"q_{kind}", h), :]
                r = copy(o, i, SCALE) if kind == "C" else nc.scalar.activation(o, i, ACT.Identity, bias=bqs[:, 0:1], scale=SCALE)
                r.then_inc(taken(f"q_{kind}", h)[0], 1)

            def normed(kind, h, ln=None):
                act.wait_ge(*filled(f"xnT_{kind}", h))
                o, i = XT[:, half(h)], PS[:, bank(f"xnT_{kind}", h), :]
                r = copy(o, i) if ln is None else nc.scalar.activation(o, i, ACT.Identity, bias=ln[:, 1:2], scale=ln[:, 0:1])
                r.then_inc(taken(f"xnT_{kind}", h)[0], 1)

            def attended(kind, h):
                act.wait_ge(*filled(f"onT_{kind}", h))
                copy(XT[:, half(h)], PS[:, bank(f"onT_{kind}", h), :]).then_inc(taken(f"onT_{kind}", h)[0], 1)

            def probs(k, n):
                kind, g = "CD"[k], CH * k + n
                act.wait_ge(*filled(f"t_{kind}", n))
                if g >= 2:
                    act.wait_ge(*(filled("o_C" if g - 2 < CH else "o_D", (g - 2) % CH // R)
                                  if (g - 2) % R == R - 1 else (pv_first, (g - 2) // R + 1)))
                nc.scalar.activation(PT[:, g % 2, :, :].rearrange("p c d -> p (c d)"), PS[:, bank(f"t_{kind}", n), :],
                                     ACT.Exp).then_inc(taken(f"t_{kind}", n)[0], 1)

            normed("C", 0)
            queries("C", 0)
            normed("C", 1)
            queries("C", 1)
            for n in range(CH + 2):
                if 1 <= n <= CH:
                    probs(0, n - 1)
                if n == 11:
                    attended("C", 0)
                if n == 15:
                    act.wait_ge(*taken("vecT"))
                    normed("D", 0, ln1)
            queries("D", 0)
            act.wait_ge(k_ready, 1)
            keys(0, range(KD, HG))
            for n in range(CH + 2):
                if 1 <= n <= CH:
                    probs(1, n - 1)
                if n == 1:
                    attended("C", 1)
                if n == 5:
                    normed("D", 1, ln1)
                if n == 6:
                    queries("D", 1)
                    act.wait_ge(k_ready, 2)
                    keys(1, range(KD, HG))
                if n == 11:
                    attended("D", 0)
                if n == 15:
                    normed("E", 0, ln2)

            def dense(i):
                h, c = divmod(i, FC)
                act.wait_ge(*filled("dense", i))
                nc.scalar.activation(HR[:, c, half(h)], PS[:, bank("dense", i), :], ACT.Gelu, bias=b1[:, E, c:c + 1])\
                    .then_inc(taken("dense", i)[0], 1)

            attended("D", 1)
            for i in range(FC):
                dense(i)
            normed("E", 1, ln2)
            act.wait_ge(gsum_ready, 1)
            nc.scalar.activation(ge[:, :, :], ge[:, :, :], ACT.Exp)
            nc.scalar.activation(gm[:, :, 2:4], gm[:, :, 2:4], ACT.Exp).then_inc(gexp_ready, 1)
            for i in range(FC, 2 * FC):
                dense(i)
            for k in range(BLOCKS):
                act.wait_ge(*filled("eh", k))
                if k >= 2:
                    act.wait_ge(*filled("ey", k - 2))
                for c in range(FC):
                    r = nc.scalar.activation(HB2[:, k % 2, c, :], PS[:, bank("eh", k), c * P:(c + 1) * P], ACT.Gelu,
                                             bias=WBUF[:, k % WB, 2 * F + c:2 * F + c + 1])
                r.then_inc(taken("eh", k)[0], 1)

        @block.gpsimd
        def _(pool):
            steps = [0]

            def link(ins):
                steps[0] += 1
                ins.then_inc(pool_step, 1)
                pool.wait_ge(pool_step, steps[0])

            g = nc.gpsimd
            g.memset(warm[:], 0.0).then_inc(warm_ready, 1)
            link(g.memset(ident[:], 0.0))
            g.affine_select(out=ident[:, :], in_=ident[:, :], compare_op=ALU.not_equal, fill=1.0, base=0,
                            pattern=[[-1, P]], channel_multiplier=1).then_inc(ident_ready, 1)
            g.memset(neg_half[:], -0.5)
            g.memset(bmask[:], 0.0)
            link(g.memset(mask8[:], 1.0))

            def rsqrt(stage, h):
                k = 2 * STAGES.index(stage) + h
                pool.wait_ge(var_ready, k + 1)
                g.tensor_tensor(rstd[:, tiles(h)], ve[:, tiles(h)], neg_half[:, tiles(h)], ALU.pow).then_inc(rstd_ready, 1)

            for r in range(R):
                v = mask8[r * SEQ:(r + 1) * SEQ, :]
                link(g.affine_select(out=v, in_=v, compare_op=ALU.is_ge, fill=0.0, base=0,
                                     pattern=[[-DH, HG]], channel_multiplier=1))
                link(g.affine_select(out=v, in_=v, compare_op=ALU.is_ge, fill=0.0, base=DH - 1,
                                     pattern=[[DH, HG]], channel_multiplier=-1))
                link(g.memset(bmask[r * SEQ:(r + 1) * SEQ, r:r + 1], 1.0))
            g.memset(ABD[:, :, :], 0.0)
            rsqrt("A", 0)
            rsqrt("A", 1)
            g.memset(VBD[:, :, :, :, :], 0.0)
            for h in range(H):
                r = g.memset(slope[:, h:h + 1], slopes[h])
            link(r)
            for u in range(2):
                g.memset(VBD[u * SEQ:(u + 1) * SEQ, :, :, u, DH:DH + 1], 1.0).then_inc(mask_ready, 1)
                pool.wait_ge(mask_ready, u + 1)
            pool.wait_ge(bsim_in, 32)
            pool.wait_ge(tg_ready, 1)
            link(g.tensor_scalar(bqvg[:, :], bqv[:, :], TG_A, None, ALU.mult))
            for h in range(2):
                pool.wait_ge(x_in[h], 16)
            g.tensor_tensor(XB[:, :, :], X0[:, :, :], over(bqvg[:, :], 1, [P, T, D]), ALU.add).then_inc(xb_ready, 1)
            pool.wait_ge(pos_in, POS)
            link(g.tensor_scalar(mneg, msk[:, :, :], 0.0, -3e38, ALU.is_equal, ALU.mult))
            link(g.tensor_scalar(mneg, mneg, 10.0, None, ALU.mult))
            pool.wait_ge(*taken("early"))
            link(g.tensor_copy(ndist[:, :, :], kpos[:, :, :]))
            link(g.tensor_tensor(ndist[:, :, :], ndist[:, :, :], over(qpos[:, :], 2, [P, T, SEQ]), ALU.subtract))
            link(g.tensor_tensor(ndist[:, :, :], ndist[:, :, :], mneg, ALU.add))

            def bias(t):
                g.tensor_tensor(BIAS[:, t, :, :], over(ndist[:, t, :], 1, [P, H, SEQ]),
                                over(slope[:, :], 2, [P, H, SEQ]), ALU.mult).then_inc(bias_ready, 1)

            for t in range(HALF):
                bias(t)
            rsqrt("B", 0)
            rsqrt("B", 1)
            for t in range(HALF, T):
                bias(t)
            rsqrt("C", 0)
            rsqrt("C", 1)

            def less_max(n):
                pool.wait_ge(mx_ready, n + 1)
                if n >= 2:
                    pool.wait_ge(*filled("t_C", n - 2))
                g.tensor_tensor(SM[:, n % 2, :, :], SSB[:, n % 2, :, :], over(mx[:, n % 2, :], 2, [P, HG, SEQ]),
                                ALU.subtract).then_inc(sub_ready, 1)

            def outer_norm(h):
                pool.wait_ge(var1_ready, h + 1)
                link(g.tensor_tensor(rstd1[:, tiles(h)], ve2[:, tiles(h)], neg_half[:, tiles(h)], ALU.pow))
                for t in range(h * HALF, (h + 1) * HALF):
                    r = g.tensor_scalar(U[:, t, :], X3[:, t, :], mv[:, t, 0:1], rstd1[:, t:t + 1], ALU.subtract, ALU.mult)
                link(r)
                g.tensor_tensor(XB[:, tiles(h), :], U[:, tiles(h), :], over(bo[:, :], 1, [P, HALF, D]), ALU.add).then_inc(xb_ready, 1)

            for n in range(CH):
                less_max(n)
                if n == 14:
                    rsqrt("D", 0)
            pool.wait_ge(rows_in, ROWS)
            outer_norm(0)
            rsqrt("D", 1)
            outer_norm(1)
            g.memset(ones[:], 1.0)
            for e in range(E):
                g.memset(rev[:, e:e + 1], float(E - e))
            link(g.memset(tri[:], 1.0))
            g.affine_select(out=tri[:, :], in_=tri[:, :], compare_op=ALU.is_gt, fill=0.0, base=0,
                            pattern=[[1, P]], channel_multiplier=-1)
            link(g.memset(seg[:, :, :], 1.0))
            g.memset(seg[:, :, 0:1], 0.0)
            for k in range(T):
                g.memset(nth[:, :, k:k + 1], float(P * k))
            for k in range(BLOCKS):
                r = g.memset(blk[:, k, :], float(k))
            link(r)
            link(g.memset(fill[:, :], 0.0))
            g.memset(fill[:, D:D + 1].bitcast(I32), NOWHERE).then_inc(fill_ready, 1)
            g.iota(BASE[:, :, D:D + 1].bitcast(I32), [[P, T], [1, 1]], base=0, channel_multiplier=1)
            g.memset(BASE[:, :, D + 2:D + 4], 0.0).then_inc(mask_ready, 1)
            rsqrt("E", 0)
            rsqrt("E", 1)
            pool.wait_ge(prefilled, 32)
            pool.wait_ge(slot_ready, 1)
            for t in range(T):
                g.indirect_dma_start(xs_dram, bass.IndirectOffsetOnAxis(ap=slot[:, t:t + 1], axis=0), XN[:, t, :], None)\
                    .then_inc(x_scattered, 16)
            for t in range(T):
                pool.wait_ge(base_ready, t + 1)
                g.indirect_dma_start(bs_dram, bass.IndirectOffsetOnAxis(ap=slot[:, t:t + 1], axis=0), BASE[:, t, :], None)\
                    .then_inc(base_scattered, 16)
            for k in range(BLOCKS):
                pool.wait_ge(ey_ready, k + 1)
                g.indirect_dma_start(out.rearrange("b s d -> (b s) d"),
                                     bass.IndirectOffsetOnAxis(ap=BS[:, k, D:D + 1].bitcast(I32), axis=0),
                                     OUTB[:, k % 4, :], None, bounds_check=N - 1, oob_is_err=False).then_inc(out_done[k % 4], 16)
            for n in range(4):
                pool.wait_ge(out_done[n], 16 * len(range(n, BLOCKS, 4)))

        @block.vector
        def _(dve):
            steps = [0]
            v = nc.vector

            def link(ins):
                steps[0] += 1
                ins.then_inc(dve_step, 1)
                dve.wait_ge(dve_step, steps[0])

            def moments(stage, h, src):
                for t in range(h * HALF, (h + 1) * HALF):
                    last = v.bn_stats(stats[:, t, :], src[:, t, :])
                link(last)
                for t in range(h * HALF, (h + 1) * HALF):
                    last = v.bn_aggr(mv[:, t, :], stats[:, t, :])
                link(last)
                var = mv[:, tiles(h), 1]
                if stage != "D":
                    v.tensor_scalar(ve[:, tiles(h)], var, EPS, None, ALU.add).then_inc(var_ready, 1)
                else:
                    v.tensor_scalar(ve[:, tiles(h)], var, 1.0 + EPS, EPS * EPS, ALU.mult, ALU.add).then_inc(var_ready, 1)
                    v.tensor_scalar(ve2[:, tiles(h)], var, EPS, None, ALU.add).then_inc(var1_ready, 1)

            def normalise(stage, h, src):
                dve.wait_ge(rstd_ready, 2 * STAGES.index(stage) + h + 1)
                for t in range(h * HALF, (h + 1) * HALF):
                    r = v.tensor_scalar(XN[:, t, :], src[:, t, :], mv[:, t, 0:1], rstd[:, t:t + 1], ALU.subtract, ALU.mult)
                r.then_inc(xn_ready, 1)

            def residual(stage, h, xin, xout, gate):
                dve.wait_ge(*filled(f"y_{stage}", h))
                yp = by_tile(bank(f"y_{stage}", h))
                if gate is None:
                    r = v.tensor_tensor(xout[:, tiles(h), :], yp, xin[:, tiles(h), :], ALU.add)
                else:
                    r = v.scalar_tensor_tensor(xout[:, tiles(h), :], yp, gate, xin[:, tiles(h), :], ALU.mult, ALU.add)
                r.then_inc(taken(f"y_{stage}", h)[0], 1)
                dve.wait_ge(*taken(f"y_{stage}", h))

            for h in range(2):
                dve.wait_ge(x_in[h], 16)
                moments("A", h, X0)
            for h in range(2):
                normalise("A", h, X0)
            v.memset(w2b[:, :], 0.0).then_inc(w2b_ready, 1)
            dve.wait_ge(w2b_ready, 1)
            dve.wait_ge(*taken("early"))
            v.tensor_scalar(w2b[:, :], w2b[:, :], wsim[:, 1:2], None, ALU.add).then_inc(w2b_ready, 1)
            for h in range(2):
                dve.wait_ge(*taken("ctxT", h))
                v.tensor_scalar(C3T[:, half(h)], CT[:, half(h)], wsim[:, 2:3], wsim[:, 0:1], ALU.mult, ALU.add).then_inc(c3_ready, 1)
            dve.wait_ge(bsim_in, 32)
            for h in range(2):
                dve.wait_ge(*filled("sim", h))
                S3 = PS[:, bank("sim", h), 0:HALF * SEQ].rearrange("p (t j) -> p t j", t=HALF)
                link(v.tensor_reduce(m8[:, tiles(h)], S3, AX_X, ALU.max))
                v.tensor_scalar(mf8[:, tiles(h)], m8[:, tiles(h)], bsim[:, 0:1], None, ALU.add).then_inc(mf_ready, 1)
                v.tensor_tensor(sim[:, tiles(h), :], S3, over(m8[:, tiles(h)], 2, [P, HALF, SEQ]), ALU.subtract)\
                    .then_inc(taken("sim", h)[0], 1)
                dve.wait_ge(*taken("sim", h))
                v.tensor_copy(s8[:, 0:1], m8[:, 0:1]).then_inc(sim_ready, 1)
            for h in range(2):
                dve.wait_ge(*filled("mT", h))
                M3 = PS[0:HALF, bank("mT", h), 0:P].rearrange("p (q i) -> p q i", q=2)
                link(v.tensor_reduce(bts[:, h, 0, :], M3, AX_X, ALU.max))
                link(v.tensor_tensor(bt[:, h, :, :], M3, over(bts[:, h, 0, :], 2, [HALF, 2, SEQ]), ALU.subtract))
                v.tensor_copy(bts[:, h, 1, :], bts[:, h, 0, :]).then_inc(taken("mT", h)[0], 1)
                dve.wait_ge(*taken("mT", h))
                v.tensor_copy(bts[:, h, 2, :], bts[:, h, 0, :]).then_inc(btmax_ready, 1)
            for h in range(2):
                dve.wait_ge(a_exp, h + 1)
                link(v.tensor_reduce(s8[:, tiles(h)], sim[:, tiles(h), :], AX_X, ALU.add))
                link(v.reciprocal(r8[:, tiles(h)], s8[:, tiles(h)]))
                for q in range(2):
                    rs = slice(q * SEQ, (q + 1) * SEQ)
                    v.tensor_tensor(ABD[rs, tiles(h), rs], sim[rs, tiles(h), :], over(r8[rs, tiles(h)], 2, [SEQ, HALF, SEQ]),
                                    ALU.mult).then_inc(a_ready, 1)
                dve.wait_ge(batt_exp, h + 1)
                link(v.tensor_reduce(bts[:, h, 1, :], bt[:, h, :, :], AX_X, ALU.add))
                link(v.reciprocal(bts[:, h, 2, :], bts[:, h, 1, :]))
                v.tensor_tensor(bt[:, h, :, :], bt[:, h, :, :], over(bts[:, h, 2, :], 2, [HALF, 2, SEQ]), ALU.mult).then_inc(bt_ready, 1)
            dve.wait_ge(mask_ready, 2)

            def keys(h, heads):
                for m in heads:
                    v.tensor_scalar(KBD[:, h * BH:(h + 1) * BH, m, :], KT[:, half(h)].rearrange("p (b j) -> p b j", b=BH),
                                    mask8[:, m:m + 1], None, ALU.mult).then_inc(kbd_dve, 1)

            for h in range(2):
                dve.wait_ge(*filled("btT", h))
                for q in range(2):
                    r = v.tensor_scalar(battm[:, tiles(h), q], PS[:, bank("btT", h), 0:HALF], bmask[:, q:q + 1], None, ALU.mult)
                r.then_inc(taken("btT", h)[0], 1)
                dve.wait_ge(*filled("hc", h))
                v.tensor_copy(hc[:, h * BH:(h + 1) * BH], PS[:, bank("hc", h), 0:BH]).then_inc(taken("hc", h)[0], 1)
                dve.wait_ge(*taken("hc", h))
                dve.wait_ge(*taken("xnT_A", h))
                v.tensor_tensor(EHC[:, half(h)].rearrange("p (b i) -> p b i", b=BH), XT[:, half(h)].rearrange("p (b i) -> p b i", b=BH),
                                over(hc[:, h * BH:(h + 1) * BH], 2, [P, BH, SEQ]), ALU.mult).then_inc(feat_ready, 1)
                dve.wait_ge(*taken("hq", h))
                v.tensor_tensor(EHT[:, half(h)], XT[:, half(h)], HT[:, half(h)], ALU.mult).then_inc(feat_ready, 1)
            dve.wait_ge(*taken("k_C", 0))
            keys(0, range(HG))
            dve.wait_ge(tg_ready, 1)
            dve.wait_ge(xb_ready, 1)
            for h in range(2):
                residual("A", h, XB, X1, TG_A)
                moments("B", h, X1)
                normalise("B", h, X1)

            for h in range(2):
                for i in range(h * HC, (h + 1) * HC):
                    dve.wait_ge(*filled("up", i))
                    dve.wait_ge(*taken("gate", i))
                    v.tensor_tensor(HB[:, i % HC, half(h)], SG[:, i % 2, :], PS[:, bank("up", i), :], ALU.mult).then_inc(taken("up", i)[0], 1)
                    dve.wait_ge(*taken("up", i))
                    v.tensor_copy(s8[:, 1:2], m8[:, 0:1]).then_inc(h_ready, 1)
                if h == 1:
                    residual("B", 0, X1, X2, TG_B)
                    moments("C", 0, X2)
                    normalise("C", 0, X2)
            residual("B", 1, X1, X2, TG_B)
            moments("C", 1, X2)
            normalise("C", 1, X2)
            dve.wait_ge(*taken("vecT"))
            v.tensor_scalar(bqs[:, :], bqk[:, 0:1], SCALE, None, ALU.mult).then_inc(bqs_ready, 1)

            def head_out(kind, t):
                dve.wait_ge(*filled(f"o_{kind}", t))
                o4 = PS[:, bank(f"o_{kind}", t), 0:H * (DH + 1)].rearrange("p (h d) -> p h d", h=H)
                if kind == "C":
                    link(v.tensor_scalar(den[:, t, :], o4[:, :, DH], 1.0, None, ALU.add))
                    link(v.reciprocal(rec[:, t, :], den[:, t, :]))
                else:
                    link(v.reciprocal(rec[:, t, :], o4[:, :, DH]))
                v.tensor_tensor(ON[:, t, :].rearrange("p (h d) -> p h d", h=H), o4[:, :, 0:DH],
                                over(rec[:, t, :], 2, [P, H, DH]), ALU.mult).then_inc(taken(f"o_{kind}", t)[0], 1)

            def keys_values(h):
                dve.wait_ge(*filled("k_D", h))
                v.tensor_scalar(KT[:, half(h)], PS[:, bank("k_D", h), :], bqk[:, 1:2], None, ALU.add).then_inc(taken("k_D", h)[0], 1)
                dve.wait_ge(*taken("k_D", h))
                v.tensor_copy(s8[:, 2:3], m8[:, 0:1]).then_inc(k_ready, 1)
                keys(h, range(KD))
                dve.wait_ge(*filled("v_D", h))
                for u in range(2):
                    rs = slice(u * SEQ, (u + 1) * SEQ)
                    bias = bv[rs, :].rearrange("p (m u d) -> p m u d", u=2, d=DH)[:, :, u, :]
                    r = v.tensor_tensor(VBD[rs, h * BH:(h + 1) * BH, :, u, 0:DH],
                                        PS[rs, bank("v_D", h), :].rearrange("p (b m d) -> p b m d", b=BH, d=DH),
                                        over(bias, 1, [SEQ, BH, HG, DH]), ALU.add)
                r.then_inc(taken("v_D", h)[0], 1)

            for n in range(CH + 3):
                if n < CH:
                    t, r = divmod(n, R)
                    dve.wait_ge(*filled("s_C", n))
                    dve.wait_ge(bias_ready, t + 1)
                    if n >= 2:
                        dve.wait_ge(sub_ready, n - 1)
                    v.tensor_tensor(SSB[:, n % 2, :, :], PS[:, bank("s_C", n), :].rearrange("p (h j) -> p h j", h=HG),
                                    BIAS[:, t, r * HG:(r + 1) * HG, :], ALU.add).then_inc(taken("s_C", n)[0], 1)
                    dve.wait_ge(*taken("s_C", n))
                    v.tensor_reduce(mx[:, n % 2, :], SSB[:, n % 2, :, :], AX_X, ALU.max).then_inc(mx_ready, 1)
                if n >= 4 and n % R == 0:
                    head_out("C", (n - 4) // R)
                if n == 13:
                    residual("C", 0, X2, X3, TG_C)
                    moments("D", 0, X3)
                if n == 15:
                    normalise("D", 0, X3)
            dve.wait_ge(rows_in, ROWS)
            keys_values(0)
            for n in range(CH + 3):
                if n < CH:
                    g = CH + n
                    dve.wait_ge(*filled("s_D", n))
                    sp3 = PS[:, bank("s_D", n), :].rearrange("p (h j) -> p h j", h=HG)
                    link(v.tensor_reduce(mx[:, n % 2, :], sp3, AX_X, ALU.max))
                    if n >= 2:
                        dve.wait_ge(*filled("t_D", n - 2))
                    v.tensor_tensor(SM[:, n % 2, :, :], sp3, over(mx[:, n % 2, :], 2, [P, HG, SEQ]),
                                    ALU.subtract).then_inc(taken("s_D", n)[0], 1)
                if n >= 4 and n % R == 0:
                    head_out("D", (n - 4) // R)
                if n == 3:
                    residual("C", 1, X2, X3, TG_C)
                    moments("D", 1, X3)
                if n == 4:
                    normalise("D", 1, X3)
                if n == 6:
                    keys_values(1)
                if n == 13:
                    dve.wait_ge(xb_ready, 2)
                    residual("D", 0, XB, X4, None)
                    moments("E", 0, X4)
                if n == 14:
                    normalise("E", 0, X4)
            def logits(h):
                dve.wait_ge(*filled("lg", h))
                L3 = PS[:, bank("lg", h), 0:HALF * (E + 2)].rearrange("p (t e) -> p t e", t=HALF)
                v.tensor_tensor(lg[:, tiles(h), E:E + 2], L3[:, :, E:E + 2], over(coefb[:, :], 1, [P, HALF, 2]), ALU.add)
                v.tensor_copy(lg[:, tiles(h), 0:E], L3[:, :, 0:E]).then_inc(taken("lg", h)[0], 1)

            logits(0)
            dve.wait_ge(xb_ready, 3)
            residual("D", 1, XB, X4, None)
            moments("E", 1, X4)
            normalise("E", 1, X4)
            for e in range(E):
                last = v.tensor_copy(b1_all[:, e, :], b1[:, e, :])
            logits(1)
            dve.wait_ge(*taken("lg", 1))
            v.tensor_reduce(gm[:, :, 0], lg[:, :, 0:E], AX_X, ALU.max)
            link(v.tensor_reduce(gm[:, :, 1], lg[:, :, E:E + 2], AX_X, ALU.max))
            v.tensor_tensor(oh[:, :, :], lg[:, :, 0:E], over(gm[:, :, 0], 2, [P, T, E]), ALU.is_equal)
            v.tensor_tensor(ge[:, :, :], lg[:, :, 0:E], over(gm[:, :, 0], 2, [P, T, E]), ALU.subtract)
            v.tensor_tensor(gm[:, :, 2:4], lg[:, :, E:E + 2], over(gm[:, :, 1], 2, [P, T, 2]), ALU.subtract).then_inc(gsum_ready, 1)
            dve.wait_ge(gsum_ready, 1)
            dve.wait_ge(mask_ready, 3)
            link(v.tensor_tensor(oh[:, :, :], oh[:, :, :], over(rev[:, :], 1, [P, T, E]), ALU.mult))
            link(v.tensor_reduce(gm[:, :, 6], oh[:, :, :], AX_X, ALU.max))
            v.tensor_tensor(oh[:, :, :], over(rev[:, :], 1, [P, T, E]), over(gm[:, :, 6], 2, [P, T, E]),
                            ALU.is_equal).then_inc(oh_ready, 1)
            dve.wait_ge(*filled("rank"))
            rk = bank("rank")
            before = PS[:, rk, 0:T * E].rearrange("p (t e) -> p e t", t=T)
            total = PS[:, rk, T * E:2 * T * E].rearrange("p (t e) -> p e t", t=T)
            A0, A1, A2, A3, A4 = (ranks[:, n, :].rearrange("p (e t) -> p e t", e=E) for n in range(5))
            link(v.tensor_copy(A4, total))
            link(v.tensor_tensor_scan(ranks[:, 0, :], seg[:, :, :].rearrange("p e t -> p (e t)"), ranks[:, 4, :], 0.0, ALU.mult, ALU.add))
            link(v.tensor_tensor(A1, over(A0[:, :, T - 1], 2, [P, E, T]), nth[:, :, :], ALU.is_gt))
            link(v.tensor_reduce(cnt[:, 0, :], A1, AX_X, ALU.add))
            link(v.tensor_tensor_scan(cnt[:, 1, :], ones[:, 0:E], cnt[:, 0, :], 0.0, ALU.mult, ALU.add))
            link(v.tensor_tensor(cnt[:, 2, :], cnt[:, 1, :], cnt[:, 0, :], ALU.subtract))
            link(v.scalar_tensor_tensor(A2, over(cnt[:, 2, :], 2, [P, E, T]), float(P), A0, ALU.mult, ALU.add))
            link(v.tensor_tensor(A2, A2, A4, ALU.subtract))
            v.tensor_tensor(A2, A2, before, ALU.add).then_inc(taken("rank")[0], 1)
            dve.wait_ge(*taken("rank"))
            link(v.tensor_tensor(A2, A2, oh[:, :, :].rearrange("p t e -> p e t"), ALU.mult))
            link(v.tensor_reduce(cnt[:, 3, :], A2.rearrange("p e t -> p t e"), AX_X, ALU.add))
            v.tensor_copy(slot[:, :], cnt[:, 3, :]).then_inc(slot_ready, 1)
            link(v.tensor_tensor(own[:, :, :], over(cnt[0:1, 1, :], 1, [1, BLOCKS, E]), blk[:, :, :], ALU.is_le))
            link(v.tensor_reduce(bexp[:, :], own[:, :, :], AX_X, ALU.add))
            link(v.tensor_scalar(bexpi[:, :], bexp[:, :], float(E - 1), None, ALU.min))
            dve.wait_ge(gexp_ready, 1)
            v.tensor_reduce(gm[:, :, 4], ge[:, :, :], AX_X, ALU.add)
            link(v.tensor_reduce(gm[:, :, 5], gm[:, :, 2:4], AX_X, ALU.add))
            link(v.reciprocal(gm[:, :, 4:6], gm[:, :, 4:6]))
            link(v.tensor_scalar(gm[:, :, 5], gm[:, :, 5], TG_D, None, ALU.mult))
            link(v.tensor_tensor(gm[:, :, 2:4], gm[:, :, 2:4], over(gm[:, :, 5], 2, [P, T, 2]), ALU.mult))
            v.tensor_tensor(BASE[:, :, D + 1], gm[:, :, 4], gm[:, :, 2], ALU.mult)
            for h in range(2):
                last = v.scalar_tensor_tensor(X3[:, tiles(h), :], X4[:, tiles(h), :], TG_D, X3[:, tiles(h), :], ALU.mult, ALU.add)
            link(last)
            chosen = [v.value_load(bexpi[0:1, k:k + 1], min_val=0, max_val=E - 1) for k in range(BLOCKS)]

            def weights(k):
                if k == 0:
                    dve.wait_ge(moe_in, MOE)
                if k >= WB:
                    dve.wait_ge(*filled("ey", k - WB))
                v.tensor_copy(WBUF[:, k % WB, :], experts[:, bass.ds(chosen[k], 1), :]).then_inc(w_copied, 1)

            def inputs(k):
                dve.wait_ge(*filled("xsT", k))
                if k >= 2:
                    dve.wait_ge(*filled("eh", k - 2))
                v.tensor_scalar(XST[:, k % 2, :], PS[:, bank("xsT", k), 0:P], ln2[:, 0:1], ln2[:, 1:2], ALU.mult, ALU.add)\
                    .then_inc(taken("xsT", k)[0], 1)

            def results(k):
                dve.wait_ge(*filled("ey", k))
                if k == 0:
                    dve.wait_ge(bs_in, 16)
                v.tensor_tensor(YB[:, k % 2, :], PS[:, bank("ey", k), 0:P], WBUF[:, k % WB, 2 * F + FC:EW], ALU.add)\
                    .then_inc(taken("ey", k)[0], 1)
                dve.wait_ge(*taken("ey", k))
                if k >= 4:
                    dve.wait_ge(out_done[k % 4], 16 * (k // 4))
                v.scalar_tensor_tensor(OUTB[:, k % 4, :], YB[:, k % 2, :], BS[:, k, D + 1:D + 2], BS[:, k, 0:D],
                                       ALU.mult, ALU.add).then_inc(ey_ready, 1)

            for h in range(2):
                dve.wait_ge(*filled("ry", h))
                v.tensor_tensor(XB[:, tiles(h), :], by_tile(bank("ry", h)), over(rb2[:, :], 1, [P, HALF, D]),
                                ALU.add).then_inc(taken("ry", h)[0], 1)
                dve.wait_ge(*taken("ry", h))
                for t in range(h * HALF, (h + 1) * HALF):
                    v.scalar_tensor_tensor(BASE[:, t, 0:D], XB[:, t, :], gm[:, t, 3:4], X3[:, t, :], ALU.mult, ALU.add)\
                        .then_inc(base_ready, 1)
            for k in range(WB):
                weights(k)
            inputs(0)
            for k in range(BLOCKS):
                if k + 1 < BLOCKS:
                    inputs(k + 1)
                if k >= 1:
                    results(k - 1)
                    if k - 1 + WB < BLOCKS:
                        weights(k - 1 + WB)
            results(BLOCKS - 1)

        @block.tensor
        def _(pe):
            mm, tr = nc.tensor.matmul, nc.tensor.transpose

            def keep_warm(name, i, n):
                b = empty(pe, name, i)
                for _ in range(n):
                    mm(PS[:, b, :], warm[:, 0:P], warm[:, :], start=True, stop=True)

            def turn_tiles(name, h, src):
                b = empty(pe, name, h)
                for t in range(h * HALF, (h + 1) * HALF):
                    r = tr(PS[:, b, tile_cols(t)], src[:, t, :], ident[:, :])
                r.then_inc(filled(name, h)[0], 1)

            def norm_transpose(stage, h):
                pe.wait_ge(xn_ready, 2 * STAGES.index(stage) + h + 1)
                turn_tiles(f"xnT_{stage}", h, XN)

            pe.wait_ge(warm_ready, 1)
            keep_warm("sim", 0, 12)
            pe.wait_ge(ident_ready, 1)
            pe.wait_ge(wsim_in, 16)
            b = empty(pe, "early")
            tr(PS[:, b, 0:3], srows[:, :], ident[0:3, 0:3])
            pe.wait_ge(qrow_ready, 1)
            tr(PS[:, b, 3:3 + T], qrowf[:, :], ident[0:T, 0:T]).then_inc(filled("early")[0], 1)
            pe.wait_ge(ctx_in, 16)
            for h in range(2):
                turn_tiles("ctxT", h, C)
            for h in range(2):
                norm_transpose("A", h)
            pe.wait_ge(w2b_ready, 2)
            for h in range(2):
                pe.wait_ge(c3_ready, h + 1)
                pe.wait_ge(*taken("xnT_A", h))
                b = empty(pe, "sim", h)
                for i in range(h * BH, (h + 1) * BH):
                    t, q = divmod(i, 2)
                    bs = slice(i * SEQ, (i + 1) * SEQ)
                    o = PS[q * SEQ:(q + 1) * SEQ, b, (t % HALF) * SEQ:(t % HALF + 1) * SEQ]
                    mm(o, XT[:, bs], C3T[:, bs], start=True, stop=False)
                    r = mm(o, w2b[:, :], CT[:, bs], start=False, stop=True)
                r.then_inc(filled("sim", h)[0], 1)
            pe.wait_ge(xw_in, 64)
            b = empty(pe, "xwT")
            for n in range(4):
                r = tr(PS[:, b, n * P:(n + 1) * P], xw[:, n, :], ident[:, :])
            r.then_inc(filled("xwT")[0], 1)
            pe.wait_ge(fw_ready, 1)
            for n in range(3 * HC):
                if n % 4 == 0:
                    b = empty(pe, "fwT", n // 4)
                r = tr(PS[:, b, (n % 4) * P:(n % 4 + 1) * P], wff[:, n, :], ident[:, :])
                if n % 4 == 3 or n == 3 * HC - 1:
                    r.then_inc(filled("fwT", n // 4)[0], 1)
            for h in range(2):
                pe.wait_ge(mf_ready, h + 1)
                tr(PS[0:HALF, empty(pe, "mT", h), 0:P], mf8[:, tiles(h)], ident[:, :]).then_inc(filled("mT", h)[0], 1)
            pe.wait_ge(*taken("xwT"))
            for h in range(2):
                mm(PS[:, empty(pe, "k_C", h), :], xwT[:, 1, :], CT[:, half(h)], start=True, stop=True).then_inc(filled("k_C", h)[0], 1)
                pe.wait_ge(a_ready, 2 * (h + 1))
                turn_tiles("aT", h, ABD)
            for h in range(2):
                pe.wait_ge(bt_ready, h + 1)
                tr(PS[:, empty(pe, "btT", h), 0:HALF], bt[:, h, :, :].rearrange("p q i -> p (q i)"), ident[0:HALF, 0:HALF])\
                    .then_inc(filled("btT", h)[0], 1)
                pe.wait_ge(*taken("aT", h))
                b = empty(pe, "hq", h)
                for t in range(h * HALF, (h + 1) * HALF):
                    r = mm(PS[:, b, tile_cols(t)], C[:, t, :], AT[:, t, :], start=True, stop=True)
                r.then_inc(filled("hq", h)[0], 1)
                pe.wait_ge(*taken("btT", h))
                b = empty(pe, "hc", h)
                for t in range(h * HALF, (h + 1) * HALF):
                    at = 2 * (t % HALF)
                    r = mm(PS[:, b, at:at + 2], XN[:, t, :], battm[:, t, :], start=True, stop=True)
                r.then_inc(filled("hc", h)[0], 1)

            def values(name, h, xT, w):
                b = empty(pe, name, h)
                for i in range(h * BH, (h + 1) * BH):
                    at = (i % BH) * SEQ
                    for u in range(2):
                        r = mm(PS[u * SEQ:(u + 1) * SEQ, b, at:at + SEQ], xT[:, i * SEQ:(i + 1) * SEQ],
                               w.rearrange("p (m u d) -> p m u d", u=2, d=DH)[:, :, u, :], start=True, stop=True)
                r.then_inc(filled(name, h)[0], 1)

            def project(name, h, lhs_of, ws):
                b = empty(pe, name, h)
                for t in range(h * HALF, (h + 1) * HALF):
                    for c, w in enumerate(ws):
                        r = mm(PS[:, b, tile_cols(t)], lhs_of(t, c), w, start=(c == 0), stop=(c == len(ws) - 1))
                r.then_inc(filled(name, h)[0], 1)

            for h in range(2):
                values("v_C", h, CT, xwT[:, 2, :])
            feats = [XT, HT, EHT, EHC]
            pe.wait_ge(wqv_in, 16)
            for h in range(2):
                pe.wait_ge(feat_ready, 2 * (h + 1))
                project("y_A", h, lambda t, c: feats[c][:, t * P:(t + 1) * P], [wqv[:, c, :] for c in range(4)])
                if h == 0:
                    pe.wait_ge(vec_in, VECS)
                    tr(PS[:, empty(pe, "vecT"), 0:NVEC], vrows[:, :], ident[0:NVEC, 0:NVEC]).then_inc(filled("vecT")[0], 1)

            for n in range(3):
                pe.wait_ge(*taken("fwT", n))
            for h in range(2):
                norm_transpose("B", h)
                if h == 1:
                    pe.wait_ge(h_ready, HC)
                    project("y_B", 0, lambda t, c: HB[:, c, t * P:(t + 1) * P], [wfT[:, 2 * HC + c, :] for c in range(HC)])
                pe.wait_ge(*taken("xnT_B", h))
                for i in range(h * HC, (h + 1) * HC):
                    c = i % HC
                    mm(PS[:, empty(pe, "gate", i), :], wfT[:, c, :], XT[:, half(h)], start=True, stop=True).then_inc(filled("gate", i)[0], 1)
                    mm(PS[:, empty(pe, "up", i), :], wfT[:, HC + c, :], XT[:, half(h)], start=True, stop=True).then_inc(filled("up", i)[0], 1)
            pe.wait_ge(h_ready, 2 * HC)
            project("y_B", 1, lambda t, c: HB[:, c, t * P:(t + 1) * P], [wfT[:, 2 * HC + c, :] for c in range(HC)])

            def queries(kind, h, w):
                pe.wait_ge(*taken(f"xnT_{kind}", h))
                mm(PS[:, empty(pe, f"q_{kind}", h), :], w, XT[:, half(h)], start=True, stop=True).then_inc(filled(f"q_{kind}", h)[0], 1)

            def queries_keys_values(h):
                queries("D", h, wqkv[:, 0:D])
                mm(PS[:, empty(pe, "k_D", h), :], wqkv[:, D:2 * D], XT[:, half(h)], start=True, stop=True).then_inc(filled("k_D", h)[0], 1)
                values("v_D", h, XT, wqkv[:, 2 * D:3 * D])

            def scores(k, n):
                kind = "CD"[k]
                t, r = divmod(n, R)
                if n % (CH // 2) == 0:
                    h = n // (CH // 2)
                    pe.wait_ge(*taken(f"q_{kind}", h))
                    pe.wait_ge(kbd_dve, HG if k == 0 else HG + KD * (h + 1))
                    if k == 1 or h == 1:
                        pe.wait_ge(kbd_act, HG if k == 0 else HG + (HG - KD) * (h + 1))
                b = empty(pe, f"s_{kind}", n)
                rs = slice(r * SEQ, (r + 1) * SEQ)
                for q in range(2):
                    i = 2 * t + q
                    x = mm(PS[q * SEQ:(q + 1) * SEQ, b, :], QT[rs, i * SEQ:(i + 1) * SEQ],
                           KBD[rs, i, :, :].rearrange("p h j -> p (h j)"), start=True, stop=True)
                x.then_inc(filled(f"s_{kind}", n)[0], 1)

            def turn(k, n):
                kind = "CD"[k]
                pe.wait_ge(*((sub_ready, n + 1) if k == 0 else taken("s_D", n)))
                b = empty(pe, f"t_{kind}", n)
                for m in range(HG // 2):
                    x = tr(PS[:, b, m * P:(m + 1) * P], SM[:, n % 2, 2 * m:2 * m + 2, :].rearrange("p h j -> p (h j)"), ident[:, :])
                x.then_inc(filled(f"t_{kind}", n)[0], 1)

            def weigh(k, n):
                kind = "CD"[k]
                t, r = divmod(n, R)
                pe.wait_ge(*taken(f"t_{kind}", n))
                if n % (CH // 2) == 0:
                    pe.wait_ge(*taken(f"v_{kind}", n // (CH // 2)))
                if r == 0:
                    b = empty(pe, f"o_{kind}", t)
                b = bank(f"o_{kind}", t)
                for m in range(HG // 2):
                    hp = r * (HG // 2) + m
                    for q in range(2):
                        at = hp * 2 * (DH + 1)
                        x = mm(PS[q * SEQ:(q + 1) * SEQ, b, at:at + 2 * (DH + 1)], PT[:, n % 2, m, q * SEQ:(q + 1) * SEQ],
                               VBD[:, 2 * t + q, hp, :, :].rearrange("p u d -> p (u d)"), start=True, stop=True)
                if r == 0:
                    x.then_inc(pv_first, 1)
                else:
                    x.then_inc(filled(f"o_{kind}", t)[0], 1)

            def output(kind, h, w):
                pe.wait_ge(*taken(f"onT_{kind}", h))
                project(f"y_{kind}", h, lambda t, c: XT[:, t * P:(t + 1) * P], [w])

            def heads_transpose(kind, h):
                for t in range(h * HALF, (h + 1) * HALF)[-2:]:
                    pe.wait_ge(*taken(f"o_{kind}", t))
                turn_tiles(f"onT_{kind}", h, ON)

            def gate_logits(h):
                pe.wait_ge(*taken("xnT_E", h))
                b = empty(pe, "lg", h)
                for t in range(h * HALF, (h + 1) * HALF):
                    at = (t % HALF) * (E + 2)
                    r = mm(PS[:, b, at:at + E + 2], XT[:, t * P:(t + 1) * P], wgc[:, :], start=True, stop=True)
                r.then_inc(filled("lg", h)[0], 1)

            def dense(i):
                h, c = divmod(i, FC)
                mm(PS[:, empty(pe, "dense", i), :], rw1[:, c * P:(c + 1) * P], XT[:, half(h)],
                   start=True, stop=True).then_inc(filled("dense", i)[0], 1)

            for h in range(2):
                norm_transpose("C", h)
                queries("C", h, xwT[:, 0, :])
            pe.wait_ge(w_in, WEIGHTS)
            for k in range(2):
                for n in range(CH + 2):
                    if n < CH:
                        scores(k, n)
                    if 1 <= n <= CH:
                        turn(k, n - 1)
                    if n >= 2:
                        weigh(k, n - 2)
                    if k == 0:
                        if n == 11:
                            heads_transpose("C", 0)
                        if n == 12:
                            output("C", 0, xwT[:, 3, :])
                        if n == 15:
                            norm_transpose("D", 0)
                        if n == 17:
                            queries_keys_values(0)
                    else:
                        if n == 1:
                            heads_transpose("C", 1)
                        if n == 2:
                            output("C", 1, xwT[:, 3, :])
                        if n == 5:
                            norm_transpose("D", 1)
                        if n == 6:
                            queries_keys_values(1)
                        if n == 11:
                            heads_transpose("D", 0)
                        if n == 12:
                            output("D", 0, wo[:, :])
                        if n == 15:
                            norm_transpose("E", 0)
                        if n == 16:
                            gate_logits(0)

            heads_transpose("D", 1)
            pe.wait_ge(rmlp_in, 32)
            dense(0)
            output("D", 1, wo[:, :])
            for i in range(1, FC):
                dense(i)
            norm_transpose("E", 1)
            gate_logits(1)
            for i in range(FC, 2 * FC):
                if i == FC + 2:
                    pe.wait_ge(oh_ready, 1)
                    b = empty(pe, "rank")
                    flat = oh[:, :, :].rearrange("p t e -> p (t e)")
                    mm(PS[:, b, 0:T * E], tri[:, :], flat, start=True, stop=True)
                    mm(PS[:, b, T * E:2 * T * E], ones[:, :], flat, start=True, stop=True).then_inc(filled("rank")[0], 1)
                dense(i)
            for h in range(2):
                for i in range(h * FC, (h + 1) * FC):
                    pe.wait_ge(*taken("dense", i))
                project("ry", h, lambda t, c: HR[:, c, t * P:(t + 1) * P], [rw2[:, c, :] for c in range(FC)])

            def turn_slots(k):
                for n, (k0, _) in enumerate(XS_PARTS):
                    if k == k0:
                        pe.wait_ge(xs_in[n], 16)
                b = empty(pe, "xsT", k)
                tr(PS[:, b, 0:P], XS[:, k, :], ident[:, :]).then_inc(filled("xsT", k)[0], 1)

            def hidden(k):
                pe.wait_ge(*taken("xsT", k))
                pe.wait_ge(w_copied, k + 1)
                b = empty(pe, "eh", k)
                for c in range(FC):
                    r = mm(PS[:, b, c * P:(c + 1) * P], WBUF[:, k % WB, c * P:(c + 1) * P], XST[:, k % 2, :], start=True, stop=True)
                r.then_inc(filled("eh", k)[0], 1)

            def down(k):
                pe.wait_ge(*taken("eh", k))
                b = empty(pe, "ey", k)
                for c in range(FC):
                    r = mm(PS[:, b, 0:P], HB2[:, k % 2, c, :], WBUF[:, k % WB, F + c * D:F + (c + 1) * D],
                           start=(c == 0), stop=(c == FC - 1))
                r.then_inc(filled("ey", k)[0], 1)

            turn_slots(0)
            for k in range(BLOCKS + 1):
                if k + 1 < BLOCKS:
                    turn_slots(k + 1)
                if k < BLOCKS:
                    hidden(k)
                if k >= 1:
                    down(k - 1)


def kernel(**inputs):
    import numpy as _np
    import concourse.bacc as _bacc
    from concourse import mybir as _mybir
    from concourse.bass_utils import run_bass_kernel_spmd as _run

    nc = _bacc.Bacc("TRN2", target_bir_lowering=False, num_devices=1)
    arrays, args = {}, {}
    for name, value in inputs.items():
        v = _np.ascontiguousarray(value)
        arrays[f"in_{name}"] = v
        args[name] = nc.dram_tensor(f"in_{name}", v.shape, _mybir.dt.from_np(v.dtype), kind="ExternalInput").ap()
    out = nc.dram_tensor("out_0", inputs["x"].shape, _mybir.dt.float32, kind="ExternalOutput").ap()
    flamingo_layers(nc, args, out)
    r = _run(nc, [arrays], core_ids=[0])
    return r.results[0]["out_0"]
```

```python
from contextlib import ExitStack

import numpy as np
import concourse.bass as bass
from concourse import mybir

F32 = mybir.dt.float32
I32 = mybir.dt.int32
BF16 = mybir.dt.bfloat16
ALU = mybir.AluOpType
ACT = mybir.ActivationFunctionType
AX_X = mybir.AxisListType.X

P = 128
BANK = 512
EPS = 1e-5


def flamingo_layers(nc: bass.Bass, a, out: bass.AP):
    B, SEQ, D = out.shape
    N = B * SEQ
    T = N // P
    HALF = T // 2
    BH = B // 2
    H = 16
    DH = D // H
    R = 2
    HG = H // R
    CH = T * R
    HC = a["ffn_w"].shape[1] // 3
    E = a["b2"].shape[0]
    FC = a["experts"].shape[2] // (2 * D + 1)
    F = FC * P
    BLOCKS = T + E - 1
    SLOTS = BLOCKS * P
    ROW = 2 * D + 4
    NOWHERE = 4 * N
    WB = 3
    SCALE = 1.0 / float(np.sqrt(DH))
    slopes = [(2.0 ** (-8.0 / H)) ** i for i in range(1, H + 1)]
    assert D == P and E == T and 2 * BANK == N

    ctx = ExitStack()
    with ctx:
        def sb(name, shape, dt=F32):
            return ctx.enter_context(nc.sbuf_tensor(name, shape, dt))

        def sem(name):
            return ctx.enter_context(nc.semaphore(name))

        X0 = sb("x_in", [P, T, D])
        X1 = sb("x_after_l0_xattn", [P, T, D])
        X2, X3 = X0, X1
        XN = sb("xn", [P, T, D])
        XB = sb("x_plus_bias", [P, T, D])
        XT = sb("xT", [P, N])
        C = sb("ctx_tokens", [P, T, D])
        U = C
        ABD = sb("attn_block_diagonal", [P, T, P])
        X4 = ABD
        CT = sb("ctxT", [P, N])
        C3T = sb("ctxT_w3_w1", [P, N])
        FEATS = sb("features_then_hidden", [P, 4, N])
        HT, EHT, EHC, HB = FEATS[:, 0, :], FEATS[:, 1, :], FEATS[:, 2, :], FEATS
        HR = FEATS
        KT = sb("kT", [P, N])
        QT = sb("qT", [P, N])
        KBD = sb("k_block_diagonal", [P, B, HG, SEQ])
        FILL = (2, 1)
        GAP = {16: 2, 17: 2, 18: 3}
        WARM = {("xnT_E", 0): 4, ("onT_D", 1): 6, ("xnT_B", 0): 10, ("xnT_C", 0): 8, ("aT", 0): 8, ("xnT_C", 1): 16, ("xnT_D", 0): 8, ("xnT_D", 1): 8}
        EW = 2 * F + FC + D
        LATE = sb("position_bias_then_experts", [P, max(T * H * SEQ, E * EW)])
        BIAS = LATE[:, 0:T * H * SEQ].rearrange("p (t h j) -> p t h j", t=T, h=H)
        VBD = sb("v_block_diagonal", [P, B, HG, 2, DH + 1])
        SSB = sb("scores_sb", [P, 2, HG, SEQ])
        SM = sb("scores_less_max", [P, 2, HG, SEQ])
        PT = sb("probsT", [P, 2, HG // 2, P])
        ON = sb("attention_out", [P, T, D])
        ident = sb("ident", [P, P])
        warm = sb("warm", [P, BANK], BF16)
        mask8 = sb("head_mask", [P, HG])
        slope = sb("slope", [P, H])
        bmask = sb("batch_row_mask", [P, 2])
        neg_half = sb("neg_half", [P, T])
        unused = sb("unused", [P, 1])
        w2b = sb("w2_over_rows", [P, SEQ])
        tg = sb("tanh_gates", [P, 4])
        TG_A, TG_C, TG_B, TG_D = (tg[:, i:i + 1] for i in range(4))
        bqvg = sb("b_qv_gated", [P, D])
        weights_a = sb("weights_a", [P, 8, D])
        xwT, wqv = weights_a[:, 0:4, :], weights_a[:, 4:8, :]
        wf2 = sb("ffn_w_then_rows", [P, 6 * HC, D])
        wff = wf2[:, 0:3 * HC, :]
        wfi = wff.bitcast(I32)
        wfT = wf2[:, 3 * HC:6 * HC, :]
        BASE = wf2[:, :, :].rearrange("p c d -> p (c d)")[:, 0:T * ROW].rearrange("p (t r) -> p t r", t=T)
        SG = sb("silu_gate", [P, 2, BANK])
        kpos = sb("key_pos_rows", [P, T, SEQ], I32)
        pos_mask = sb("query_pos_mask", [P, T * (1 + SEQ)], I32)
        msk = pos_mask[:, T:].rearrange("p (t j) -> p t j", t=T)
        mneg = msk.bitcast(F32)
        ndist = sb("minus_dist", [P, T, SEQ])
        sim = sb("sim_less_max", [P, T, SEQ])
        AT = sb("attnT", [P, T, P])
        stats = sb("bn_stats", [P, T, 6])
        mv = sb("mean_var", [P, T, 2])
        ve = sb("var_plus_eps", [P, T])
        ve2 = sb("var_plus_eps_inner", [P, T])
        rstd = sb("rstd", [P, T])
        rstd1 = sb("rstd_outer", [P, T])
        m8 = sb("row_max", [P, T])
        mf8 = sb("row_max_sim", [P, T])
        s8 = sb("row_sum", [P, T])
        r8 = sb("row_recip", [P, T])
        bt = sb("batt_rows", [HALF, 2, 2, SEQ])
        bts = sb("batt_stats", [HALF, 2, 3, 2])
        battm = sb("batt_masked", [P, T, 2])
        hc = sb("hc_barT", [P, B])
        mx = sb("head_max", [P, 2, HG])
        den = sb("head_den", [P, T, H])
        rec = sb("head_recip", [P, T, H])
        weights_b = sb("weights_b", [P, 4 * D + 2 * F])
        wqkv, wo, rw1 = weights_b[:, 0:3 * D], weights_b[:, 3 * D:4 * D], weights_b[:, 4 * D:4 * D + F]
        rw2 = weights_b[:, 4 * D + F:].rearrange("p (c d) -> p c d", c=FC)
        bqs = sb("b_q_scaled", [P, 1])
        vrows = sb("vector_rows", [P, 4 * D + 7])
        bqv, bv, bo, rb2 = (vrows[:, n * D:(n + 1) * D] for n in range(4))
        coefb, gates, bsim = vrows[:, 4 * D:4 * D + 2], vrows[:, 4 * D + 2:4 * D + 6], vrows[:, 4 * D + 6:4 * D + 7]
        vec = sb("vector_cols", [P, 10 + FC + E + 2])
        wsim, bqk, ln1, ln2 = vec[:, 0:3], vec[:, 3:5], vec[:, 6:8], vec[:, 8:10]
        rb1, wgc = vec[:, 10:10 + FC], vec[:, 10 + FC:]
        lg = sb("coefficient_logits", [P, T, 2])
        gm = sb("gate_small", [P, T, 8])
        ge = sb("gate_exp", [P, T, E])
        oh_by_e = sb("one_hot", [P, E, T])
        oh = oh_by_e[:, :, :].rearrange("p e t -> p t e")
        rev = sb("expert_rank", [P, E])
        tri = sb("not_before", [P, P])
        ones = sb("ones", [P, P])
        ranks = sb("ranks", [P, 4, T * E])
        seg = sb("scan_restarts", [P, E, T])
        nth = sb("multiples", [P, E, T])
        blk = sb("block_numbers", [1, BLOCKS, E])
        cnt = sb("block_counts", [P, 3, E + 1])
        own = sb("block_of_expert", [1, BLOCKS, E])
        bexp = sb("block_expert", [1, BLOCKS])
        bexpi = sb("block_expert_int", [1, BLOCKS], I32)
        slot = sb("slot", [P, T], I32)
        fill = sb("empty_row", [P, ROW])
        HB2 = SSB[:, :, :, :].rearrange("p u h j -> p (u h j)").rearrange("p (u c n) -> p u c n", u=2, c=FC)
        sm_flat = SM[:, :, :, :].rearrange("p u h j -> p (u h j)").rearrange("p (u d) -> p u d", d=D)
        XST, YB, OUTB = sm_flat[:, 0:2, :], sm_flat[:, 2:4, :], sm_flat[:, 4:8, :]
        qpos = sb("query_pos_cols", [P, T])
        experts = LATE[:, 0:E * EW].rearrange("p (e w) -> p e w", e=E)
        spare = KBD[:, :, :, :].rearrange("p b h j -> p (b h j)")
        WBUF = spare[:, 0:WB * EW].rearrange("p (k w) -> p k w", k=WB)
        XS = spare[:, WB * EW:WB * EW + BLOCKS * ROW].rearrange("p (k r) -> p k r", k=BLOCKS)
        assert WB * EW + BLOCKS * ROW <= B * HG * SEQ

        xs_dram = nc.dram_tensor("rows_by_slot", (SLOTS, ROW), F32).ap()
        PS = ctx.enter_context(nc.psum_tensor("ps", [P, 8, BANK], F32))

        USES = [("xnT_A", 0, 2), ("xnT_A", 1, 3), ("k_C", 0, 0), ("sim", 0, 4), ("sim", 1, 5), ("k_C", 1, 1), ("v_C", 0, 6),
                ("mT", 0, 2), ("mT", 1, 3), ("v_C", 1, 7), ("aT", 0, 4), ("aT", 1, 5), ("btT", 0, 0), ("hq", 0, 6), ("hc", 0, 2),
                ("btT", 1, 1), ("hq", 1, 7), ("hc", 1, 3), ("y_A", 0, 4), ("y_A", 1, 5), ("xnT_B", 0, 6)]
        USES += [u for i in range(HC) for u in (("gate", i, i % 2), ("up", i, 2 + i % 2))] + [("xnT_B", 1, 7), ("y_B", 0, 4)]
        USES += [u for i in range(HC, 2 * HC) for u in (("gate", i, i % 2), ("up", i, 2 + i % 2))] + [("xnT_C", 0, 6), ("q_C", 0, 6), ("y_B", 1, 5)]
        BESIDE = {("C", 1, 1): [("xnT_C", 1, 7)], ("C", 2, 1): [("q_C", 1, 7)], ("C", 12, 0): [("onT_C", 0, 6)],
                  ("C", 12, 1): [("y_C", 0, 7)], ("C", 15, 0): [("xnT_D", 0, 6)], ("C", 15, 1): [("q_D", 0, 7), ("k_D", 0, 6)],
                  ("C", 16, 1): [("v_D", 0, 7)],
                  ("D", 0, 0): [("onT_C", 1, 6)], ("D", 1, 0): [("y_C", 1, 7)], ("D", 3, 0): [("xnT_D", 1, 6)],
                  ("D", 3, 1): [("q_D", 1, 7), ("k_D", 1, 6)], ("D", 4, 0): [("v_D", 1, 7)], ("D", 12, 0): [("onT_D", 0, 6)],
                  ("D", 12, 1): [("y_D", 0, 7)], ("D", 17, 1): [("xnT_E", 0, 6)], ("D", 18, 1): [("lg", 0, 7)]}
        for kind in "CD":
            for n in range(CH + 3):
                if n < CH:
                    USES.append((f"s_{kind}", n, 4 + n % 2))
                USES += BESIDE.get((kind, n, 0), [])
                if 2 <= n < CH + 2:
                    USES.append((f"t_{kind}", n - 2, n % 2))
                if n >= 3 and (n - 3) % R == 0:
                    USES.append((f"o_{kind}", (n - 3) // R, 2 + (n - 3) // R % 2))
                USES += BESIDE.get((kind, n, 1), [])
        HBANKS = (0, 1, 4, 5)
        DENSE = [("dense", i, HBANKS[i % 4]) for i in range(2 * FC)]
        USES += [DENSE[0], ("onT_D", 1, 6), DENSE[1], ("y_D", 1, 7)] + DENSE[2:FC] + [("ry", 0, 2), ("xnT_E", 1, 6), ("lg", 1, 7)]
        USES += [("rank", 0, 6)] + DENSE[FC:] + [("ry", 1, 3), ("ry", 2, 2), ("xsT", 0, 6)]
        for k in range(BLOCKS + 1):
            if k + 1 < BLOCKS:
                USES.append(("xsT", k + 1, 6 + (k + 1) % 2))
            if k < BLOCKS:
                USES.append(("eh", k, k % 2))
            if k >= 1:
                USES.append(("ey", k - 1, 4 + (k - 1) % 2))
        use = {}
        for name, i, b in USES:
            use[name, i] = (b, sum(1 for x, _ in use.values() if x == b))

        bank_full = [sem(f"bank{b}_full") for b in range(8)]
        bank_taken = [sem(f"bank{b}_taken") for b in range(8)]

        def bank(name, i=0):
            return use[name, i][0]

        def filled(name, i=0):
            b, n = use[name, i]
            return bank_full[b], n + 1

        def taken(name, i=0):
            b, n = use[name, i]
            return bank_taken[b], n + 1

        def empty(pe, name, i=0):
            b, n = use[name, i]
            if n:
                pe.wait_ge(bank_taken[b], n)
            return b

        (vec_in, rows_in, pos_in, fw_in, wa_in, wb_in, moe_in, prefilled, scattered) = (
            sem(n) for n in "vec_in rows_in pos_in fw_in wa_in wb_in moe_in prefilled scattered".split())
        ctxT_in, ctx_in = [sem("ctxT0_in"), sem("ctxT1_in")], sem("ctx_in")
        x_in = [sem("x0_in"), sem("x1_in")]
        xs_in = [sem(f"xs_in{n}") for n in range(4)]
        out_done = [sem(f"out_done{n}") for n in range(4)]
        ident_ready, mask_ready, rstd_ready, xb_ready, bias_ready, fill_ready, sub_ready, warm_ready, carried = (
            sem(n) for n in "ident_ready mask_ready rstd_ready xb_ready bias_ready fill_ready sub_ready warm_ready carried".split())
        pv_first = sem("pv_first")
        tg_ready, fw_ready, a_exp, batt_exp, kbd_act, gexp_ready = (
            sem(n) for n in "tg_ready fw_ready a_exp batt_exp kbd_act gexp_ready".split())
        (var_ready, var1_ready, xn_ready, w2b_ready, c3_ready, mf_ready, sim_ready, a_ready, btmax_ready, bt_ready,
         feat_ready, h_ready, mx_ready, kbd_dve, gsum_ready, oh_ready, slot_ready, base_ready,
         x4_ready, w_copied, ey_ready, bqs_ready) = (
            sem(n) for n in ("var_ready var1_ready xn_ready w2b_ready c3_ready mf_ready sim_ready a_ready btmax_ready bt_ready "
                             "feat_ready h_ready mx_ready kbd_dve gsum_ready oh_ready "
                             "slot_ready base_ready x4_ready w_copied ey_ready bqs_ready").split())
        dve_step, pool_step = sem("dve_step"), sem("pool_step")
        block = ctx.enter_context(nc.Block())

        def rows(ap, n=P):
            return ap.unsqueeze(0).broadcast_to([n, ap.shape[0]])

        def over(ap, axis, shape):
            return ap.unsqueeze(axis).broadcast_to(shape)

        def tiles(h):
            return slice(h * HALF, (h + 1) * HALF)

        def half(h):
            return slice(h * BANK, (h + 1) * BANK)

        def tile_cols(t):
            return slice((t % HALF) * P, (t % HALF + 1) * P)

        def by_tile(b):
            return PS[:, b, :].rearrange("p (t d) -> p t d", t=HALF)

        POS = 16 * 3
        MOE = 16 * 2
        XS_PARTS = ((0, 1), (1, 3), (3, 8), (8, BLOCKS))
        KD = 5
        STAGES = "ABCDE"

        @block.sync
        def _(sp):
            for h in range(2):
                sp.dma_start(X0[:, tiles(h), :], a["x"][:, tiles(h), :]).then_inc(x_in[h], 16)
            sp.dma_start(vrows[:, :], rows(a["vector_rows"])).then_inc(rows_in, 16)
            sp.dma_start(C[:, :, :], a["ctx"]).then_inc(ctx_in, 16)
            sp.dma_start(weights_a[:, :, :], a["weights_a"]).then_inc(wa_in, 16)
            sp.dma_start(pos_mask[:, :], a["query_pos_mask"]).then_inc(pos_in, 16)
            for q in range(2):
                sp.dma_start(kpos[q * SEQ:(q + 1) * SEQ, :, :], over(a["key_pos"][q], 0, [SEQ, T, SEQ])).then_inc(pos_in, 16)
            sp.dma_start(wfi, a["ffn_w"]).then_inc(fw_in, 16)
            sp.dma_start(weights_b[:, :], a["weights_b"]).then_inc(wb_in, 16)
            sp.wait_ge(fill_ready, 1)
            sp.dma_start(xs_dram.rearrange("(k p) r -> p k r", p=P), over(fill[:, :], 1, [P, BLOCKS, ROW])).then_inc(prefilled, 16)
            sp.wait_ge(*taken("s_C", CH - 2))
            sp.wait_ge(*taken("s_C", CH - 1))
            sp.dma_start(experts[:, :, 0:2 * F + FC], a["experts"]).then_inc(moe_in, 16)
            sp.dma_start(experts[:, :, 2 * F + FC:EW], over(a["b2"], 0, [P, E, D])).then_inc(moe_in, 16)
            sp.wait_ge(scattered, 16 * T)
            for n, (k0, k1) in enumerate(XS_PARTS):
                sp.dma_start(XS[:, k0:k1, :], xs_dram.rearrange("(k p) r -> p k r", p=P)[:, k0:k1, :]).then_inc(xs_in[n], 16)

        @block.scalar
        def _(act):
            def copy(dst, src, scale=None):
                if scale is None:
                    return nc.scalar.activation(dst, src, ACT.Copy)
                return nc.scalar.activation(dst, src, ACT.Copy, scale=scale)

            for h in range(2):
                act.dma_start(CT[:, half(h)], a["ctxT"][:, half(h)]).then_inc(ctxT_in[h], 16)
                if h == 0:
                    act.dma_start(vec[:, :], a["vector_cols"]).then_inc(vec_in, 16)
            act.wait_ge(rows_in, 16)
            nc.scalar.activation(tg[:, :], gates, ACT.Tanh).then_inc(tg_ready, 1)
            for h in range(2):
                act.wait_ge(*filled("xnT_A", h))
                copy(XT[:, half(h)], PS[:, bank("xnT_A", h), :]).then_inc(taken("xnT_A", h)[0], 1)

            def keys_out(h):
                act.wait_ge(*filled("k_C", h))
                copy(KT[:, half(h)], PS[:, bank("k_C", h), :]).then_inc(taken("k_C", h)[0], 1)

            def values_out(h):
                act.wait_ge(*filled("v_C", h))
                for u in range(2):
                    rs = slice(u * SEQ, (u + 1) * SEQ)
                    r = copy(VBD[rs, h * BH:(h + 1) * BH, :, u, 0:DH],
                             PS[rs, bank("v_C", h), :].rearrange("p (b m d) -> p b m d", b=BH, d=DH))
                r.then_inc(taken("v_C", h)[0], 1)

            keys_out(0)
            for h in range(2):
                act.wait_ge(sim_ready, h + 1)
                nc.scalar.activation(sim[:, tiles(h), :], sim[:, tiles(h), :], ACT.Exp).then_inc(a_exp, 1)
                act.wait_ge(btmax_ready, h + 1)
                nc.scalar.activation(bt[:, h, :, :], bt[:, h, :, :], ACT.Exp).then_inc(batt_exp, 1)
            keys_out(1)
            act.wait_ge(mask_ready, 2)
            values_out(0)
            for h in range(2):
                act.wait_ge(*filled("aT", h))
                copy(AT[:, tiles(h), :], by_tile(bank("aT", h))).then_inc(taken("aT", h)[0], 1)
            values_out(1)
            for h in range(2):
                act.wait_ge(*filled("hq", h))
                copy(HT[:, half(h)], PS[:, bank("hq", h), :]).then_inc(taken("hq", h)[0], 1)
            act.wait_ge(fw_in, 16)
            copy(wfT, wfi, float(np.float32(1.0 / 127.0))).then_inc(fw_ready, 1)
            act.wait_ge(*taken("k_C", 1))

            def keys(h, heads):
                for m in heads:
                    nc.scalar.activation(KBD[:, h * BH:(h + 1) * BH, m, :], KT[:, half(h)].rearrange("p (b j) -> p b j", b=BH),
                                         ACT.Copy, scale=mask8[:, m:m + 1]).then_inc(kbd_act, 1)

            def queries(kind, h):
                act.wait_ge(*filled(f"q_{kind}", h))
                o, i = QT[:, half(h)], PS[:, bank(f"q_{kind}", h), :]
                r = copy(o, i, SCALE) if kind == "C" else nc.scalar.activation(o, i, ACT.Identity, bias=bqs[:, 0:1], scale=SCALE)
                r.then_inc(taken(f"q_{kind}", h)[0], 1)

            def normed(kind, h, ln=None):
                act.wait_ge(*filled(f"xnT_{kind}", h))
                o, i = XT[:, half(h)], PS[:, bank(f"xnT_{kind}", h), :]
                r = copy(o, i) if ln is None else nc.scalar.activation(o, i, ACT.Identity, bias=ln[:, 1:2], scale=ln[:, 0:1])
                r.then_inc(taken(f"xnT_{kind}", h)[0], 1)

            for h in range(2):
                act.wait_ge(*filled("xnT_B", h))
                copy(XT[:, half(h)], PS[:, bank("xnT_B", h), :]).then_inc(taken("xnT_B", h)[0], 1)
                for i in range(h * HC, (h + 1) * HC):
                    act.wait_ge(*filled("gate", i))
                    if i >= 2:
                        act.wait_ge(h_ready, i - 1)
                    nc.scalar.activation(SG[:, i % 2, :], PS[:, bank("gate", i), :], ACT.Silu).then_inc(taken("gate", i)[0], 1)
                    if h == 0 or i == 2 * HC - 1:
                        keys(1, range(2 * (i % HC), 2 * (i % HC) + 2) if h == 0 else range(2 * HC, HG))

            def attended(kind, h):
                act.wait_ge(*filled(f"onT_{kind}", h))
                copy(XT[:, half(h)], PS[:, bank(f"onT_{kind}", h), :]).then_inc(taken(f"onT_{kind}", h)[0], 1)

            def probs(k, n):
                kind, g = "CD"[k], CH * k + n
                act.wait_ge(*filled(f"t_{kind}", n))
                if g >= 2:
                    act.wait_ge(*(filled("o_C" if g - 2 < CH else "o_D", (g - 2) % CH // R)
                                  if (g - 2) % R == R - 1 else (pv_first, (g - 2) // R + 1)))
                nc.scalar.activation(PT[:, g % 2, :, :].rearrange("p c d -> p (c d)"), PS[:, bank(f"t_{kind}", n), :],
                                     ACT.Exp).then_inc(taken(f"t_{kind}", n)[0], 1)

            normed("C", 0)
            queries("C", 0)
            act.wait_ge(bqs_ready, 1)
            for n in range(CH + 3):
                if n == 12:
                    attended("C", 0)
                if n == 15:
                    normed("D", 0, ln1)
                if 2 <= n < CH + 2:
                    probs(0, n - 2)
                if n == 1:
                    normed("C", 1)
                if n == 2:
                    queries("C", 1)
                if n == 15:
                    queries("D", 0)
                if n == 15:
                    act.wait_ge(*taken("k_D", 0))
                    keys(0, range(KD, HG))
            for n in range(CH + 3):
                if n == 0:
                    attended("C", 1)
                if n == 3:
                    normed("D", 1, ln1)
                if n == 12:
                    attended("D", 0)
                if 2 <= n < CH + 2:
                    probs(1, n - 2)
                if n == 17:
                    normed("E", 0, ln2)
                if n == 3:
                    queries("D", 1)
                if 4 <= n < 4 + HG - KD:
                    act.wait_ge(*taken("k_D", 1))
                    keys(1, [KD + n - 4])

            def dense(i):
                h, c = divmod(i, FC)
                act.wait_ge(*filled("dense", i))
                nc.scalar.activation(HR[:, c, half(h)], PS[:, bank("dense", i), :], ACT.Gelu, bias=rb1[:, c:c + 1])\
                    .then_inc(taken("dense", i)[0], 1)

            def gate_exps(h):
                act.wait_ge(gsum_ready, h + 1)
                nc.scalar.activation(ge[:, tiles(h), :], ge[:, tiles(h), :], ACT.Exp)
                nc.scalar.activation(gm[:, tiles(h), 2:4], gm[:, tiles(h), 2:4], ACT.Exp).then_inc(gexp_ready, 1)

            attended("D", 1)
            gate_exps(0)
            for i in range(FC):
                dense(i)
            normed("E", 1, ln2)
            nc.scalar.activation(unused[:, :], neg_half[:, 0:1], ACT.Exp)
            gate_exps(1)
            for i in range(FC, 2 * FC):
                dense(i)
            for k in range(BLOCKS):
                act.wait_ge(*filled("eh", k))
                if k >= 2:
                    act.wait_ge(*filled("ey", k - 2))
                for c in range(FC):
                    r = nc.scalar.activation(HB2[:, k % 2, c, :], PS[:, bank("eh", k), c * P:(c + 1) * P], ACT.Gelu,
                                             bias=WBUF[:, k % WB, 2 * F + c:2 * F + c + 1])
                r.then_inc(taken("eh", k)[0], 1)

        @block.gpsimd
        def _(pool):
            steps = [0]

            def link(ins):
                steps[0] += 1
                ins.then_inc(pool_step, 1)
                pool.wait_ge(pool_step, steps[0])

            g = nc.gpsimd
            g.memset(warm[:], 0.0).then_inc(warm_ready, 1)
            link(g.memset(ident[:], 0.0))
            g.affine_select(out=ident[:, :], in_=ident[:, :], compare_op=ALU.not_equal, fill=1.0, base=0,
                            pattern=[[-1, P]], channel_multiplier=1).then_inc(ident_ready, 1)
            g.memset(neg_half[:], -0.5)
            g.memset(bmask[:], 0.0)
            link(g.memset(mask8[:], 1.0))

            def rsqrt(stage, h):
                k = 2 * STAGES.index(stage) + h
                pool.wait_ge(var_ready, k + 1)
                g.tensor_tensor(rstd[:, tiles(h)], ve[:, tiles(h)], neg_half[:, tiles(h)], ALU.pow).then_inc(rstd_ready, 1)

            for r in range(R):
                v = mask8[r * SEQ:(r + 1) * SEQ, :]
                link(g.affine_select(out=v, in_=v, compare_op=ALU.is_ge, fill=0.0, base=0,
                                     pattern=[[-DH, HG]], channel_multiplier=1))
                link(g.affine_select(out=v, in_=v, compare_op=ALU.is_ge, fill=0.0, base=DH - 1,
                                     pattern=[[DH, HG]], channel_multiplier=-1))
                link(g.memset(bmask[r * SEQ:(r + 1) * SEQ, r:r + 1], 1.0))
            g.memset(ABD[:, :, :], 0.0)
            rsqrt("A", 0)
            rsqrt("A", 1)
            g.memset(VBD[:, :, :, :, :], 0.0)
            for h in range(H):
                r = g.memset(slope[:, h:h + 1], slopes[h])
            link(r)
            for u in range(2):
                g.memset(VBD[u * SEQ:(u + 1) * SEQ, :, :, u, DH:DH + 1], 1.0).then_inc(mask_ready, 1)
                pool.wait_ge(mask_ready, u + 1)
            pool.wait_ge(rows_in, 16)
            pool.wait_ge(tg_ready, 1)
            link(g.tensor_scalar(bqvg[:, :], bqv, TG_A, None, ALU.mult))
            for h in range(2):
                pool.wait_ge(x_in[h], 16)
            g.tensor_tensor(XB[:, :, :], X0[:, :, :], over(bqvg[:, :], 1, [P, T, D]), ALU.add).then_inc(xb_ready, 1)
            pool.wait_ge(pos_in, POS)
            link(g.tensor_scalar(mneg, msk, 0.0, -3e38, ALU.is_equal, ALU.mult))
            g.tensor_copy(qpos[:, :], pos_mask[:, 0:T])
            link(g.tensor_copy(ndist[:, :, :], kpos[:, :, :]))
            link(g.tensor_tensor(ndist[:, :, :], ndist[:, :, :], over(qpos[:, :], 2, [P, T, SEQ]), ALU.subtract))
            link(g.tensor_tensor(ndist[:, :, :], ndist[:, :, :], mneg, ALU.add))

            def bias(t):
                g.tensor_tensor(BIAS[:, t, :, :], over(ndist[:, t, :], 1, [P, H, SEQ]),
                                over(slope[:, :], 2, [P, H, SEQ]), ALU.mult).then_inc(bias_ready, 1)

            for t in range(HALF):
                bias(t)
            rsqrt("B", 0)
            rsqrt("B", 1)
            for t in range(HALF, T):
                bias(t)
            rsqrt("C", 0)
            rsqrt("C", 1)

            def less_max(n):
                pool.wait_ge(mx_ready, n + 1)
                if n >= 2:
                    pool.wait_ge(*filled("t_C", n - 2))
                g.tensor_tensor(SM[:, n % 2, :, :], SSB[:, n % 2, :, :], over(mx[:, n % 2, :], 2, [P, HG, SEQ]),
                                ALU.subtract).then_inc(sub_ready, 1)

            def outer_norm(h):
                pool.wait_ge(var1_ready, h + 1)
                link(g.tensor_tensor(rstd1[:, tiles(h)], ve2[:, tiles(h)], neg_half[:, tiles(h)], ALU.pow))
                for t in range(h * HALF, (h + 1) * HALF):
                    r = g.tensor_scalar(U[:, t, :], X3[:, t, :], mv[:, t, 0:1], rstd1[:, t:t + 1], ALU.subtract, ALU.mult)
                link(r)
                g.tensor_tensor(XB[:, tiles(h), :], U[:, tiles(h), :], over(bo, 1, [P, HALF, D]), ALU.add).then_inc(xb_ready, 1)

            for n in range(CH):
                less_max(n)
                if n == 13:
                    rsqrt("D", 0)
            outer_norm(0)
            rsqrt("D", 1)
            outer_norm(1)
            g.memset(ones[:], 1.0)
            for e in range(E):
                g.memset(rev[:, e:e + 1], float(E - e))
            g.memset(cnt[:, 0, 0:1], 0.0)
            link(g.memset(tri[:], 0.0))
            g.affine_select(out=tri[:, :], in_=tri[:, :], compare_op=ALU.is_gt, fill=-1.0, base=0,
                            pattern=[[1, P]], channel_multiplier=-1)
            link(g.memset(seg[:, :, :], 1.0))
            g.memset(seg[:, :, 0:1], 0.0)
            for k in range(T):
                g.memset(nth[:, :, k:k + 1], float(P * k))
            for k in range(BLOCKS):
                r = g.memset(blk[:, k, :], float(k))
            link(r)
            link(g.memset(fill[:, :], 0.0))
            g.memset(fill[:, 2 * D:2 * D + 1].bitcast(I32), NOWHERE).then_inc(fill_ready, 1)
            g.iota(BASE[:, :, 2 * D:2 * D + 1].bitcast(I32), [[P, T], [1, 1]], base=0, channel_multiplier=1)
            g.memset(BASE[:, :, 2 * D + 2:ROW], 0.0).then_inc(mask_ready, 1)
            rsqrt("E", 0)

            def carry(h):
                pool.wait_ge(x4_ready, h + 1)
                for t in range(h * HALF, (h + 1) * HALF):
                    r = g.tensor_scalar(BASE[:, t, D:2 * D], X4[:, t, :], TG_D, None, ALU.mult)
                link(r)
                g.tensor_tensor(BASE[:, tiles(h), D:2 * D], BASE[:, tiles(h), D:2 * D], X3[:, tiles(h), :], ALU.add).then_inc(carried, 1)

            carry(0)
            rsqrt("E", 1)
            carry(1)
            pool.wait_ge(prefilled, 16)
            pool.wait_ge(slot_ready, 1)
            for t in range(T):
                pool.wait_ge(base_ready, t + 1)
                g.indirect_dma_start(xs_dram, bass.IndirectOffsetOnAxis(ap=slot[:, t:t + 1], axis=0), BASE[:, t, :], None)\
                    .then_inc(scattered, 16)
            for k in range(BLOCKS):
                pool.wait_ge(ey_ready, k + 1)
                g.indirect_dma_start(out.rearrange("b s d -> (b s) d"),
                                     bass.IndirectOffsetOnAxis(ap=XS[:, k, 2 * D:2 * D + 1].bitcast(I32), axis=0),
                                     OUTB[:, k % 4, :], None, bounds_check=N - 1, oob_is_err=False).then_inc(out_done[k % 4], 16)
            for n in range(4):
                pool.wait_ge(out_done[n], 16 * len(range(n, BLOCKS, 4)))

        @block.vector
        def _(dve):
            steps = [0]
            v = nc.vector

            def link(ins):
                steps[0] += 1
                ins.then_inc(dve_step, 1)
                dve.wait_ge(dve_step, steps[0])

            def moments(stage, h, src, src_ready=None):
                for t in range(h * HALF, (h + 1) * HALF):
                    last = v.bn_stats(stats[:, t, :], src[:, t, :])
                link(last)
                for t in range(h * HALF, (h + 1) * HALF):
                    last = v.bn_aggr(mv[:, t, :], stats[:, t, :])
                link(last)
                if src_ready is not None:
                    v.tensor_copy(s8[:, 3:4], m8[:, 0:1]).then_inc(src_ready, 1)
                var = mv[:, tiles(h), 1]
                if stage != "D":
                    v.tensor_scalar(ve[:, tiles(h)], var, EPS, None, ALU.add).then_inc(var_ready, 1)
                else:
                    v.tensor_scalar(ve[:, tiles(h)], var, 1.0 + EPS, EPS * EPS, ALU.mult, ALU.add).then_inc(var_ready, 1)
                    v.tensor_scalar(ve2[:, tiles(h)], var, EPS, None, ALU.add).then_inc(var1_ready, 1)

            def normalise(stage, h, src, dst=XN):
                dve.wait_ge(rstd_ready, 2 * STAGES.index(stage) + h + 1)
                for t in range(h * HALF, (h + 1) * HALF):
                    r = v.tensor_scalar(dst[:, t, 0:D], src[:, t, :], mv[:, t, 0:1], rstd[:, t:t + 1], ALU.subtract, ALU.mult)
                r.then_inc(xn_ready, 1)

            def residual(stage, h, xin, xout, gate):
                dve.wait_ge(*filled(f"y_{stage}", h))
                yp = by_tile(bank(f"y_{stage}", h))
                if gate is None:
                    r = v.tensor_tensor(xout[:, tiles(h), :], yp, xin[:, tiles(h), :], ALU.add)
                else:
                    r = v.scalar_tensor_tensor(xout[:, tiles(h), :], yp, gate, xin[:, tiles(h), :], ALU.mult, ALU.add)
                r.then_inc(taken(f"y_{stage}", h)[0], 1)
                dve.wait_ge(*taken(f"y_{stage}", h))

            for h in range(2):
                dve.wait_ge(x_in[h], 16)
                moments("A", h, X0)
            for h in range(2):
                normalise("A", h, X0)
            v.memset(w2b[:, :], 0.0).then_inc(w2b_ready, 1)
            dve.wait_ge(w2b_ready, 1)
            dve.wait_ge(vec_in, 16)
            v.tensor_scalar(w2b[:, :], w2b[:, :], wsim[:, 1:2], None, ALU.add).then_inc(w2b_ready, 1)
            for h in range(2):
                dve.wait_ge(ctxT_in[h], 16)
                v.tensor_scalar(C3T[:, half(h)], CT[:, half(h)], wsim[:, 2:3], wsim[:, 0:1], ALU.mult, ALU.add).then_inc(c3_ready, 1)
            dve.wait_ge(rows_in, 16)
            for h in range(2):
                dve.wait_ge(*filled("sim", h))
                S3 = PS[:, bank("sim", h), 0:HALF * SEQ].rearrange("p (t j) -> p t j", t=HALF)
                link(v.tensor_reduce(m8[:, tiles(h)], S3, AX_X, ALU.max))
                v.tensor_scalar(mf8[:, tiles(h)], m8[:, tiles(h)], bsim[:, 0:1], None, ALU.add).then_inc(mf_ready, 1)
                v.tensor_tensor(sim[:, tiles(h), :], S3, over(m8[:, tiles(h)], 2, [P, HALF, SEQ]), ALU.subtract)\
                    .then_inc(taken("sim", h)[0], 1)
                dve.wait_ge(*taken("sim", h))
                v.tensor_copy(s8[:, 0:1], m8[:, 0:1]).then_inc(sim_ready, 1)
            for h in range(2):
                dve.wait_ge(*filled("mT", h))
                M3 = PS[0:HALF, bank("mT", h), 0:P].rearrange("p (q i) -> p q i", q=2)
                link(v.tensor_reduce(bts[:, h, 0, :], M3, AX_X, ALU.max))
                link(v.tensor_tensor(bt[:, h, :, :], M3, over(bts[:, h, 0, :], 2, [HALF, 2, SEQ]), ALU.subtract))
                v.tensor_copy(bts[:, h, 1, :], bts[:, h, 0, :]).then_inc(taken("mT", h)[0], 1)
                dve.wait_ge(*taken("mT", h))
                v.tensor_copy(bts[:, h, 2, :], bts[:, h, 0, :]).then_inc(btmax_ready, 1)
            for h in range(2):
                dve.wait_ge(a_exp, h + 1)
                link(v.tensor_reduce(s8[:, tiles(h)], sim[:, tiles(h), :], AX_X, ALU.add))
                link(v.reciprocal(r8[:, tiles(h)], s8[:, tiles(h)]))
                for q in range(2):
                    rs = slice(q * SEQ, (q + 1) * SEQ)
                    v.tensor_tensor(ABD[rs, tiles(h), rs], sim[rs, tiles(h), :], over(r8[rs, tiles(h)], 2, [SEQ, HALF, SEQ]),
                                    ALU.mult).then_inc(a_ready, 1)
                dve.wait_ge(batt_exp, h + 1)
                link(v.tensor_reduce(bts[:, h, 1, :], bt[:, h, :, :], AX_X, ALU.add))
                link(v.reciprocal(bts[:, h, 2, :], bts[:, h, 1, :]))
                v.tensor_tensor(bt[:, h, :, :], bt[:, h, :, :], over(bts[:, h, 2, :], 2, [HALF, 2, SEQ]), ALU.mult).then_inc(bt_ready, 1)
            dve.wait_ge(mask_ready, 2)

            def keys(h, heads):
                for m in heads:
                    v.tensor_scalar(KBD[:, h * BH:(h + 1) * BH, m, :], KT[:, half(h)].rearrange("p (b j) -> p b j", b=BH),
                                    mask8[:, m:m + 1], None, ALU.mult).then_inc(kbd_dve, 1)

            for h in range(2):
                dve.wait_ge(*filled("btT", h))
                for q in range(2):
                    r = v.tensor_scalar(battm[:, tiles(h), q], PS[:, bank("btT", h), 0:HALF], bmask[:, q:q + 1], None, ALU.mult)
                r.then_inc(taken("btT", h)[0], 1)
                dve.wait_ge(*filled("hc", h))
                v.tensor_copy(hc[:, h * BH:(h + 1) * BH], PS[:, bank("hc", h), 0:BH]).then_inc(taken("hc", h)[0], 1)
                dve.wait_ge(*taken("hc", h))
                dve.wait_ge(*taken("xnT_A", h))
                v.tensor_tensor(EHC[:, half(h)].rearrange("p (b i) -> p b i", b=BH), XT[:, half(h)].rearrange("p (b i) -> p b i", b=BH),
                                over(hc[:, h * BH:(h + 1) * BH], 2, [P, BH, SEQ]), ALU.mult).then_inc(feat_ready, 1)
                dve.wait_ge(*taken("hq", h))
                v.tensor_tensor(EHT[:, half(h)], XT[:, half(h)], HT[:, half(h)], ALU.mult).then_inc(feat_ready, 1)
            dve.wait_ge(*taken("k_C", 0))
            keys(0, range(HG))
            dve.wait_ge(tg_ready, 1)
            dve.wait_ge(xb_ready, 1)
            for h in range(2):
                residual("A", h, XB, X1, TG_A)
                moments("B", h, X1)
                normalise("B", h, X1)

            for h in range(2):
                for i in range(h * HC, (h + 1) * HC):
                    dve.wait_ge(*filled("up", i))
                    dve.wait_ge(*taken("gate", i))
                    v.tensor_tensor(HB[:, i % HC, half(h)], SG[:, i % 2, :], PS[:, bank("up", i), :], ALU.mult).then_inc(taken("up", i)[0], 1)
                    dve.wait_ge(*taken("up", i))
                    v.tensor_copy(s8[:, 1:2], m8[:, 0:1]).then_inc(h_ready, 1)
                    if i == HC:
                        residual("B", 0, X1, X2, TG_B)
                        moments("C", 0, X2)
                    if i == HC + 1:
                        normalise("C", 0, X2)
            residual("B", 1, X1, X2, TG_B)
            moments("C", 1, X2)
            normalise("C", 1, X2)
            v.tensor_scalar(bqs[:, :], bqk[:, 0:1], SCALE, None, ALU.mult).then_inc(bqs_ready, 1)

            def head_out(kind, t):
                dve.wait_ge(*filled(f"o_{kind}", t))
                o4 = PS[:, bank(f"o_{kind}", t), 0:H * (DH + 1)].rearrange("p (h d) -> p h d", h=H)
                if kind == "C":
                    link(v.tensor_scalar(den[:, t, :], o4[:, :, DH], 1.0, None, ALU.add))
                    link(v.reciprocal(rec[:, t, :], den[:, t, :]))
                else:
                    link(v.reciprocal(rec[:, t, :], o4[:, :, DH]))
                v.tensor_tensor(ON[:, t, :].rearrange("p (h d) -> p h d", h=H), o4[:, :, 0:DH],
                                over(rec[:, t, :], 2, [P, H, DH]), ALU.mult).then_inc(taken(f"o_{kind}", t)[0], 1)

            def keys_out(h):
                dve.wait_ge(*filled("k_D", h))
                v.tensor_scalar(KT[:, half(h)], PS[:, bank("k_D", h), :], bqk[:, 1:2], None, ALU.add).then_inc(taken("k_D", h)[0], 1)
                dve.wait_ge(*taken("k_D", h))

            def values_out(h):
                dve.wait_ge(*filled("v_D", h))
                for u in range(2):
                    rs = slice(u * SEQ, (u + 1) * SEQ)
                    bias = bv[rs, :].rearrange("p (m u d) -> p m u d", u=2, d=DH)[:, :, u, :]
                    r = v.tensor_tensor(VBD[rs, h * BH:(h + 1) * BH, :, u, 0:DH],
                                        PS[rs, bank("v_D", h), :].rearrange("p (b m d) -> p b m d", b=BH, d=DH),
                                        over(bias, 1, [SEQ, BH, HG, DH]), ALU.add)
                r.then_inc(taken("v_D", h)[0], 1)

            for n in range(CH + 4):
                if n < CH:
                    t, r = divmod(n, R)
                    dve.wait_ge(*filled("s_C", n))
                    dve.wait_ge(bias_ready, t + 1)
                    if n >= 2:
                        dve.wait_ge(sub_ready, n - 1)
                    v.tensor_tensor(SSB[:, n % 2, :, :], PS[:, bank("s_C", n), :].rearrange("p (h j) -> p h j", h=HG),
                                    BIAS[:, t, r * HG:(r + 1) * HG, :], ALU.add).then_inc(taken("s_C", n)[0], 1)
                    dve.wait_ge(*taken("s_C", n))
                    v.tensor_reduce(mx[:, n % 2, :], SSB[:, n % 2, :, :], AX_X, ALU.max).then_inc(mx_ready, 1)
                if n >= 5 and (n - 5) % R == 0:
                    head_out("C", (n - 5) // R)
                if n == 13:
                    residual("C", 0, X2, X3, TG_C)
                    moments("D", 0, X3)
                if n == 14:
                    normalise("D", 0, X3)
                if n == 16:
                    keys_out(0)
                    keys(0, range(KD))
                    values_out(0)
            for n in range(CH + 4):
                if n < CH:
                    g = CH + n
                    dve.wait_ge(*filled("s_D", n))
                    sp3 = PS[:, bank("s_D", n), :].rearrange("p (h j) -> p h j", h=HG)
                    link(v.tensor_reduce(mx[:, n % 2, :], sp3, AX_X, ALU.max))
                    if n >= 2:
                        dve.wait_ge(*filled("t_D", n - 2))
                    v.tensor_tensor(SM[:, n % 2, :, :], sp3, over(mx[:, n % 2, :], 2, [P, HG, SEQ]),
                                    ALU.subtract).then_inc(taken("s_D", n)[0], 1)
                if n >= 5 and (n - 5) % R == 0:
                    head_out("D", (n - 5) // R)
                if n == 1:
                    residual("C", 1, X2, X3, TG_C)
                    moments("D", 1, X3)
                if n == 2:
                    normalise("D", 1, X3)
                if n == 3:
                    keys_out(1)
                if 4 <= n < 4 + (KD + 1) // 2:
                    keys(1, range(KD)[2 * (n - 4):2 * (n - 3)])
                if n == 7:
                    values_out(1)
                if n == 13:
                    dve.wait_ge(xb_ready, 2)
                    residual("D", 0, XB, X4, None)
                    moments("E", 0, X4, x4_ready)
                if n == 15:
                    normalise("E", 0, X4, BASE)
            def gate_inputs(h):
                dve.wait_ge(*filled("lg", h))
                L3 = PS[:, bank("lg", h), 0:HALF * (E + 2)].rearrange("p (t e) -> p t e", t=HALF)
                ts, shape = tiles(h), [P, HALF, E]
                v.tensor_reduce(gm[:, ts, 0], L3[:, :, 0:E], AX_X, ALU.max)
                link(v.tensor_tensor(lg[:, ts, :], L3[:, :, E:E + 2], over(coefb, 1, [P, HALF, 2]), ALU.add))
                link(v.tensor_tensor(oh[:, ts, :], L3[:, :, 0:E], over(gm[:, ts, 0], 2, shape), ALU.is_equal))
                link(v.tensor_tensor(oh[:, ts, :], oh[:, ts, :], over(rev[:, :], 1, shape), ALU.mult))
                link(v.tensor_reduce(gm[:, ts, 6], oh[:, ts, :], AX_X, ALU.max))
                v.tensor_tensor(oh[:, ts, :], over(rev[:, :], 1, shape), over(gm[:, ts, 6], 2, shape), ALU.is_equal).then_inc(oh_ready, 1)
                v.tensor_tensor(ge[:, ts, :], L3[:, :, 0:E], over(gm[:, ts, 0], 2, shape), ALU.subtract).then_inc(taken("lg", h)[0], 1)
                link(v.tensor_reduce(gm[:, ts, 1], lg[:, ts, :], AX_X, ALU.max))
                v.tensor_tensor(gm[:, ts, 2:4], lg[:, ts, :], over(gm[:, ts, 1], 2, [P, HALF, 2]), ALU.subtract).then_inc(gsum_ready, 1)

            def gate_values(h):
                ts = tiles(h)
                dve.wait_ge(gexp_ready, h + 1)
                v.tensor_reduce(gm[:, ts, 4], ge[:, ts, :], AX_X, ALU.add)
                link(v.tensor_reduce(gm[:, ts, 5], gm[:, ts, 2:4], AX_X, ALU.add))
                link(v.reciprocal(gm[:, ts, 4:6], gm[:, ts, 4:6]))
                link(v.tensor_scalar(gm[:, ts, 5], gm[:, ts, 5], TG_D, None, ALU.mult))
                link(v.tensor_tensor(gm[:, ts, 2:4], gm[:, ts, 2:4], over(gm[:, ts, 5], 2, [P, HALF, 2]), ALU.mult))
                link(v.tensor_tensor(BASE[:, ts, 2 * D + 1], gm[:, ts, 4], gm[:, ts, 2], ALU.mult))

            def dense_bias(h):
                dve.wait_ge(carried, h + 1)
                for t in range(h * HALF, (h + 1) * HALF):
                    r = v.scalar_tensor_tensor(BASE[:, t, D:2 * D], rb2, gm[:, t, 3:4], BASE[:, t, D:2 * D], ALU.mult, ALU.add)
                link(r)

            def base(i, some):
                dve.wait_ge(*filled("ry", i))
                for t in some:
                    v.scalar_tensor_tensor(BASE[:, t, D:2 * D], PS[:, bank("ry", i), tile_cols(t)], gm[:, t, 3:4],
                                           BASE[:, t, D:2 * D], ALU.mult, ALU.add).then_inc(base_ready, 1)

            dve.wait_ge(mask_ready, 3)
            gate_inputs(0)
            dve.wait_ge(xb_ready, 3)
            residual("D", 1, XB, X4, None)
            moments("E", 1, X4, x4_ready)
            gate_values(0)
            normalise("E", 1, X4, BASE)
            dense_bias(0)
            gate_inputs(1)
            dve.wait_ge(*filled("rank"))
            rk = bank("rank")
            after = PS[:, rk, 0:T * E].rearrange("p (e t) -> p e t", t=T)
            A0, A1, A2, A3 = (ranks[:, n, :].rearrange("p (e t) -> p e t", e=E) for n in range(4))
            link(v.tensor_tensor_scan(ranks[:, 0, :], seg[:, :, :].rearrange("p e t -> p (e t)"), PS[:, rk, T * E:2 * T * E],
                                      0.0, ALU.mult, ALU.add))
            link(v.tensor_tensor(A1, over(A0[:, :, T - 1], 2, [P, E, T]), nth[:, :, :], ALU.is_gt))
            v.tensor_tensor(A2, A0, after, ALU.add).then_inc(taken("rank")[0], 1)
            link(v.tensor_reduce(cnt[:, 0, 1:E + 1], A1, AX_X, ALU.add))
            link(v.tensor_tensor_scan(cnt[:, 1, :], ones[:, 0:E + 1], cnt[:, 0, :], 0.0, ALU.mult, ALU.add))
            link(v.scalar_tensor_tensor(A3, over(cnt[:, 1, 0:E], 2, [P, E, T]), float(P), A2, ALU.mult, ALU.add))
            link(v.tensor_tensor(A3, A3, oh_by_e[:, :, :], ALU.mult))
            link(v.tensor_reduce(cnt[:, 2, 0:T], A3.rearrange("p e t -> p t e"), AX_X, ALU.add))
            v.tensor_copy(slot[:, :], cnt[:, 2, 0:T]).then_inc(slot_ready, 1)
            base(0, range(HALF))
            link(v.tensor_tensor(own[:, :, :], over(cnt[0:1, 1, 1:E + 1], 1, [1, BLOCKS, E]), blk[:, :, :], ALU.is_le))
            link(v.tensor_reduce(bexp[:, :], own[:, :, :], AX_X, ALU.add))
            link(v.tensor_scalar(bexpi[:, :], bexp[:, :], float(E - 1), None, ALU.min))
            chosen = []

            def read_experts(upto):
                for k in range(len(chosen), upto):
                    chosen.append(v.value_load(bexpi[0:1, k:k + 1], min_val=0, max_val=E - 1))

            gate_values(1)
            dense_bias(1)
            read_experts(2)
            base(1, (HALF, HALF + 1))
            base(2, (HALF + 2, HALF + 3))
            def weights(k):
                if k == 0:
                    dve.wait_ge(moe_in, MOE)
                if k >= WB:
                    dve.wait_ge(*filled("ey", k - WB))
                v.tensor_copy(WBUF[:, k % WB, :], experts[:, bass.ds(chosen[k], 1), :]).then_inc(w_copied, 1)

            def inputs(k):
                dve.wait_ge(*filled("xsT", k))
                if k >= 2:
                    dve.wait_ge(*filled("eh", k - 2))
                v.tensor_scalar(XST[:, k % 2, :], PS[:, bank("xsT", k), 0:P], ln2[:, 0:1], ln2[:, 1:2], ALU.mult, ALU.add)\
                    .then_inc(taken("xsT", k)[0], 1)

            def results(k):
                dve.wait_ge(*filled("ey", k))
                v.tensor_tensor(YB[:, k % 2, :], PS[:, bank("ey", k), 0:P], WBUF[:, k % WB, 2 * F + FC:EW], ALU.add)\
                    .then_inc(taken("ey", k)[0], 1)
                dve.wait_ge(*taken("ey", k))
                if k >= 4:
                    dve.wait_ge(out_done[k % 4], 16 * (k // 4))
                v.scalar_tensor_tensor(OUTB[:, k % 4, :], YB[:, k % 2, :], XS[:, k, 2 * D + 1:2 * D + 2], XS[:, k, D:2 * D],
                                       ALU.mult, ALU.add).then_inc(ey_ready, 1)

            read_experts(WB)
            for k in range(WB):
                weights(k)
            read_experts(11)
            inputs(0)
            for k in range(BLOCKS):
                if k + 1 < BLOCKS:
                    inputs(k + 1)
                read_experts(min(12 + k, BLOCKS))
                if k >= 1:
                    results(k - 1)
                    if k - 1 + WB < BLOCKS:
                        weights(k - 1 + WB)
            results(BLOCKS - 1)

        @block.tensor
        def _(pe):
            mm, tr = nc.tensor.matmul, nc.tensor.transpose

            def keep_warm(name, i, n):
                b = empty(pe, name, i)
                for _ in range(n):
                    mm(PS[:, b, :], warm[:, 0:P], warm[:, :], start=True, stop=True)

            def turn_tiles(name, h, src):
                b = empty(pe, name, h)
                for t in range(h * HALF, (h + 1) * HALF):
                    r = tr(PS[:, b, tile_cols(t)], src[:, t, 0:P], ident[:, :])
                r.then_inc(filled(name, h)[0], 1)

            def stay_warm(name, h):
                if (name, h) in WARM:
                    keep_warm(name, h, WARM[name, h])

            def norm_transpose(stage, h):
                stay_warm(f"xnT_{stage}", h)
                pe.wait_ge(xn_ready, 2 * STAGES.index(stage) + h + 1)
                turn_tiles(f"xnT_{stage}", h, BASE if stage == "E" else XN)

            def values(name, h, xT, w):
                b = empty(pe, name, h)
                for i in range(h * BH, (h + 1) * BH):
                    at = (i % BH) * SEQ
                    for u in range(2):
                        r = mm(PS[u * SEQ:(u + 1) * SEQ, b, at:at + SEQ], xT[:, i * SEQ:(i + 1) * SEQ],
                               w.rearrange("p (m u d) -> p m u d", u=2, d=DH)[:, :, u, :], start=True, stop=True)
                r.then_inc(filled(name, h)[0], 1)

            def keys_C(h):
                mm(PS[:, empty(pe, "k_C", h), :], xwT[:, 1, :], CT[:, half(h)], start=True, stop=True).then_inc(filled("k_C", h)[0], 1)

            pe.wait_ge(warm_ready, 1)
            keep_warm("sim", 0, 12)
            pe.wait_ge(ident_ready, 1)
            for h in range(2):
                norm_transpose("A", h)
            pe.wait_ge(wa_in, 16)
            pe.wait_ge(ctxT_in[0], 16)
            keys_C(0)
            pe.wait_ge(w2b_ready, 2)
            for h in range(2):
                pe.wait_ge(c3_ready, h + 1)
                pe.wait_ge(*taken("xnT_A", h))
                b = empty(pe, "sim", h)
                for i in range(h * BH, (h + 1) * BH):
                    t, q = divmod(i, 2)
                    bs = slice(i * SEQ, (i + 1) * SEQ)
                    o = PS[q * SEQ:(q + 1) * SEQ, b, (t % HALF) * SEQ:(t % HALF + 1) * SEQ]
                    mm(o, XT[:, bs], C3T[:, bs], start=True, stop=False)
                    r = mm(o, w2b[:, :], CT[:, bs], start=False, stop=True)
                r.then_inc(filled("sim", h)[0], 1)
            keys_C(1)
            values("v_C", 0, CT, xwT[:, 2, :])
            for h in range(2):
                pe.wait_ge(mf_ready, h + 1)
                tr(PS[0:HALF, empty(pe, "mT", h), 0:P], mf8[:, tiles(h)], ident[:, :]).then_inc(filled("mT", h)[0], 1)
            values("v_C", 1, CT, xwT[:, 2, :])
            for h in range(2):
                stay_warm("aT", h)
                pe.wait_ge(a_ready, 2 * (h + 1))
                turn_tiles("aT", h, ABD)
            pe.wait_ge(ctx_in, 16)
            for h in range(2):
                stay_warm("btT", h)
                pe.wait_ge(bt_ready, h + 1)
                tr(PS[:, empty(pe, "btT", h), 0:HALF], bt[:, h, :, :].rearrange("p q i -> p (q i)"), ident[0:HALF, 0:HALF])\
                    .then_inc(filled("btT", h)[0], 1)
                pe.wait_ge(*taken("aT", h))
                b = empty(pe, "hq", h)
                for t in range(h * HALF, (h + 1) * HALF):
                    r = mm(PS[:, b, tile_cols(t)], C[:, t, :], AT[:, t, :], start=True, stop=True)
                r.then_inc(filled("hq", h)[0], 1)
                pe.wait_ge(*taken("btT", h))
                b = empty(pe, "hc", h)
                for t in range(h * HALF, (h + 1) * HALF):
                    at = 2 * (t % HALF)
                    r = mm(PS[:, b, at:at + 2], XN[:, t, :], battm[:, t, :], start=True, stop=True)
                r.then_inc(filled("hc", h)[0], 1)

            def project(name, h, lhs_of, ws):
                b = empty(pe, name, h)
                for t in range(h * HALF, (h + 1) * HALF):
                    for c, w in enumerate(ws):
                        r = mm(PS[:, b, tile_cols(t)], lhs_of(t, c), w, start=(c == 0), stop=(c == len(ws) - 1))
                r.then_inc(filled(name, h)[0], 1)

            feats = [XT, HT, EHT, EHC]
            for h in range(2):
                stay_warm("y_A", h)
                pe.wait_ge(feat_ready, 2 * (h + 1))
                project("y_A", h, lambda t, c: feats[c][:, t * P:(t + 1) * P], [wqv[:, c, :] for c in range(4)])

            def queries(kind, h, w):
                pe.wait_ge(*taken(f"xnT_{kind}", h))
                mm(PS[:, empty(pe, f"q_{kind}", h), :], w, XT[:, half(h)], start=True, stop=True).then_inc(filled(f"q_{kind}", h)[0], 1)

            pe.wait_ge(fw_ready, 1)
            for h in range(2):
                norm_transpose("B", h)
                if h == 1:
                    pe.wait_ge(h_ready, HC)
                    project("y_B", 0, lambda t, c: HB[:, c, t * P:(t + 1) * P], [wfT[:, 2 * HC + c, :] for c in range(HC)])
                pe.wait_ge(*taken("xnT_B", h))
                for i in range(h * HC, (h + 1) * HC):
                    c = i % HC
                    mm(PS[:, empty(pe, "gate", i), :], wfT[:, c, :], XT[:, half(h)], start=True, stop=True).then_inc(filled("gate", i)[0], 1)
                    mm(PS[:, empty(pe, "up", i), :], wfT[:, HC + c, :], XT[:, half(h)], start=True, stop=True).then_inc(filled("up", i)[0], 1)
            norm_transpose("C", 0)
            queries("C", 0, xwT[:, 0, :])
            pe.wait_ge(h_ready, 2 * HC)
            project("y_B", 1, lambda t, c: HB[:, c, t * P:(t + 1) * P], [wfT[:, 2 * HC + c, :] for c in range(HC)])

            def queries_keys(h):
                queries("D", h, wqkv[:, 0:D])
                mm(PS[:, empty(pe, "k_D", h), :], wqkv[:, D:2 * D], XT[:, half(h)], start=True, stop=True).then_inc(filled("k_D", h)[0], 1)

            def scores(k, n):
                kind = "CD"[k]
                t, r = divmod(n, R)
                if n % (CH // 2) == 0:
                    h = n // (CH // 2)
                    pe.wait_ge(*taken(f"q_{kind}", h))
                    pe.wait_ge(kbd_dve, HG if k == 0 else HG + KD * (h + 1))
                    if k == 1 or h == 1:
                        pe.wait_ge(kbd_act, HG if k == 0 else HG + (HG - KD) * (h + 1))
                b = empty(pe, f"s_{kind}", n)
                rs = slice(r * SEQ, (r + 1) * SEQ)
                for q in range(2):
                    i = 2 * t + q
                    x = mm(PS[q * SEQ:(q + 1) * SEQ, b, :], QT[rs, i * SEQ:(i + 1) * SEQ],
                           KBD[rs, i, :, :].rearrange("p h j -> p (h j)"), start=True, stop=True)
                x.then_inc(filled(f"s_{kind}", n)[0], 1)

            def turn(k, n):
                kind = "CD"[k]
                if n < CH - 3:
                    keep_warm(f"t_{kind}", n, FILL[n % 2])
                pe.wait_ge(*((sub_ready, n + 1) if k == 0 else taken("s_D", n)))
                b = empty(pe, f"t_{kind}", n)
                for m in range(HG // 2):
                    x = tr(PS[:, b, m * P:(m + 1) * P], SM[:, n % 2, 2 * m:2 * m + 2, :].rearrange("p h j -> p (h j)"), ident[:, :])
                x.then_inc(filled(f"t_{kind}", n)[0], 1)

            def weigh(k, n):
                kind = "CD"[k]
                t, r = divmod(n, R)
                pe.wait_ge(*taken(f"t_{kind}", n))
                if n % (CH // 2) == 0:
                    pe.wait_ge(*taken(f"v_{kind}", n // (CH // 2)))
                if r == 0:
                    b = empty(pe, f"o_{kind}", t)
                b = bank(f"o_{kind}", t)
                for m in range(HG // 2):
                    hp = r * (HG // 2) + m
                    for q in range(2):
                        at = hp * 2 * (DH + 1)
                        x = mm(PS[q * SEQ:(q + 1) * SEQ, b, at:at + 2 * (DH + 1)], PT[:, n % 2, m, q * SEQ:(q + 1) * SEQ],
                               VBD[:, 2 * t + q, hp, :, :].rearrange("p u d -> p (u d)"), start=True, stop=True)
                if r == 0:
                    x.then_inc(pv_first, 1)
                else:
                    x.then_inc(filled(f"o_{kind}", t)[0], 1)

            def output(kind, h, w):
                pe.wait_ge(*taken(f"onT_{kind}", h))
                project(f"y_{kind}", h, lambda t, c: XT[:, t * P:(t + 1) * P], [w])

            def heads_transpose(kind, h):
                stay_warm(f"onT_{kind}", h)
                for t in range(h * HALF, (h + 1) * HALF)[-2:]:
                    pe.wait_ge(*taken(f"o_{kind}", t))
                turn_tiles(f"onT_{kind}", h, ON)

            def gate_logits(h):
                pe.wait_ge(*taken("xnT_E", h))
                b = empty(pe, "lg", h)
                for t in range(h * HALF, (h + 1) * HALF):
                    at = (t % HALF) * (E + 2)
                    r = mm(PS[:, b, at:at + E + 2], XT[:, t * P:(t + 1) * P], wgc, start=True, stop=True)
                r.then_inc(filled("lg", h)[0], 1)

            def dense(i):
                h, c = divmod(i, FC)
                mm(PS[:, empty(pe, "dense", i), :], rw1[:, c * P:(c + 1) * P], XT[:, half(h)],
                   start=True, stop=True).then_inc(filled("dense", i)[0], 1)

            pe.wait_ge(wb_in, 16)
            pe.wait_ge(vec_in, 16)
            for n in range(CH + 3):
                if n < CH:
                    scores(0, n)
                if n == 12:
                    heads_transpose("C", 0)
                if n == 15:
                    norm_transpose("D", 0)
                if 2 <= n < CH + 2:
                    turn(0, n - 2)
                if n == 15:
                    queries_keys(0)
                if n >= 3:
                    weigh(0, n - 3)
                if n == 1:
                    norm_transpose("C", 1)
                if n == 2:
                    queries("C", 1, xwT[:, 0, :])
                if n == 12:
                    output("C", 0, xwT[:, 3, :])
                if n == 16:
                    values("v_D", 0, XT, wqkv[:, 2 * D:3 * D])
                if n in GAP:
                    keep_warm("s_D", 0, GAP[n])
            for n in range(CH + 3):
                if n < CH:
                    scores(1, n)
                if n == 0:
                    heads_transpose("C", 1)
                if n == 1:
                    output("C", 1, xwT[:, 3, :])
                if n == 3:
                    norm_transpose("D", 1)
                if n == 4:
                    values("v_D", 1, XT, wqkv[:, 2 * D:3 * D])
                if n == 12:
                    heads_transpose("D", 0)
                if 2 <= n < CH + 2:
                    turn(1, n - 2)
                if n == 3:
                    queries_keys(1)
                if n >= 3:
                    weigh(1, n - 3)
                if n == 12:
                    output("D", 0, wo)
                if n == 17:
                    norm_transpose("E", 0)
                if n == 18:
                    gate_logits(0)

            def dense_out(i, some):
                b = empty(pe, "ry", i) if some[0] in (0, HALF) else bank("ry", i)
                for t in some:
                    for c in range(FC):
                        r = mm(PS[:, b, tile_cols(t)], HR[:, c, t * P:(t + 1) * P], rw2[:, c, :], start=(c == 0), stop=(c == FC - 1))
                return r

            dense(0)
            heads_transpose("D", 1)
            dense(1)
            output("D", 1, wo)
            for i in range(2, FC):
                dense(i)
            for i in range(FC):
                pe.wait_ge(*taken("dense", i))
            dense_out(0, [0])
            norm_transpose("E", 1)
            dense_out(0, [1])
            gate_logits(1)
            dense_out(0, [2])
            pe.wait_ge(mask_ready, 3)
            pe.wait_ge(oh_ready, 2)
            b = empty(pe, "rank")
            flat = oh_by_e[:, :, :].rearrange("p e t -> p (e t)")
            mm(PS[:, b, 0:T * E], tri[:, :], flat, start=True, stop=True)
            mm(PS[:, b, T * E:2 * T * E], ones[:, :], flat, start=True, stop=True).then_inc(filled("rank")[0], 1)
            dense_out(0, [3]).then_inc(filled("ry", 0)[0], 1)
            for i in range(FC, 2 * FC):
                dense(i)
            for i in range(FC, 2 * FC):
                pe.wait_ge(*taken("dense", i))
            dense_out(1, [HALF, HALF + 1]).then_inc(filled("ry", 1)[0], 1)
            pe.wait_ge(base_ready, HALF)
            dense_out(2, [HALF + 2, HALF + 3]).then_inc(filled("ry", 2)[0], 1)
            keep_warm("eh", 0, 34)

            def turn_slots(k):
                for n, (k0, _) in enumerate(XS_PARTS):
                    if k == k0:
                        pe.wait_ge(xs_in[n], 16)
                b = empty(pe, "xsT", k)
                tr(PS[:, b, 0:P], XS[:, k, 0:D], ident[:, :]).then_inc(filled("xsT", k)[0], 1)

            def hidden(k):
                pe.wait_ge(*taken("xsT", k))
                pe.wait_ge(w_copied, k + 1)
                b = empty(pe, "eh", k)
                for c in range(FC):
                    r = mm(PS[:, b, c * P:(c + 1) * P], WBUF[:, k % WB, c * P:(c + 1) * P], XST[:, k % 2, :], start=True, stop=True)
                r.then_inc(filled("eh", k)[0], 1)

            def down(k):
                pe.wait_ge(*taken("eh", k))
                b = empty(pe, "ey", k)
                for c in range(FC):
                    r = mm(PS[:, b, 0:P], HB2[:, k % 2, c, :], WBUF[:, k % WB, F + c * D:F + (c + 1) * D],
                           start=(c == 0), stop=(c == FC - 1))
                r.then_inc(filled("ey", k)[0], 1)

            turn_slots(0)
            for k in range(BLOCKS + 1):
                if k + 1 < BLOCKS:
                    turn_slots(k + 1)
                if k < BLOCKS:
                    hidden(k)
                if k >= 1:
                    down(k - 1)


def layout(x, ctx_1024, itok_BxS_8_8191, itok_BxS2_1_8191, mask_BxSxS2_if1, g_xattn, g_ffn, L0_xattn_w_sim, L0_xattn_b_sim,
           L0_xattn_W_qv, L0_xattn_b_qv, L0_ffn_w_gate, L0_ffn_w_up, L0_ffn_w_down, L1_xattn_W_q, L1_xattn_W_k, L1_xattn_W_v,
           L1_xattn_W_o, L1_ffn_ln1_g, L1_ffn_ln1_b, L1_ffn_Wqkv, L1_ffn_bqkv, L1_ffn_Wo, L1_ffn_bo, L1_ffn_ln2_g, L1_ffn_ln2_b,
           L1_ffn_gate_w, L1_ffn_W1, L1_ffn_b1, L1_ffn_W2, L1_ffn_b2, L1_ffn_rW1, L1_ffn_rb1, L1_ffn_rW2, L1_ffn_rb2,
           L1_ffn_coef_w, L1_ffn_coef_b):
    import numpy as np

    B, SEQ, D = x.shape
    E = L1_ffn_W1.shape[0]

    def by_token(v):
        return v.reshape(-1, 128, v.shape[-1]).transpose(1, 0, 2)

    def chunks(w):
        return w.reshape(-1, 128, w.shape[-1]).transpose(1, 0, 2)

    def cols(v):
        return v.reshape(-1, 128).T

    def flat(w):
        return w.reshape(w.shape[0], -1)

    experts = [np.concatenate([L1_ffn_W1[e], flat(chunks(L1_ffn_W2[e])), cols(L1_ffn_b1[e])], axis=1) for e in range(E)]
    return {
        "x": by_token(x),
        "ctx": by_token(ctx_1024),
        "ctxT": ctx_1024.reshape(B * SEQ, D).T,
        "vector_cols": np.concatenate(
            [cols(v) for v in (L0_xattn_w_sim, L1_ffn_bqkv, L1_ffn_ln1_g, L1_ffn_ln1_b, L1_ffn_ln2_g, L1_ffn_ln2_b, L1_ffn_rb1)]
            + [L1_ffn_gate_w, L1_ffn_coef_w], axis=1),
        "vector_rows": np.concatenate([L0_xattn_b_qv, L1_ffn_bqkv[2 * D:], L1_ffn_bo, L1_ffn_rb2, L1_ffn_coef_b, g_xattn, g_ffn,
                                       L0_xattn_b_sim]),
        "weights_a": np.concatenate([np.stack([w.T for w in (L1_xattn_W_q, L1_xattn_W_k, L1_xattn_W_v, L1_xattn_W_o)], axis=1),
                                     chunks(L0_xattn_W_qv)], axis=1),
        "weights_b": np.concatenate([L1_ffn_Wqkv, L1_ffn_Wo, L1_ffn_rW1, flat(chunks(L1_ffn_rW2))], axis=1),
        "ffn_w": np.concatenate([L0_ffn_w_gate.T.reshape(D, -1, 128), L0_ffn_w_up.T.reshape(D, -1, 128),
                                 chunks(L0_ffn_w_down.T)], axis=1),
        "query_pos_mask": np.concatenate([cols(itok_BxS_8_8191), flat(by_token(mask_BxSxS2_if1))], axis=1),
        "key_pos": itok_BxS2_1_8191.reshape(-1, 2, SEQ).transpose(1, 0, 2),
        "experts": np.stack(experts, axis=1),
        "b2": L1_ffn_b2,
    }


def kernel(**inputs):
    import numpy as _np
    import concourse.bacc as _bacc
    from concourse import mybir as _mybir
    from concourse.bass_utils import run_bass_kernel_spmd as _run

    nc = _bacc.Bacc("TRN2", target_bir_lowering=False, num_devices=1)
    arrays, args = {}, {}
    for name, value in layout(**{name: _np.asarray(value) for name, value in inputs.items()}).items():
        v = _np.ascontiguousarray(value)
        arrays[f"in_{name}"] = v
        args[name] = nc.dram_tensor(f"in_{name}", v.shape, _mybir.dt.from_np(v.dtype), kind="ExternalInput").ap()
    out = nc.dram_tensor("out_0", inputs["x"].shape, _mybir.dt.float32, kind="ExternalOutput").ap()
    flamingo_layers(nc, args, out)
    r = _run(nc, [arrays], core_ids=[0])
    return r.results[0]["out_0"]
```
